# Optimizing a Trainium2 kernel written in Bass

```python
import numpy as np
import jax
import jax.numpy as jnp

def _softmax(x, axis=-1):
    return jax.nn.softmax(x, axis=axis)

def _gelu(x):
    return jax.nn.gelu(x, approximate=True)

def _silu(x):
    return jax.nn.silu(x)

def _sigmoid(x):
    return jax.nn.sigmoid(x)

def _layernorm(x, axis=-1, eps=1e-05):
    m = jnp.mean(x, axis=axis, keepdims=True)
    v = jnp.var(x, axis=axis, keepdims=True)
    return (x - m) / jnp.sqrt(v + eps)

def _scatter_add(tgt, idx, src, axis=0):
    return tgt.at[idx].add(src)

def _segment_sum(src, seg, n):
    return jax.ops.segment_sum(src, seg, n)
kernel_name = 'mk_conv_attn_hybrid_d2_conv_nhwc768_r4_da23c5'

def setup_inputs(seed: int=0):
    np.random.seed(seed)
    _w = jnp.asarray

    def _rec_inputs():
        import jax
        import jax.numpy as jnp
        _gk = jax.random.key(seed)
        x = -0.0004039 + 1 * jax.random.normal(jax.random.fold_in(_gk, 1), (4, 16, 16, 192), jnp.float32)
        return x
    x = _rec_inputs()

    def _L0_conv_setup():
        import jax, jax.numpy as jnp
        import numpy as np
        B_, H_, W_, DM = (4, 16, 16, 192)
        DI = int(0.5 * DM)
        N = 16
        R = -(-DM // 16)
        K = 4

        def selective_scan(xs, dts, As, Bs, Cs, Dsk):
            u = jnp.moveaxis(xs, -1, 0)
            d = jnp.moveaxis(dts, -1, 0)
            Bt = jnp.moveaxis(Bs, -1, 0)
            Ct = jnp.moveaxis(Cs, -1, 0)

            def step(h, inp):
                u_t, d_t, B_t, C_t = inp
                dA = jnp.exp(d_t[..., None] * As)
                h = h * dA + (d_t * u_t)[..., None] * B_t[:, :, None, :]
                y = jnp.einsum('bkcn,bkn->bkc', h, C_t)
                return (h, y)
            h0 = jnp.zeros(u.shape[1:] + (As.shape[-1],), u.dtype)
            _, ys = jax.lax.scan(step, h0, (u, d, Bt, Ct))
            ys = jnp.moveaxis(ys, 0, -1)
            return ys + Dsk[None, :, :, None] * xs
        key = jax.random.key(seed)
        ks = jax.random.split(key, 8)
        s = lambda i, shape, sc=0.02: jax.random.normal(ks[i], shape, jnp.float32) * sc
        return dict(x=jax.random.normal(ks[0], (B_, H_, W_, DM), jnp.float32), in_proj_w=s(1, (2 * DI, DM)), conv_w=s(2, (DI, 1, 3, 3)), conv_b=jnp.zeros((DI,), jnp.float32), x_proj_w=s(3, (K, R + 2 * N, DI)), dt_projs_w=s(4, (K, DI, R)), dt_projs_b=s(5, (K, DI)), A_logs=jnp.log(jnp.tile(jnp.arange(1, N + 1, dtype=jnp.float32)[None, :], (K * DI, 1))), Ds=jnp.ones((K * DI,), jnp.float32), out_norm_g=jnp.ones((DI,), jnp.float32), out_norm_b=jnp.zeros((DI,), jnp.float32), out_proj_w=s(6, (DM, DI)))
    _L0_conv_all = _L0_conv_setup()
    _L0_conv_in = {k: v for k, v in _L0_conv_all.items() if k in ('in_proj_w', 'conv_w', 'conv_b', 'x_proj_w', 'dt_projs_w', 'dt_projs_b', 'A_logs', 'Ds', 'out_norm_g', 'out_norm_b', 'out_proj_w')}
    del _L0_conv_all

    def _L1_attn_setup():
        import jax, jax.numpy as jnp
        import numpy as np
        B, S, D, H = (8, 256, 192, 12)
        HS = D // H
        key = jax.random.key(seed)
        k1, k2, k3 = jax.random.split(key, 3)
        x = jax.random.normal(k1, (B, S, D), dtype=jnp.float32)
        W_attn = jax.random.normal(k2, (D, 3 * H * HS), dtype=jnp.float32) * 0.02
        b_attn = jnp.zeros((3 * H * HS,), dtype=jnp.float32)
        W_proj = jax.random.normal(k3, (H * HS, D), dtype=jnp.float32) * 0.02
        b_proj = jnp.zeros((D,), dtype=jnp.float32)
        return {'x': x, 'W_attn': W_attn, 'b_attn': b_attn, 'W_proj': W_proj, 'b_proj': b_proj}
    _L1_attn_all = _L1_attn_setup()
    _L1_attn_in = {k: v for k, v in _L1_attn_all.items() if k in ('W_attn', 'b_attn', 'W_proj', 'b_proj')}
    del _L1_attn_all

    def _L1_ffn_setup():
        import jax, jax.numpy as jnp
        import numpy as np
        E = 192
        H = 12
        D = E // H
        HID = 768
        NEXP = 4
        TOPK = 2
        EPS = 1e-05

        def _ln(x, g, b):
            m = jnp.mean(x, axis=-1, keepdims=True)
            v = jnp.mean(jnp.square(x - m), axis=-1, keepdims=True)
            return (x - m) * jax.lax.rsqrt(v + EPS) * g + b
        key = jax.random.key(seed)
        ks = jax.random.split(key, 10)
        s = 0.02
        return {'x': jax.random.normal(ks[0], (8, 256, E), jnp.float32), 'ln1_g': jnp.ones((E,), jnp.float32), 'ln1_b': jnp.zeros((E,), jnp.float32), 'in_w': jax.random.normal(ks[1], (3 * E, E), jnp.float32) * s, 'in_b': jnp.zeros((3 * E,), jnp.float32), 'out_w': jax.random.normal(ks[2], (E, E), jnp.float32) * s, 'out_b': jnp.zeros((E,), jnp.float32), 'mlp_w1': jax.random.normal(ks[3], (E, HID), jnp.float32) * s, 'mlp_b1': jnp.zeros((HID,), jnp.float32), 'mlp_w2': jax.random.normal(ks[4], (HID, E), jnp.float32) * s, 'mlp_b2': jnp.zeros((E,), jnp.float32), 'ln2_g': jnp.ones((E,), jnp.float32), 'ln2_b': jnp.zeros((E,), jnp.float32), 'gate_w': jax.random.normal(ks[5], (NEXP, E), jnp.float32) * s, 'gate_b': jnp.zeros((NEXP,), jnp.float32), 'exp_w1': jax.random.normal(ks[6], (NEXP, E, HID), jnp.float32) * s, 'exp_b1': jnp.zeros((NEXP, HID), jnp.float32), 'exp_w2': jax.random.normal(ks[7], (NEXP, HID, E), jnp.float32) * s, 'exp_b2': jnp.zeros((NEXP, E), jnp.float32)}
    _L1_ffn_all = _L1_ffn_setup()
    _L1_ffn_in = {k: v for k, v in _L1_ffn_all.items() if k in ('ln1_g', 'ln1_b', 'in_w', 'in_b', 'out_w', 'out_b', 'mlp_w1', 'mlp_b1', 'mlp_w2', 'mlp_b2', 'ln2_g', 'ln2_b', 'gate_w', 'gate_b', 'exp_w1', 'exp_b1', 'exp_w2', 'exp_b2')}
    del _L1_ffn_all
    return {'x': x, 'L0_conv_in_proj_w': _L0_conv_in['in_proj_w'], 'L0_conv_conv_w': _L0_conv_in['conv_w'], 'L0_conv_conv_b': _L0_conv_in['conv_b'], 'L0_conv_x_proj_w': _L0_conv_in['x_proj_w'], 'L0_conv_dt_projs_w': _L0_conv_in['dt_projs_w'], 'L0_conv_dt_projs_b': _L0_conv_in['dt_projs_b'], 'L0_conv_A_logs': _L0_conv_in['A_logs'], 'L0_conv_Ds': _L0_conv_in['Ds'], 'L0_conv_out_norm_g': _L0_conv_in['out_norm_g'], 'L0_conv_out_norm_b': _L0_conv_in['out_norm_b'], 'L0_conv_out_proj_w': _L0_conv_in['out_proj_w'], 'L1_attn_W_attn': _L1_attn_in['W_attn'], 'L1_attn_b_attn': _L1_attn_in['b_attn'], 'L1_attn_W_proj': _L1_attn_in['W_proj'], 'L1_attn_b_proj': _L1_attn_in['b_proj'], 'L1_ffn_ln1_g': _L1_ffn_in['ln1_g'], 'L1_ffn_ln1_b': _L1_ffn_in['ln1_b'], 'L1_ffn_in_w': _L1_ffn_in['in_w'], 'L1_ffn_in_b': _L1_ffn_in['in_b'], 'L1_ffn_out_w': _L1_ffn_in['out_w'], 'L1_ffn_out_b': _L1_ffn_in['out_b'], 'L1_ffn_mlp_w1': _L1_ffn_in['mlp_w1'], 'L1_ffn_mlp_b1': _L1_ffn_in['mlp_b1'], 'L1_ffn_mlp_w2': _L1_ffn_in['mlp_w2'], 'L1_ffn_mlp_b2': _L1_ffn_in['mlp_b2'], 'L1_ffn_ln2_g': _L1_ffn_in['ln2_g'], 'L1_ffn_ln2_b': _L1_ffn_in['ln2_b'], 'L1_ffn_gate_w': _L1_ffn_in['gate_w'], 'L1_ffn_gate_b': _L1_ffn_in['gate_b'], 'L1_ffn_exp_w1': _L1_ffn_in['exp_w1'], 'L1_ffn_exp_b1': _L1_ffn_in['exp_b1'], 'L1_ffn_exp_w2': _L1_ffn_in['exp_w2'], 'L1_ffn_exp_b2': _L1_ffn_in['exp_b2']}

def reference(x, L0_conv_in_proj_w, L0_conv_conv_w, L0_conv_conv_b, L0_conv_x_proj_w, L0_conv_dt_projs_w, L0_conv_dt_projs_b, L0_conv_A_logs, L0_conv_Ds, L0_conv_out_norm_g, L0_conv_out_norm_b, L0_conv_out_proj_w, L1_attn_W_attn, L1_attn_b_attn, L1_attn_W_proj, L1_attn_b_proj, L1_ffn_ln1_g, L1_ffn_ln1_b, L1_ffn_in_w, L1_ffn_in_b, L1_ffn_out_w, L1_ffn_out_b, L1_ffn_mlp_w1, L1_ffn_mlp_b1, L1_ffn_mlp_w2, L1_ffn_mlp_b2, L1_ffn_ln2_g, L1_ffn_ln2_b, L1_ffn_gate_w, L1_ffn_gate_b, L1_ffn_exp_w1, L1_ffn_exp_b1, L1_ffn_exp_w2, L1_ffn_exp_b2):
    import jax
    import jax.numpy as jnp

    def _L0_conv_ref(x, in_proj_w, conv_w, conv_b, x_proj_w, dt_projs_w, dt_projs_b, A_logs, Ds, out_norm_g, out_norm_b, out_proj_w):
        import jax, jax.numpy as jnp
        import numpy as np
        B_, H_, W_, DM = (4, 16, 16, 192)
        DI = int(0.5 * DM)
        N = 16
        R = -(-DM // 16)
        K = 4

        def selective_scan(xs, dts, As, Bs, Cs, Dsk):
            u = jnp.moveaxis(xs, -1, 0)
            d = jnp.moveaxis(dts, -1, 0)
            Bt = jnp.moveaxis(Bs, -1, 0)
            Ct = jnp.moveaxis(Cs, -1, 0)

            def step(h, inp):
                u_t, d_t, B_t, C_t = inp
                dA = jnp.exp(d_t[..., None] * As)
                h = h * dA + (d_t * u_t)[..., None] * B_t[:, :, None, :]
                y = jnp.einsum('bkcn,bkn->bkc', h, C_t)
                return (h, y)
            h0 = jnp.zeros(u.shape[1:] + (As.shape[-1],), u.dtype)
            _, ys = jax.lax.scan(step, h0, (u, d, Bt, Ct))
            ys = jnp.moveaxis(ys, 0, -1)
            return ys + Dsk[None, :, :, None] * xs
        B, H, W, _ = x.shape
        L = H * W
        xz = x @ in_proj_w.T
        xh, z = jnp.split(xz, 2, axis=-1)
        xc = jnp.transpose(xh, (0, 3, 1, 2))
        xc = jax.lax.conv_general_dilated(xc, conv_w, (1, 1), 'SAME', feature_group_count=DI)
        xc = jax.nn.silu(xc + conv_b[None, :, None, None])
        x_flat = xc.reshape(B, DI, L)
        x_t = jnp.transpose(xc, (0, 1, 3, 2)).reshape(B, DI, L)
        x_hwwh = jnp.stack([x_flat, x_t], 1)
        xs = jnp.concatenate([x_hwwh, jnp.flip(x_hwwh, -1)], 1)
        x_dbl = jnp.einsum('bkdl,kcd->bkcl', xs, x_proj_w)
        dts, Bs, Cs = jnp.split(x_dbl, [R, R + N], axis=2)
        dts = jnp.einsum('bkrl,kdr->bkdl', dts, dt_projs_w)
        dts = jax.nn.softplus(dts + dt_projs_b[None, :, :, None])
        As = -jnp.exp(A_logs).reshape(K, DI, N)
        out_y = selective_scan(xs, dts, As, Bs, Cs, Ds.reshape(K, DI))
        inv_y = jnp.flip(out_y[:, 2:4], -1)
        wh_y = jnp.transpose(out_y[:, 1].reshape(B, DI, W, H), (0, 1, 3, 2)).reshape(B, DI, L)
        invwh_y = jnp.transpose(inv_y[:, 1].reshape(B, DI, W, H), (0, 1, 3, 2)).reshape(B, DI, L)
        y = out_y[:, 0] + inv_y[:, 0] + wh_y + invwh_y
        y = jnp.transpose(y, (0, 2, 1)).reshape(B, H, W, DI)
        mu = y.mean(-1, keepdims=True)
        var = y.var(-1, keepdims=True)
        y = (y - mu) / jnp.sqrt(var + 1e-05) * out_norm_g + out_norm_b
        y = y * jax.nn.silu(z)
        return y @ out_proj_w.T

    def _L1_attn_ref(x, W_attn, b_attn, W_proj, b_proj):
        import jax, jax.numpy as jnp
        import numpy as np
        B, S, D, H = (8, 256, 192, 12)
        HS = D // H
        b, s, d = x.shape
        qkv = (x @ W_attn + b_attn).reshape(b, s, 3, H, HS)
        q, k, v = (qkv[:, :, 0], qkv[:, :, 1], qkv[:, :, 2])
        scale = jnp.sqrt(jnp.asarray(HS, dtype=x.dtype))
        scores = jnp.einsum('bqhd,bkhd->bhqk', q, k) / scale
        causal = jnp.tril(jnp.ones((s, s), dtype=bool))
        scores = jnp.where(causal, scores, -jnp.inf)
        attn = jax.nn.softmax(scores, axis=-1)
        out = jnp.einsum('bhqk,bkhd->bqhd', attn, v).reshape(b, s, H * HS)
        return out @ W_proj + b_proj

    def _L1_ffn_ref(x, ln1_g, ln1_b, in_w, in_b, out_w, out_b, mlp_w1, mlp_b1, mlp_w2, mlp_b2, ln2_g, ln2_b, gate_w, gate_b, exp_w1, exp_b1, exp_w2, exp_b2):
        import jax, jax.numpy as jnp
        import numpy as np
        E = 192
        H = 12
        D = E // H
        HID = 768
        NEXP = 4
        TOPK = 2
        EPS = 1e-05

        def _ln(x, g, b):
            m = jnp.mean(x, axis=-1, keepdims=True)
            v = jnp.mean(jnp.square(x - m), axis=-1, keepdims=True)
            return (x - m) * jax.lax.rsqrt(v + EPS) * g + b
        B, N, _ = x.shape
        h = _ln(x, ln1_g, ln1_b)
        qkv = h @ in_w.T + in_b
        q, k, v = jnp.split(qkv, 3, axis=-1)
        q = q.reshape(B, N, H, D)
        k = k.reshape(B, N, H, D)
        v = v.reshape(B, N, H, D)
        scores = jnp.einsum('bqhd,bkhd->bhqk', q, k) / jnp.sqrt(jnp.float32(D))
        attn = jax.nn.softmax(scores, axis=-1)
        ctx = jnp.einsum('bhqk,bkhd->bqhd', attn, v).reshape(B, N, E)
        x = x + ctx @ out_w.T + out_b
        x = x + jax.nn.gelu(x @ mlp_w1 + mlp_b1, approximate=False) @ mlp_w2 + mlp_b2
        xm = _ln(x, ln2_g, ln2_b)
        logits = xm @ gate_w.T + gate_b
        topv, topi = jax.lax.top_k(logits, TOPK)
        gates = jax.nn.softmax(topv, axis=-1)
        onehot = jax.nn.one_hot(topi, NEXP, dtype=x.dtype)
        comb = jnp.einsum('bnk,bnke->bne', gates, onehot)
        moe_out = jnp.zeros_like(x)
        for e in range(NEXP):
            he = jax.nn.gelu(xm @ exp_w1[e] + exp_b1[e], approximate=False)
            oe = he @ exp_w2[e] + exp_b2[e]
            moe_out = moe_out + comb[..., e:e + 1] * oe
        return x + moe_out

    def _gn(v, G=32, eps=1e-05):
        B_, H_, W_, C_ = v.shape
        g = v.reshape(B_, H_, W_, G, C_ // G)
        m = jnp.mean(g, axis=(1, 2, 4), keepdims=True)
        s = jnp.var(g, axis=(1, 2, 4), keepdims=True)
        return ((g - m) / jnp.sqrt(s + eps)).reshape(v.shape)

    def _ln_c(v, eps=1e-06):
        m = jnp.mean(v, axis=-1, keepdims=True)
        s = jnp.var(v, axis=-1, keepdims=True)
        return (v - m) / jnp.sqrt(s + eps)

    def _ln_t(v, eps=1e-05):
        m = jnp.mean(v, axis=-1, keepdims=True)
        s = jnp.var(v, axis=-1, keepdims=True)
        return (v - m) / jnp.sqrt(s + eps)

    def _to_tokens(v):
        B_, H_, W_, C_ = v.shape
        return v.reshape(B_, H_ * W_, C_)

    def _from_tokens(t, like):
        return t.reshape(like.shape)
    x = x + _L0_conv_ref(_gn(x), L0_conv_in_proj_w, L0_conv_conv_w, L0_conv_conv_b, L0_conv_x_proj_w, L0_conv_dt_projs_w, L0_conv_dt_projs_b, L0_conv_A_logs, L0_conv_Ds, L0_conv_out_norm_g, L0_conv_out_norm_b, L0_conv_out_proj_w)
    t = _to_tokens(x)
    t = t + _L1_attn_ref(_ln_t(t), L1_attn_W_attn, L1_attn_b_attn, L1_attn_W_proj, L1_attn_b_proj)
    t = t + _L1_ffn_ref(_ln_t(t), L1_ffn_ln1_g, L1_ffn_ln1_b, L1_ffn_in_w, L1_ffn_in_b, L1_ffn_out_w, L1_ffn_out_b, L1_ffn_mlp_w1, L1_ffn_mlp_b1, L1_ffn_mlp_w2, L1_ffn_mlp_b2, L1_ffn_ln2_g, L1_ffn_ln2_b, L1_ffn_gate_w, L1_ffn_gate_b, L1_ffn_exp_w1, L1_ffn_exp_b1, L1_ffn_exp_w2, L1_ffn_exp_b2)
    x = _from_tokens(t, x)
    return x

_drawn_inputs = setup_inputs


def setup_inputs(seed=0):
    import zlib

    import numpy as np

    out = dict(_drawn_inputs(seed))
    spreads = {'L0_conv_conv_b': (0.0, 0.1),
     'L0_conv_Ds': (1.0, 0.6),
     'L0_conv_out_norm_g': (1.0, 0.6),
     'L0_conv_out_norm_b': (0.0, 0.8),
     'L1_attn_b_attn': (0.0, 0.302),
     'L1_attn_b_proj': (0.0, 0.1),
     'L1_ffn_ln1_g': (1.0, 0.6),
     'L1_ffn_ln1_b': (0.0, 0.8),
     'L1_ffn_in_b': (0.0, 0.507),
     'L1_ffn_out_b': (0.0, 0.315),
     'L1_ffn_mlp_b1': (0.0, 0.476),
     'L1_ffn_mlp_b2': (0.0, 0.351),
     'L1_ffn_ln2_g': (1.0, 0.6),
     'L1_ffn_ln2_b': (0.0, 2.0),
     'L1_ffn_gate_b': (0.0, 0.508),
     'L1_ffn_exp_b1': (0.0, 0.73),
     'L1_ffn_exp_b2': (0.0, 0.433)}
    factors = {'L0_conv_conv_w': 8.0,
     'L0_conv_x_proj_w': 64.0,
     'L0_conv_dt_projs_w': 64.0,
     'L0_conv_dt_projs_b': 64.0,
     'L0_conv_A_logs': 64.0,
     'L1_attn_W_attn': 4.744,
     'L1_ffn_in_w': 8.0,
     'L1_ffn_out_w': 3.824}
    for name, (base, spread) in spreads.items():
        noise = np.random.default_rng([zlib.crc32(name.encode()), seed]).standard_normal(out[name].shape)
        drawn = base * np.exp(spread * noise) if base else spread * noise
        out[name] = jnp.asarray(drawn.astype(out[name].dtype))
    for name, factor in factors.items():
        out[name] = (out[name] * factor).astype(out[name].dtype)
    return out
```

```python
from contextlib import ExitStack

import concourse.bass as bass
from concourse import mybir

F32 = mybir.dt.float32
BF16 = mybir.dt.bfloat16
ALU = mybir.AluOpType
ACT = mybir.ActivationFunctionType
AX = mybir.AxisListType

IMAGES, SIDE, WIDTH = 4, 16, 192
TOKENS = SIDE * SIDE
TILES = TOKENS // 128
INNER, STATE, PATHS, RANK = 96, 16, 4, 12
PACK = 128 // STATE
GROUPS = INNER // PACK
GN_GROUP = WIDTH // 32
HEADS, HEAD = 12, 16
QUAD = 4
HTILES = HEADS // QUAD
UNITS = HEADS // 2
HIDDEN, EXPERTS, TOPK = 768, 4, 2
HCH = HIDDEN // 128
HT_BANKS = [(0, 1), (2,)]
CH = [(0, 128), (128, 64)]
EPS = 1e-5
MASKED = -1e30
A_LOG_MAX = 80.0


def build(nc, t):
    ctx = ExitStack()
    with ctx:
        def sb(name, shape, dt=F32):
            return ctx.enter_context(nc.sbuf_tensor(name, shape, dt))

        def bank(name):
            return ctx.enter_context(nc.psum_tensor(name, [128, 512], F32))

        def sem(name):
            return ctx.enter_context(nc.semaphore(name))

        ident = sb("ident", [128, 128])
        identb = sb("identb", [128, 128], BF16)
        maskq = sb("maskq", [128, 128], BF16)
        maskk = sb("maskk", [128, 128], BF16)
        gsum = sb("gsum", [128, 2, WIDTH])
        sel = sb("sel", [128, PACK])
        dsum = sb("dsum", [INNER, 1])
        ddiag = sb("ddiag", [INNER, INNER])
        half = sb("half", [128, 2])
        lower = sb("lower", [128, EXPERTS, EXPERTS])
        w_in = sb("w_in", [128, 2, WIDTH])
        w_conv = sb("w_conv", [INNER, 9])
        b_conv = sb("b_conv", [INNER, 1])
        w_x = sb("w_x", [INNER, PATHS, RANK + 2 * STATE])
        w_dt = sb("w_dt", [RANK, PATHS, INNER])
        b_dt = sb("b_dt", [INNER, PATHS])
        a_log = sb("a_log", [128, GROUPS * PATHS])
        a_neg = sb("a_neg", [128, GROUPS * PATHS])
        ds_in = sb("ds_in", [INNER, PATHS])
        on_g = sb("on_g", [128, INNER])
        on_b = sb("on_b", [128, INNER])
        w_out = sb("w_out", [INNER, WIDTH])
        w_q = [sb(f"w_q{l}", [128, 2, HTILES, QUAD, 32]) for l in range(2)]
        w_k = [sb(f"w_k{l}", [128, 2, HTILES, QUAD, 32]) for l in range(2)]
        w_v = [sb(f"w_v{l}", [128, 2, WIDTH]) for l in range(2)]
        w_o = [sb(f"w_o{l}", [128, 2, WIDTH]) for l in range(2)]
        b_q = [sb(f"b_q{l}", [128, HTILES]) for l in range(2)]
        b_k = [sb(f"b_k{l}", [128, HTILES]) for l in range(2)]
        b_v = [sb(f"b_v{l}", [128, WIDTH]) for l in range(2)]
        b_o = [sb(f"b_o{l}", [128, WIDTH]) for l in range(2)]
        ln_g = [sb(f"ln_g{i}", [128, WIDTH]) for i in range(2)]
        ln_b = [sb(f"ln_b{i}", [128, WIDTH]) for i in range(2)]
        w_up = sb("w_up", [128, 1 + EXPERTS, 2, HIDDEN])
        b_up = sb("b_up", [128, 1 + EXPERTS, HCH])
        w_dn = sb("w_dn", [128, 1 + EXPERTS, HCH, WIDTH])
        b_dn = sb("b_dn", [128, WIDTH])
        b_ex = sb("b_ex", [EXPERTS, WIDTH])
        w_gate = sb("w_gate", [128, 2, EXPERTS])
        b_gate = sb("b_gate", [128, EXPERTS])

        x_tok = sb("x_tok", [128, TILES, WIDTH])
        gn_raw = sb("gn_raw", [128, 2, 6])
        gn_mv = sb("gn_mv", [128, 2, 2])
        gn_sq = sb("gn_sq", [128, 2])
        gn_m = sb("gn_m", [128, 2, 2])
        gn_var = sb("gn_var", [128, 2])
        gn_rstd = sb("gn_rstd", [128, 2])
        gn_shift = sb("gn_shift", [128, 2])
        xgT = sb("xgT", [128, 2, TOKENS])
        pad = sb("pad", [INNER, SIDE + 2, SIDE + 2])
        conv = sb("conv", [INNER, TOKENS])
        conv_e = sb("conv_e", [INNER, TOKENS])
        z_e = sb("z_e", [128, TILES, INNER])
        z_gate = sb("z_gate", [128, TILES, INNER])
        xs = sb("xs", [INNER, 2, TOKENS])
        xdbl = sb("xdbl", [RANK + 2 * STATE, PATHS, TOKENS])
        delta = sb("delta", [INNER, PATHS, TOKENS])
        delta_x = sb("delta_x", [INNER, PATHS, TOKENS])
        B_rows = sb("B_rows", [128, PATHS * TOKENS])
        C_rows = sb("C_rows", [128, PATHS * TOKENS])
        d_rows = [sb(f"d_rows{i}", [128, PATHS, TOKENS]) for i in range(2)]
        dx_rows = [sb(f"dx_rows{i}", [128, PATHS * TOKENS]) for i in range(2)]
        decay = [sb(f"decay{i}", [128, PATHS, TOKENS]) for i in range(2)]
        state = [sb(f"state{i}", [128, PATHS, TOKENS]) for i in range(2)]
        by_row = [sb(f"by_row{i}", [128, 2, TOKENS]) for i in range(2)]
        y_g = sb("y_g", [128, TILES, INNER])
        yT = sb("yT", [INNER, TOKENS])
        x1 = sb("x1", [128, TILES, WIDTH])

        norm_raw = sb("norm_raw", [128, 5, TILES, 6])
        norm_mv = sb("norm_mv", [128, 5, TILES, 2])
        norm_var = sb("norm_var", [128, 5, TILES])
        norm_rstd = sb("norm_rstd", [128, 5, TILES])
        norm_shift = sb("norm_shift", [128, 5, TILES])
        h_tok = sb("h_tok", [128, TILES, WIDTH])
        hT = sb("hT", [128, 2, TOKENS])
        qT = sb("qT", [128, HTILES, TOKENS])
        kT = sb("kT", [128, HTILES, TOKENS])
        v_aug = sb("v_aug", [128, TILES, HEADS, HEAD + 1])
        top = sb("top", [128, 2, TILES, 128])
        probs = [sb(f"probs{i}", [128, 2, 2, TOKENS]) for i in range(2)]
        den = sb("den", [128, TILES * HEADS])
        ctx_tok = sb("ctx_tok", [128, TILES, WIDTH])
        res = sb("res", [128, TILES, WIDTH])
        x2 = sb("x2", [128, TILES, WIDTH])
        v_tok = sb("v_tok", [128, TILES, WIDTH])
        v2 = sb("v2", [128, TILES, WIDTH])
        v3 = sb("v3", [128, TILES, WIDTH])
        act = [sb(f"act{i}", [128, HCH, TOKENS]) for i in range(2)]
        logit = sb("logit", [128, TILES, EXPERTS])
        beats = sb("beats", [128, TILES, EXPERTS, EXPERTS])
        ties = sb("ties", [128, TILES, EXPERTS, EXPERTS])
        rank = sb("rank", [128, TILES, EXPERTS])
        best = sb("best", [128, TILES])
        gate = sb("gate", [128, TILES, EXPERTS])
        gsumr = sb("gsumr", [128, TILES])
        gateT = sb("gateT", [EXPERTS, TOKENS])
        out_tok = sb("out_tok", [128, TILES, WIDTH])

        pa = [bank(f"pa{i}") for i in range(3)]
        ps = ctx.enter_context(nc.psum_tensor("ps", [128, 4, 512], F32))
        pm = bank("pm")

        w_a = sem("weights_a_loaded")
        w_b = sem("weights_b_loaded")
        zeroed = sem("zeroed")
        consts = sem("constants_built")
        pool_set = sem("pool_setup_chain")
        ready_a = sem("decay_rates_ready")

        per_image = []

        def isem(name):
            s = sem(name)
            per_image.append(s)
            return s

        x_in = isem("x_loaded")
        x_turned = isem("x_turned")
        gn_stats = isem("gn_channel_stats")
        gn_sums = isem("gn_group_sums")
        gn_v = isem("gn_variance")
        gn_r = isem("gn_rstd")
        xg_done = isem("x_group_normed")
        xh_done = isem("conv_input_ready")
        z_done = isem("z_ready")
        conv_done = isem("conv_done")
        silu_e = isem("silu_exponentials")
        u_done = isem("scan_input_ready")
        z_used = isem("z_gated")
        xs_done = isem("scan_orders_ready")
        xd_done = isem("x_dbl_ready")
        xd_copied = isem("x_dbl_copied")
        bc_in = isem("BC_rows_loaded")
        dt_done = isem("dt_ready")
        dt_sum = isem("dt_with_bias_ready")
        sp_a = isem("softplus_exp_ready")
        sp_u = isem("softplus_sum_ready")
        sp_l = isem("softplus_log_ready")
        d_done = isem("delta_ready")
        dx_done = isem("delta_x_ready")
        d_in = [isem(f"delta_rows_loaded{i}") for i in range(2)]
        dx_in = [isem(f"delta_x_rows_loaded{i}") for i in range(2)]
        decay_done = isem("decay_ready")
        scan_done = isem("state_scanned")
        sc_done = isem("state_times_C")
        y_part = isem("y_group_summed")
        yg_done = isem("y_gated")
        y_turned = isem("y_turned")
        yT_done = isem("yT_copied")
        o_done = isem("scan_output_projected")
        x1_done = isem("x1_ready")
        var_done = [isem(f"variance_ready{i}") for i in range(5)]
        rstd_done = [isem(f"rstd_ready{i}") for i in range(5)]
        h_done = [isem(f"normed_ready{i}") for i in range(2)]
        h_turned = [isem(f"normed_turned{i}") for i in range(2)]
        hT_done = [isem(f"normed_T_copied{i}") for i in range(2)]
        q_done = [isem(f"queries_projected{i}") for i in range(2)]
        k_done = [isem(f"keys_projected{i}") for i in range(2)]
        v_done = [isem(f"values_projected{i}") for i in range(2)]
        q_copied = [isem(f"q_and_v_copied{i}") for i in range(2)]
        k_copied = [isem(f"k_copied{i}") for i in range(2)]
        s_done = [isem(f"scores_ready{i}") for i in range(2)]
        top_done = [isem(f"row_max_ready{i}") for i in range(2)]
        top_turned = [isem(f"row_max_turned{i}") for i in range(2)]
        q_shifted = [isem(f"row_max_in_q{i}") for i in range(2)]
        st_done = [isem(f"shifted_scores_ready{i}") for i in range(2)]
        p_done = [isem(f"probs_ready{i}") for i in range(2)]
        av_done = [isem(f"context_summed{i}") for i in range(2)]
        ctx_done = [isem(f"context_ready{i}") for i in range(2)]
        ctx_turned = [isem(f"context_turned{i}") for i in range(2)]
        ctxT_done = [isem(f"context_T_copied{i}") for i in range(2)]
        proj_done = [isem(f"attention_projected{i}") for i in range(2)]
        res_done = [isem(f"residual_ready{i}") for i in range(2)]
        x2_done = isem("attention_added")
        m_turned = [isem(f"mlp_input_turned{i}") for i in range(2)]
        mT_done = [isem(f"mlp_input_T_copied{i}") for i in range(2)]
        v2_done = isem("v2_ready")
        mres_done = isem("mlp_residual_ready")
        xm_done = isem("moe_input_ready")
        v3_done = isem("v3_ready")
        base_done = isem("output_residual_ready")
        up_done = isem("hidden_ready")
        gelu_done = isem("gelu_ready")
        dn_done = isem("down_ready")
        dn_used = isem("down_used")
        lg_done = isem("logits_ready")
        lg_shift = isem("logits_shifted")
        gate_e = isem("gate_exponentials")
        gate_done = isem("gates_ready")
        gate_turned = isem("gates_turned")
        gateT_done = isem("gates_T_copied")
        gb_done = isem("gated_biases_ready")
        acc_done = isem("output_started")
        out_done = isem("output_ready")
        stored = isem("output_stored")
        dve_chain = isem("vector_chain")
        act_chain = isem("scalar_chain")
        pool_chain = isem("gpsimd_chain")
        numbers = sorted(s.num for s in per_image)
        assert numbers == list(range(numbers[0], numbers[0] + len(numbers)))
        clear_range = range(numbers[0], numbers[-1] + 1)

        def chained(eng, chain):
            count = [0]

            def link(ins):
                count[0] += 1
                ins.then_inc(chain, 1)
                eng.wait_ge(chain, count[0])
            return link

        a_loads = [
            (w_in[:, 0, :], t["w_in"][0:128, :]), (w_in[0:64, 1, :], t["w_in"][128:192, :]),
            (w_conv[:, :], t["w_conv"]), (b_conv[:, :], t["b_conv"]),
            (w_x[:, :, :], t["w_x"]), (w_dt[:, :, :], t["w_dt"]), (b_dt[:, :], t["b_dt"]),
            (a_log[:, :], t["a_log"]), (ds_in[:, :], t["ds"]),
            (on_g[:, :], t["on_g"].partition_broadcast(128)),
            (on_b[:, :], t["on_b"].partition_broadcast(128)),
            (w_out[:, :], t["w_out"]),
        ]
        b_loads = []
        for l in range(2):
            w, b = t[f"w_qkv{l}"], t[f"b_qkv{l}"]
            for c, (c0, cn) in enumerate(CH):
                for part, dst in ((0, w_q[l]), (1, w_k[l])):
                    for ht in range(HTILES):
                        first = part * WIDTH + ht * QUAD * HEAD
                        b_loads.append((dst[0:cn, c, ht, :, 0:HEAD],
                                        w[c0:c0 + cn, first:first + QUAD * HEAD]
                                        .rearrange("k (j i) -> k j i", i=HEAD)))
                b_loads.append((w_v[l][0:cn, c, :], w[c0:c0 + cn, 2 * WIDTH:3 * WIDTH]))
                b_loads.append((w_o[l][0:cn, c, :], t[f"w_o{l}"][c0:c0 + cn, :]))
            for part, dst in ((0, b_q[l]), (1, b_k[l])):
                heads = b[part * WIDTH:(part + 1) * WIDTH].rearrange("(t j i) -> j i t", j=QUAD, i=HEAD)
                for j in range(QUAD):
                    b_loads.append((dst[32 * j:32 * j + HEAD, :], heads[j]))
            b_loads.append((b_v[l][:, :], b[2 * WIDTH:3 * WIDTH].partition_broadcast(128)))
            b_loads.append((b_o[l][:, :], t[f"b_o{l}"].partition_broadcast(128)))
            b_loads.append((ln_g[l][:, :], t[f"ln_g{l}"].partition_broadcast(128)))
            b_loads.append((ln_b[l][:, :], t[f"ln_b{l}"].partition_broadcast(128)))
        for c, (c0, cn) in enumerate(CH):
            b_loads.append((w_up[0:cn, 0, c, :], t["mlp_w1"][c0:c0 + cn, :]))
            b_loads.append((w_gate[0:cn, c, :], t["w_gate"][c0:c0 + cn, :]))
            for e in range(EXPERTS):
                b_loads.append((w_up[0:cn, 1 + e, c, :], t["exp_w1"][e, c0:c0 + cn, :]))
        b_loads.append((w_dn[:, 0, :, :], t["mlp_w2"].rearrange("(m p) n -> p m n", p=128)))
        for e in range(EXPERTS):
            b_loads.append((w_dn[:, 1 + e, :, :], t["exp_w2"][e].rearrange("(m p) n -> p m n", p=128)))
        b_loads += [
            (b_up[:, :, :], t["b_up"]), (b_dn[:, :], t["mlp_b2"].partition_broadcast(128)),
            (b_ex[:, :], t["exp_b2"]), (b_gate[:, :], t["b_gate"].partition_broadcast(128)),
        ]

        with nc.Block() as block:
            @block.sync
            def _(sp):
                with nc.allow_non_contiguous_dma(reason="short rows of heads and biases, once"):
                    for dst, src in a_loads:
                        sp.dma_start(dst, src).then_inc(w_a, 16)
                    sp.wait_ge(consts, 1)
                    for dst, src in b_loads:
                        sp.dma_start(dst, src).then_inc(w_b, 16)

            @block.gpsimd
            def _(pool):
                link = chained(pool, pool_set)
                for tile, value in ((ident, 0.0), (maskq, 0.0), (maskk, 0.0), (gsum, 1.0 / GN_GROUP),
                                    (sel, 1.0), (ddiag, 0.0), (half, -0.5), (lower, 1.0),
                                    (b_q[0], 0.0), (b_q[1], 0.0), (b_k[0], 0.0), (b_k[1], 0.0)):
                    link(nc.gpsimd.memset(tile[:], value))
                link(nc.gpsimd.affine_select(out=ident[:, :], in_=ident[:, :], compare_op=ALU.not_equal,
                                             fill=1.0, base=0, pattern=[[-1, 128]], channel_multiplier=1))
                link(nc.gpsimd.affine_select(out=maskq[:, :], in_=maskq[:, :], compare_op=ALU.is_ge,
                                             fill=MASKED, base=0, pattern=[[-1, 128]], channel_multiplier=1))
                link(nc.gpsimd.affine_select(out=maskk[:, :], in_=maskk[:, :], compare_op=ALU.is_ge,
                                             fill=MASKED, base=0, pattern=[[1, 128]], channel_multiplier=-1))
                for c, (c0, cn) in enumerate(CH):
                    for base, sign in ((c0, 1), (GN_GROUP - 1 - c0, -1)):
                        link(nc.gpsimd.affine_select(
                            out=gsum[:, c, :], in_=gsum[:, c, :], compare_op=ALU.is_ge, fill=0.0, base=base,
                            pattern=[[-GN_GROUP * sign, WIDTH // GN_GROUP], [0, GN_GROUP]],
                            channel_multiplier=sign))
                for base, sign in ((0, 1), (STATE - 1, -1)):
                    link(nc.gpsimd.affine_select(out=sel[:, :], in_=sel[:, :], compare_op=ALU.is_ge, fill=0.0,
                                                 base=base, pattern=[[-STATE * sign, PACK]],
                                                 channel_multiplier=sign))
                link(nc.gpsimd.affine_select(out=lower[:, :, :], in_=lower[:, :, :], compare_op=ALU.is_gt,
                                             fill=0.0, base=0, pattern=[[1, EXPERTS], [-1, EXPERTS]],
                                             channel_multiplier=0))
                for l in range(2):
                    for j in range(QUAD):
                        link(nc.gpsimd.affine_select(
                            out=b_k[l][:, :], in_=b_k[l][:, :], compare_op=ALU.not_equal, fill=1.0,
                            base=-(32 * j + HEAD), pattern=[[0, HTILES]], channel_multiplier=1))
                pool.wait_ge(zeroed, 1)
                nc.gpsimd.tensor_copy(identb[:, :], ident[:, :]).then_inc(consts, 1)

            @block.vector
            def _(dve):
                for l in range(2):
                    for w in (w_q[l], w_k[l]):
                        nc.vector.memset(w[:], 0.0)
                for buf in (pad, gn_raw, gn_mv, gn_m, top, decay[0], decay[1]):
                    nc.vector.memset(buf[:], 0.0)
                nc.vector.memset(v_aug[:, :, :, HEAD:HEAD + 1], 1.0).then_inc(zeroed, 1)
                dve.wait_ge(w_a, 16 * len(a_loads))
                dve.wait_ge(consts, 1)
                nc.vector.tensor_reduce(dsum[:, :], ds_in[:, :], AX.X, ALU.add)
                nc.vector.tensor_scalar(a_log[:, :], a_log[:, :], A_LOG_MAX, None,
                                        ALU.min).then_inc(zeroed, 1)
                dve.wait_ge(zeroed, 2)
                nc.vector.tensor_scalar(ddiag[:, :], ident[0:INNER, 0:INNER], dsum[:, 0:1], None,
                                        ALU.mult).then_inc(zeroed, 1)
                dve.wait_ge(ready_a, 1)
                nc.vector.tensor_scalar(a_neg[:, :], a_neg[:, :], -1.0, None, ALU.mult).then_inc(zeroed, 1)

            @block.scalar
            def _(sc):
                sc.wait_ge(zeroed, 2)
                nc.scalar.activation(a_neg[:, :], a_log[:, :], ACT.Exp).then_inc(ready_a, 1)

        def turn(first, second, src):
            for tl in range(TILES):
                for c, (c0, cn) in enumerate(CH):
                    mm = nc.tensor.transpose((first, second)[c][0:cn, tl * 128:(tl + 1) * 128],
                                             src[:, tl, c0:c0 + cn], ident[:, :])
            return mm

        def chunks(out, lhs, rhs, start=True):
            for c, (_, cn) in enumerate(CH):
                mm = nc.tensor.matmul(out, lhs(c, cn), rhs(c, cn), start=(c == 0), stop=(c == 1))
            return mm

        def head_rows(first, ht):
            return ps[:, first + ht // 2, TOKENS * (ht % 2):TOKENS * (ht % 2 + 1)]

        def flat(buf):
            return buf[:, :, :].rearrange("p k l -> p (k l)")

        def tile_states(g, k, tl):
            buf = state[g % 2][:, k, :] if k % 2 == 0 else by_row[g % 2][:, k // 2, :]
            return buf[:, 128 * tl:128 * (tl + 1)]

        def image(a_at, b_at):
            run_a, run_b = a_at is not None, b_at is not None

            with nc.Block() as block:
                @block.sync
                def _(sp):
                    if run_a:
                        sp.dma_start(x_tok[:, :, :],
                                     t["x"][bass.ds(a_at, 1)].rearrange("o (t p) c -> p (o t) c", p=128)
                                     ).then_inc(x_in, 16)
                        sp.wait_ge(xd_copied, 2)
                        for dst, first in ((B_rows, RANK), (C_rows, RANK + STATE)):
                            for c in range(PACK):
                                sp.dma_start(dst[STATE * c:STATE * (c + 1), :], xdbl[first:first + STATE, :, :]
                                             .rearrange("n k l -> n (k l)")).then_inc(bc_in, 16)
                        for g in range(GROUPS):
                            rows = slice(PACK * g, PACK * (g + 1))
                            if g == 0:
                                sp.wait_ge(d_done, 1)
                            if g >= 2:
                                sp.wait_ge(decay_done, g - 1)
                            sp.dma_start(d_rows[g % 2][:, :, :], delta[rows, :, :].rearrange("c k l -> c (k l)")
                                         .unsqueeze(1).to_broadcast([PACK, STATE, PATHS * TOKENS])
                                         ).then_inc(d_in[g % 2], 16)
                            if g == 0:
                                sp.wait_ge(dx_done, 1)
                            if g >= 2:
                                sp.wait_ge(scan_done, g - 1)
                            sp.dma_start(dx_rows[g % 2][:, :], delta_x[rows, :, :].rearrange("c k l -> c (k l)")
                                         .unsqueeze(1).to_broadcast([PACK, STATE, PATHS * TOKENS])
                                         ).then_inc(dx_in[g % 2], 16)
                    if run_b:
                        sp.wait_ge(w_b, 16 * len(b_loads))
                        sp.wait_ge(out_done, TILES)
                        sp.dma_start(t["out"][bass.ds(b_at, 1)].rearrange("o (t p) c -> p (o t) c", p=128),
                                     out_tok[:, :, :]).then_inc(stored, 16)
                        sp.wait_ge(stored, 16)

                @block.tensor
                def _(pe):
                    def a_prep():
                        if run_a:
                            pe.wait_ge(x_in, 16)
                            turn(pa[1][:, 0:TOKENS], pa[1][:, TOKENS:2 * TOKENS], x_tok).then_inc(x_turned, 1)
                            pe.wait_ge(gn_stats, 1)
                            for m, (m0, mn) in enumerate(CH):
                                mm = chunks(pa[2][0:mn, 2 * m:2 * m + 2],
                                            lambda c, cn: gsum[0:cn, c, m0:m0 + mn],
                                            lambda c, cn: gn_mv[0:cn, c, :])
                            mm.then_inc(gn_sums, 1)
                            pe.wait_ge(xg_done, 2)
                            chunks(pa[2][0:INNER, 0:TOKENS], lambda c, cn: w_in[0:cn, c, 0:INNER],
                                   lambda c, cn: xgT[0:cn, c, :]).then_inc(xh_done, 1)
                            for tl in range(TILES):
                                mm = chunks(pa[1][:, INNER * tl:INNER * (tl + 1)],
                                            lambda c, cn: xgT[0:cn, c, 128 * tl:128 * (tl + 1)],
                                            lambda c, cn: w_in[0:cn, c, INNER:2 * INNER])
                            mm.then_inc(z_done, 1)
                            pe.wait_ge(z_used, 1)
                            pe.wait_ge(xs_done, 1)
                            for k in range(PATHS):
                                mm = nc.tensor.matmul(pa[1 + k // 2][0:RANK + 2 * STATE,
                                                                     TOKENS * (k % 2):TOKENS * (k % 2 + 1)],
                                                      w_x[:, k, :], xs[:, k % 2, :], start=True, stop=True)
                                if k % 2:
                                    mm.then_inc(xd_done, 1)
                            for tl in range(TILES):
                                nc.tensor.matmul(pa[0][:, INNER * tl:INNER * (tl + 1)],
                                                 xs[:, 0, 128 * tl:128 * (tl + 1)], ddiag[:, :],
                                                 start=(tl == 0), stop=False, skip_group_check=True)
                            pe.wait_ge(xd_copied, 2)
                            for k in range(PATHS):
                                mm = nc.tensor.matmul(pa[1 + k // 2][0:INNER,
                                                                     TOKENS * (k % 2):TOKENS * (k % 2 + 1)],
                                                      w_dt[:, k, :], xdbl[0:RANK, k, :], start=True, stop=True)
                            mm.then_inc(dt_done, 1)

                    def a_scan(g):
                        if run_a:
                            pe.wait_ge(sc_done, g + 1)
                            for tl in range(TILES):
                                for k in range(PATHS):
                                    at = INNER * tl + PACK * g
                                    mm = nc.tensor.matmul(pa[0][:, at:at + PACK], tile_states(g, k, tl), sel[:, :],
                                                          start=False, stop=(g == GROUPS - 1 and k == 3),
                                                          skip_group_check=True)
                            mm.then_inc(y_part, 1)

                    def a_post():
                        if run_a:
                            pe.wait_ge(yg_done, TILES)
                            for tl in range(TILES):
                                mm = nc.tensor.transpose(pa[1][0:INNER, 128 * tl:128 * (tl + 1)],
                                                         y_g[:, tl, :], ident[:, :])
                            mm.then_inc(y_turned, 1)
                            pe.wait_ge(yT_done, 1)
                            for tl in range(TILES):
                                mm = nc.tensor.matmul(pa[2][:, WIDTH * tl:WIDTH * (tl + 1)],
                                                      yT[:, 128 * tl:128 * (tl + 1)], w_out[:, :],
                                                      start=True, stop=True)
                            mm.then_inc(o_done, 1)

                    def attention(l):
                        causal = l == 0
                        pe.wait_ge(h_done[l], TILES)
                        turn(pm, ps[:, 3, :], h_tok).then_inc(h_turned[l], 1)
                        pe.wait_ge(hT_done[l], 2)
                        for hts in HT_BANKS:
                            for first, w, done in ((0, w_q[l], q_done[l]), (2, w_k[l], k_done[l])):
                                for ht in hts:
                                    mm = chunks(head_rows(first, ht),
                                                lambda c, cn: w[0:cn, c, ht, :, :]
                                                .rearrange("k j i -> k (j i)"),
                                                lambda c, cn: hT[0:cn, c, :])
                                mm.then_inc(done, 1)
                        for tl in range(TILES):
                            mm = chunks(pm[:, WIDTH * tl:WIDTH * (tl + 1)],
                                        lambda c, cn: hT[0:cn, c, 128 * tl:128 * (tl + 1)],
                                        lambda c, cn: w_v[l][0:cn, c, :])
                        mm.then_inc(v_done[l], 1)

                        def scores(u):
                            if u == 0:
                                pe.wait_ge(q_copied[l], HTILES + 1)
                                pe.wait_ge(k_copied[l], HTILES)
                            if u >= 2:
                                pe.wait_ge(p_done[l], u - 1)
                            for j in range(2):
                                row = 32 * (2 * (u % 2) + j)
                                b = ps[:, 2 * (u % 2) + j, :]
                                for i in range(TILES):
                                    keys = 128 * (i + 1) if causal else TOKENS
                                    mm = nc.tensor.matmul(b[:, TOKENS * i:TOKENS * i + keys],
                                                     qT[row:row + HEAD, u // 2, 128 * i:128 * (i + 1)],
                                                     kT[row:row + HEAD, u // 2, 0:keys],
                                                     start=(i == 0), stop=not causal, skip_group_check=True)
                            if causal:
                                for j in range(2):
                                    for i in range(TILES):
                                        at = TOKENS * i + 128 * i
                                        mm = nc.tensor.matmul(ps[:, 2 * (u % 2) + j, at:at + 128], identb[:, :],
                                                         maskq[:, :], start=False, stop=True,
                                                         skip_group_check=True)
                            mm.then_inc(s_done[l], 1)

                        def row_max(u):
                            pe.wait_ge(top_done[l], u + 1)
                            for i in range(TILES):
                                mm = nc.tensor.transpose(ps[:, 2 * (u % 2), 128 * i:128 * (i + 1)],
                                                         top[:, u % 2, i, :], ident[:, :])
                            mm.then_inc(top_turned[l], 1)

                        def shifted(u):
                            pe.wait_ge(q_shifted[l], u + 1)
                            for j in range(2):
                                row = 32 * (2 * (u % 2) + j)
                                b = ps[:, 2 * (u % 2) + j, :]
                                for i in range(TILES):
                                    q0 = 128 * i if causal else 0
                                    mm = nc.tensor.matmul(b[:, TOKENS * i + q0:TOKENS * (i + 1)],
                                                     kT[row:row + HEAD + 1, u // 2, 128 * i:128 * (i + 1)],
                                                     qT[row:row + HEAD + 1, u // 2, q0:TOKENS],
                                                     start=(i == 0), stop=not causal, skip_group_check=True)
                            if causal:
                                for j in range(2):
                                    for i in range(TILES):
                                        at = TOKENS * i + 128 * i
                                        mm = nc.tensor.matmul(ps[:, 2 * (u % 2) + j, at:at + 128], identb[:, :],
                                                         maskk[:, :], start=False, stop=True,
                                                         skip_group_check=True)
                            mm.then_inc(st_done[l], 1)

                        def context(u):
                            pe.wait_ge(p_done[l], u + 1)
                            for j in range(2):
                                head = 2 * u + j
                                for i in range(TILES):
                                    at = (i * HEADS + head) * (HEAD + 1)
                                    last = i if causal else TILES - 1
                                    for kt in range(last + 1):
                                        mm = nc.tensor.matmul(pm[:, at:at + HEAD + 1],
                                                              probs[u % 2][:, j, kt, 128 * i:128 * (i + 1)],
                                                              v_aug[:, kt, head, :],
                                                              start=(kt == 0), stop=(kt == last))
                            mm.then_inc(av_done[l], 1)

                        scores(0)
                        for u in range(UNITS):
                            if u + 1 < UNITS:
                                scores(u + 1)
                            row_max(u)
                            if u >= 1:
                                context(u - 1)
                            if l * UNITS + u >= 1:
                                a_scan(l * UNITS + u - 1)
                            shifted(u)
                        context(UNITS - 1)

                        pe.wait_ge(ctx_done[l], 1)
                        turn(ps[:, 0, :], ps[:, 1, :], ctx_tok).then_inc(ctx_turned[l], 1)
                        pe.wait_ge(ctxT_done[l], 2)
                        for tl in range(TILES):
                            mm = chunks(ps[:, 2, WIDTH * tl:WIDTH * (tl + 1)],
                                        lambda c, cn: hT[0:cn, c, 128 * tl:128 * (tl + 1)],
                                        lambda c, cn: w_o[l][0:cn, c, :])
                        mm.then_inc(proj_done[l], 1)

                    def up(e):
                        for m in range(HCH):
                            n = e * HCH + m
                            pair = n // 2
                            if m % 2 == 0 and pair >= 4:
                                pe.wait_ge(gelu_done, 2 * (pair - 3))
                            mm = chunks(ps[:, pair % 4, TOKENS * (m % 2):TOKENS * (m % 2 + 1)],
                                        lambda c, cn: w_up[0:cn, e, c, 128 * m:128 * (m + 1)],
                                        lambda c, cn: hT[0:cn, c, :])
                            if m % 2:
                                mm.then_inc(up_done, 1)

                    def down(e):
                        pe.wait_ge(gelu_done, HCH * (e + 1))
                        if e >= 2:
                            pe.wait_ge(dn_used, e - 1)
                        for tl in range(TILES):
                            for m in range(HCH):
                                mm = nc.tensor.matmul(pm[:, WIDTH * tl:WIDTH * (tl + 1)],
                                                      act[e % 2][:, m, 128 * tl:128 * (tl + 1)],
                                                      w_dn[:, e, m, :], start=(m == 0), stop=(m == HCH - 1))
                        mm.then_inc(dn_done, 1)

                    def mlp_and_experts():
                        pe.wait_ge(v2_done, 1)
                        turn(pm, ps[:, 3, :], v2).then_inc(m_turned[0], 1)
                        pe.wait_ge(mT_done[0], 2)
                        up(0)
                        down(0)
                        pe.wait_ge(xm_done, TILES)
                        turn(pm, ps[:, 3, :], h_tok).then_inc(m_turned[1], 1)
                        pe.wait_ge(mT_done[1], 2)
                        for tl in range(TILES):
                            mm = chunks(pm[:, EXPERTS * tl:EXPERTS * (tl + 1)],
                                        lambda c, cn: hT[0:cn, c, 128 * tl:128 * (tl + 1)],
                                        lambda c, cn: w_gate[0:cn, c, :])
                        mm.then_inc(lg_done, 1)
                        up(1)
                        pe.wait_ge(gate_done, 1)
                        for tl in range(TILES):
                            mm = nc.tensor.transpose(pm[0:EXPERTS, 128 * tl:128 * (tl + 1)],
                                                     gate[:, tl, :], ident[:, :])
                        mm.then_inc(gate_turned, 1)
                        pe.wait_ge(gateT_done, 1)
                        for tl in range(TILES):
                            mm = nc.tensor.matmul(pm[:, WIDTH * tl:WIDTH * (tl + 1)],
                                                  gateT[:, 128 * tl:128 * (tl + 1)], b_ex[:, :],
                                                  start=True, stop=True)
                        mm.then_inc(gb_done, 1)
                        pe.wait_ge(acc_done, 1)
                        for e in range(1, 1 + EXPERTS):
                            if e < EXPERTS:
                                up(e + 1)
                            down(e)

                    a_prep()
                    if run_b:
                        pe.wait_ge(w_b, 16 * len(b_loads))
                        attention(0)
                        attention(1)
                        a_scan(GROUPS - 1)
                        mlp_and_experts()
                    else:
                        for g in range(GROUPS):
                            a_scan(g)
                    a_post()

                @block.vector
                def _(dve):
                    link = chained(dve, dve_chain)

                    def norm(i, src, dst, count=TILES, done=None):
                        for tl in range(count):
                            ins = nc.vector.bn_stats(norm_raw[:, i, tl, :], src(tl))
                        link(ins)
                        for tl in range(count):
                            ins = nc.vector.bn_aggr(norm_mv[:, i, tl, :], norm_raw[:, i, tl, :])
                        link(ins)
                        nc.vector.tensor_scalar(norm_var[:, i, :], norm_mv[:, i, :, 1], EPS, None,
                                                ALU.add).then_inc(var_done[i], 1)
                        dve.wait_ge(rstd_done[i], 1)
                        link(nc.vector.scalar_tensor_tensor(
                            out=norm_shift[:, i, :], in0=norm_mv[:, i, :, 0], scalar=-1.0,
                            in1=norm_rstd[:, i, :], op0=ALU.mult, op1=ALU.mult))
                        for tl in range(count):
                            ins = nc.vector.tensor_scalar(dst(tl), src(tl), norm_rstd[:, i, tl:tl + 1],
                                                          norm_shift[:, i, tl:tl + 1], ALU.mult, ALU.add)
                            if done is not None:
                                ins.then_inc(done, 1)
                        return ins

                    def rows(gain):
                        return gain[:, :].unsqueeze(1).to_broadcast([128, TILES, gain.shape[1]])

                    def a_prep():
                        if not run_a:
                            return
                        dve.wait_ge(x_turned, 1)
                        xT = pa[1][:, :].rearrange("p (c l) -> p c l", c=2)
                        for c, (_, cn) in enumerate(CH):
                            ins = nc.vector.bn_stats(gn_raw[0:cn, c, :], xT[0:cn, c, :])
                        link(ins)
                        for c, (_, cn) in enumerate(CH):
                            ins = nc.vector.bn_aggr(gn_mv[0:cn, c, :], gn_raw[0:cn, c, :])
                        link(ins)
                        link(nc.vector.tensor_tensor(gn_sq[:, :], gn_mv[:, :, 0], gn_mv[:, :, 0], ALU.mult))
                        nc.vector.tensor_tensor(gn_mv[:, :, 1], gn_mv[:, :, 1], gn_sq[:, :],
                                                ALU.add).then_inc(gn_stats, 1)
                        dve.wait_ge(gn_sums, 1)
                        for c, (_, cn) in enumerate(CH):
                            ins = nc.vector.tensor_copy(gn_m[0:cn, c, :], pa[2][0:cn, 2 * c:2 * c + 2])
                        link(ins)
                        link(nc.vector.tensor_tensor(gn_sq[:, :], gn_m[:, :, 0], gn_m[:, :, 0], ALU.mult))
                        link(nc.vector.tensor_tensor(gn_var[:, :], gn_m[:, :, 1], gn_sq[:, :], ALU.subtract))
                        nc.vector.tensor_scalar(gn_var[:, :], gn_var[:, :], 0.0, EPS,
                                                ALU.max, ALU.add).then_inc(gn_v, 1)
                        dve.wait_ge(gn_r, 1)
                        link(nc.vector.scalar_tensor_tensor(
                            out=gn_shift[:, :], in0=gn_m[:, :, 0], scalar=-1.0, in1=gn_rstd[:, :],
                            op0=ALU.mult, op1=ALU.mult))
                        for c, (_, cn) in enumerate(CH):
                            nc.vector.tensor_scalar(xgT[0:cn, c, :], xT[0:cn, c, :], gn_rstd[0:cn, c:c + 1],
                                                    gn_shift[0:cn, c:c + 1], ALU.mult,
                                                    ALU.add).then_inc(xg_done, 1)
                        dve.wait_ge(xh_done, 1)
                        link(nc.vector.tensor_copy(pad[:, 1:SIDE + 1, 1:SIDE + 1],
                                                   pa[2][0:INNER, 0:TOKENS].rearrange("p (h w) -> p h w",
                                                                                      w=SIDE)))
                        conv2 = conv[:, :].rearrange("p (h w) -> p h w", w=SIDE)
                        for tap in range(9):
                            window = pad[:, tap // 3:tap // 3 + SIDE, tap % 3:tap % 3 + SIDE]
                            if tap == 0:
                                ins = nc.vector.tensor_scalar(conv2, window, w_conv[:, 0:1], b_conv[:, 0:1],
                                                              ALU.mult, ALU.add)
                            else:
                                ins = nc.vector.scalar_tensor_tensor(
                                    out=conv2, in0=window, scalar=w_conv[:, tap:tap + 1], in1=conv2,
                                    op0=ALU.mult, op1=ALU.add)
                            if tap < 8:
                                link(ins)
                        ins.then_inc(conv_done, 1)
                        dve.wait_ge(silu_e, 1)
                        link(nc.vector.tensor_scalar(z_e[:, :, :], z_e[:, :, :], 1.0, None, ALU.add))
                        link(nc.vector.reciprocal(z_e[:, :, :], z_e[:, :, :]))
                        nc.vector.tensor_tensor(z_gate[:, :, :], pa[1][:, 0:TILES * INNER]
                                                .rearrange("p (t c) -> p t c", t=TILES), z_e[:, :, :],
                                                ALU.mult).then_inc(z_used, 1)
                        dve.wait_ge(silu_e, 2)
                        link(nc.vector.tensor_scalar(conv_e[:, :], conv_e[:, :], 1.0, None, ALU.add))
                        link(nc.vector.reciprocal(conv_e[:, :], conv_e[:, :]))
                        nc.vector.tensor_tensor(xs[:, 0, :], conv[:, :], conv_e[:, :],
                                                ALU.mult).then_inc(u_done, 1)
                        dve.wait_ge(xd_done, 1)
                        nc.vector.tensor_copy(xdbl[:, 0:2, :], pa[1][0:RANK + 2 * STATE, :]
                                              .rearrange("p (k l) -> p k l", k=2)).then_inc(xd_copied, 1)
                        dve.wait_ge(dt_done, 1)
                        for k in range(PATHS):
                            ins = nc.vector.tensor_scalar(
                                delta[:, k, :], pa[1 + k // 2][0:INNER, TOKENS * (k % 2):TOKENS * (k % 2 + 1)],
                                b_dt[:, k:k + 1], None, ALU.add)
                        ins.then_inc(dt_sum, 1)
                        dve.wait_ge(sp_a, 1)
                        one_e, log_u = d_rows[0][0:INNER, :, :], d_rows[1][0:INNER, :, :]
                        nc.vector.tensor_scalar(one_e, delta_x[:, :, :], 1.0, None, ALU.add).then_inc(sp_u, 1)
                        dve.wait_ge(sp_u, 1)
                        link(nc.vector.scalar_tensor_tensor(
                            out=flat(delta_x), in0=one_e.rearrange("p k l -> p (k l)"), scalar=1.0,
                            in1=flat(delta_x), op0=ALU.subtract, op1=ALU.subtract))
                        link(nc.vector.scalar_tensor_tensor(
                            out=flat(delta), in0=flat(delta), scalar=0.0, in1=flat(delta_x),
                            op0=ALU.max, op1=ALU.subtract))
                        dve.wait_ge(sp_l, 1)
                        nc.vector.tensor_tensor(delta[:, :, :], delta[:, :, :], log_u,
                                                ALU.add).then_inc(d_done, 1)
                        dve.wait_ge(d_done, 1)
                        dve.wait_ge(xs_done, 1)
                        nc.vector.tensor_tensor(
                            delta_x[:, :, :].rearrange("p (d o) l -> p d (o l)", d=2),
                            delta[:, :, :].rearrange("p (d o) l -> p d (o l)", d=2),
                            xs[:, :, :].rearrange("p o l -> p (o l)").unsqueeze(1)
                            .to_broadcast([INNER, 2, 2 * TOKENS]), ALU.mult).then_inc(dx_done, 1)

                    def a_scan(g):
                        if not run_a:
                            return
                        dve.wait_ge(dx_in[g % 2], 16 * (g // 2 + 1))
                        if g == 0:
                            dve.wait_ge(bc_in, 16 * 2 * PACK)
                        link(nc.vector.tensor_tensor(dx_rows[g % 2][:, :], dx_rows[g % 2][:, :],
                                                     B_rows[:, :], ALU.mult))
                        dve.wait_ge(decay_done, g + 1)
                        if g >= 2:
                            dve.wait_ge(y_part, g - 1)
                        for both in (slice(0, 2 * TOKENS), slice(4 * TOKENS - 1, 2 * TOKENS - 1, -1)):
                            ins = nc.vector.tensor_tensor_scan(
                                flat(state[g % 2])[:, both], flat(decay[g % 2])[:, both],
                                dx_rows[g % 2][:, both], 0.0, ALU.mult, ALU.add)
                        ins.then_inc(scan_done, 1)

                    def a_post():
                        if not run_a:
                            return
                        dve.wait_ge(y_part, GROUPS)
                        link(norm(0, lambda tl: pa[0][:, INNER * tl:INNER * (tl + 1)],
                                  lambda tl: y_g[:, tl, :]))
                        link(nc.vector.tensor_tensor(y_g[:, :, :], y_g[:, :, :], rows(on_g), ALU.mult))
                        link(nc.vector.tensor_tensor(y_g[:, :, :], y_g[:, :, :], rows(on_b), ALU.add))
                        nc.vector.tensor_tensor(y_g[:, :, :], y_g[:, :, :], z_gate[:, :, :],
                                                ALU.mult).then_inc(yg_done, TILES)
                        dve.wait_ge(y_turned, 1)
                        nc.vector.tensor_copy(yT[:, :], pa[1][0:INNER, 0:TOKENS]).then_inc(yT_done, 1)
                        dve.wait_ge(o_done, 1)
                        if run_b:
                            dve.wait_ge(res_done[0], 1)
                        nc.vector.tensor_tensor(x1[:, :, :], pa[2][:, 0:TILES * WIDTH]
                                                .rearrange("p (t c) -> p t c", t=TILES), x_tok[:, :, :],
                                                ALU.add).then_inc(x1_done, 1)

                    def copy_first(done, src):
                        nc.vector.tensor_copy(hT[:, 0, :], src[:, 0:TOKENS]).then_inc(done, 1)

                    def attention(l):
                        causal = l == 0
                        dve.wait_ge(h_turned[l], 1)
                        copy_first(hT_done[l], pm)
                        for ht in range(HTILES):
                            dve.wait_ge(q_done[l], ht // 2 + 1)
                            nc.vector.tensor_scalar(qT[:, ht, :], head_rows(0, ht), b_q[l][:, ht:ht + 1],
                                                    HEAD ** -0.5, ALU.add, ALU.mult).then_inc(q_copied[l], 1)
                        dve.wait_ge(v_done[l], 1)
                        nc.vector.tensor_tensor(
                            v_aug[:, :, :, 0:HEAD],
                            pm[:, 0:TILES * WIDTH].rearrange("p (t h d) -> p t h d", t=TILES, d=HEAD),
                            b_v[l][:, :].rearrange("p (h d) -> p h d", d=HEAD).unsqueeze(1)
                            .to_broadcast([128, TILES, HEADS, HEAD]), ALU.add).then_inc(q_copied[l], 1)

                        def row_max(u):
                            dve.wait_ge(s_done[l], u + 1)
                            par = u % 2
                            first = 64 * par + HEAD
                            pair = ps[:, 2 * par:2 * par + 2, :]
                            if causal:
                                for i in range(TILES):
                                    ins = nc.vector.tensor_reduce(
                                        top[:, par, i, first:first + 33:32],
                                        pair[:, :, TOKENS * i:TOKENS * i + 128 * (i + 1)],
                                        AX.X, ALU.max, negate=True)
                            else:
                                ins = nc.vector.tensor_reduce(
                                    top[:, par, :, first:first + 33:32],
                                    pair.rearrange("p j (i k) -> p i j k", i=TILES),
                                    AX.X, ALU.max, negate=True)
                            ins.then_inc(top_done[l], 1)

                        def shift(u):
                            dve.wait_ge(top_turned[l], u + 1)
                            half_rows = slice(64 * (u % 2), 64 * (u % 2) + 64)
                            nc.vector.tensor_tensor(qT[half_rows, u // 2, :], qT[half_rows, u // 2, :],
                                                    ps[half_rows, 2 * (u % 2), 0:TOKENS],
                                                    ALU.add).then_inc(q_shifted[l], 1)

                        row_max(0)
                        for u in range(UNITS):
                            shift(u)
                            if u + 1 < UNITS:
                                row_max(u + 1)
                            a_scan(l * UNITS + u)
                        dve.wait_ge(av_done[l], UNITS)
                        sums = pm[:, 0:TILES * HEADS * (HEAD + 1)].rearrange("p (h d) -> p h d", d=HEAD + 1)
                        link(nc.vector.reciprocal(den[:, :], sums[:, :, HEAD]))
                        nc.vector.tensor_tensor(
                            ctx_tok[:, :, :].rearrange("p t (h d) -> p (t h) d", d=HEAD), sums[:, :, 0:HEAD],
                            den[:, :].unsqueeze(2).to_broadcast([128, TILES * HEADS, HEAD]),
                            ALU.mult).then_inc(ctx_done[l], 1)
                        dve.wait_ge(ctx_turned[l], 1)
                        copy_first(ctxT_done[l], ps[:, 0, :])
                        dve.wait_ge(proj_done[l], 1)
                        dve.wait_ge(res_done[l], 1)
                        return ps[:, 2, 0:TILES * WIDTH].rearrange("p (t c) -> p t c", t=TILES)

                    def two_tiles(bank):
                        return bank[:, 0:TILES * WIDTH].rearrange("p (t c) -> p t c", t=TILES)

                    def affine(i, src, done):
                        link(norm(2 + i + 1, src, lambda tl: h_tok[:, tl, :]))
                        link(nc.vector.tensor_tensor(h_tok[:, :, :], h_tok[:, :, :], rows(ln_g[i]), ALU.mult))
                        nc.vector.tensor_tensor(h_tok[:, :, :], h_tok[:, :, :], rows(ln_b[i]),
                                                ALU.add).then_inc(done, TILES)

                    def gates():
                        dve.wait_ge(lg_done, 1)
                        link(nc.vector.tensor_tensor(
                            logit[:, :, :], pm[:, 0:TILES * EXPERTS].rearrange("p (t e) -> p t e", t=TILES),
                            rows(b_gate), ALU.add))
                        for tl in range(TILES):
                            other = logit[:, tl, :].unsqueeze(1).to_broadcast([128, EXPERTS, EXPERTS])
                            own = logit[:, tl, :].unsqueeze(2).to_broadcast([128, EXPERTS, EXPERTS])
                            nc.vector.tensor_tensor(beats[:, tl, :, :], other, own, ALU.is_gt)
                            ins = nc.vector.tensor_tensor(ties[:, tl, :, :], other, own, ALU.is_equal)
                        nc.vector.tensor_reduce(best[:, :], logit[:, :, :], AX.X, ALU.max)
                        link(ins)
                        for tl in range(TILES):
                            ins = nc.vector.tensor_tensor(ties[:, tl, :, :], ties[:, tl, :, :],
                                                          lower[:, :, :], ALU.mult)
                        link(ins)
                        nc.vector.tensor_tensor(gate[:, :, :], logit[:, :, :],
                                                best[:, :].unsqueeze(2).to_broadcast([128, TILES, EXPERTS]),
                                                ALU.subtract).then_inc(lg_shift, 1)
                        link(nc.vector.tensor_tensor(beats[:, :, :, :], beats[:, :, :, :], ties[:, :, :, :],
                                                     ALU.add))
                        link(nc.vector.tensor_reduce(rank[:, :, :], beats[:, :, :, :], AX.X, ALU.add))
                        dve.wait_ge(gate_e, 1)
                        link(nc.vector.scalar_tensor_tensor(
                            out=gate[:, :, :], in0=rank[:, :, :], scalar=TOPK - 0.5, in1=gate[:, :, :],
                            op0=ALU.is_lt, op1=ALU.mult))
                        link(nc.vector.tensor_reduce(gsumr[:, :], gate[:, :, :], AX.X, ALU.add))
                        link(nc.vector.reciprocal(gsumr[:, :], gsumr[:, :]))
                        nc.vector.tensor_tensor(gate[:, :, :], gate[:, :, :],
                                                gsumr[:, :].unsqueeze(2).to_broadcast([128, TILES, EXPERTS]),
                                                ALU.mult).then_inc(gate_done, 1)
                        dve.wait_ge(gate_done, 1)
                        dve.wait_ge(gate_turned, 1)
                        nc.vector.tensor_copy(gateT[:, :], pm[0:EXPERTS, 0:TOKENS]).then_inc(gateT_done, 1)

                    def phase_b():
                        dve.wait_ge(w_b, 16 * len(b_loads))
                        norm(1, lambda tl: x1[:, tl, :], lambda tl: h_tok[:, tl, :], done=h_done[0])
                        summed = attention(0)
                        link(nc.vector.tensor_tensor(x2[:, :, :], summed, res[:, :, :], ALU.add))
                        link(norm(2, lambda tl: x2[:, tl, :], lambda tl: v_tok[:, tl, :]))
                        affine(0, lambda tl: v_tok[:, tl, :], h_done[1])
                        summed = attention(1)
                        nc.vector.tensor_tensor(v2[:, :, :], summed, res[:, :, :], ALU.add).then_inc(v2_done, 1)
                        dve.wait_ge(m_turned[0], 1)
                        copy_first(mT_done[0], pm)
                        dve.wait_ge(dn_done, 1)
                        dve.wait_ge(mres_done, 1)
                        nc.vector.tensor_tensor(v3[:, :, :], two_tiles(pm), res[:, :, :],
                                                ALU.add).then_inc(v3_done, 1)
                        dve.wait_ge(v3_done, 1)
                        affine(1, lambda tl: v3[:, tl, :], xm_done)
                        dve.wait_ge(m_turned[1], 1)
                        copy_first(mT_done[1], pm)
                        gates()
                        dve.wait_ge(gb_done, 1)
                        dve.wait_ge(base_done, 1)
                        nc.vector.tensor_tensor(out_tok[:, :, :], two_tiles(pm), out_tok[:, :, :],
                                                ALU.add).then_inc(acc_done, 1)
                        dve.wait_ge(acc_done, 1)
                        for e in range(1, 1 + EXPERTS):
                            dve.wait_ge(dn_done, e + 1)
                            for tl in range(TILES):
                                ins = nc.vector.scalar_tensor_tensor(
                                    out=out_tok[:, tl, :], in0=pm[:, WIDTH * tl:WIDTH * (tl + 1)],
                                    scalar=gate[:, tl, e - 1:e], in1=out_tok[:, tl, :],
                                    op0=ALU.mult, op1=ALU.add)
                                if e == EXPERTS:
                                    ins.then_inc(out_done, 1)
                            if e < EXPERTS:
                                ins.then_inc(dn_used, 1)
                                dve.wait_ge(dn_used, e)

                    a_prep()
                    if run_b:
                        phase_b()
                    else:
                        for g in range(GROUPS):
                            a_scan(g)
                    a_post()

                @block.scalar
                def _(sc):
                    link = chained(sc, act_chain)

                    def a_prep():
                        if not run_a:
                            return
                        sc.wait_ge(z_done, 1)
                        nc.scalar.activation(z_e[:, :, :], pa[1][:, 0:TILES * INNER]
                                             .rearrange("p (t c) -> p t c", t=TILES), ACT.Exp,
                                             scale=-1.0).then_inc(silu_e, 1)
                        sc.wait_ge(conv_done, 1)
                        nc.scalar.activation(conv_e[:, :], conv[:, :], ACT.Exp, scale=-1.0).then_inc(silu_e, 1)
                        sc.wait_ge(xd_done, 2)
                        nc.scalar.activation(xdbl[:, 2:4, :], pa[2][0:RANK + 2 * STATE, :]
                                             .rearrange("p (k l) -> p k l", k=2),
                                             ACT.Copy).then_inc(xd_copied, 1)
                        sc.wait_ge(dt_sum, 1)
                        link(nc.scalar.activation(delta_x[:, :, :], delta[:, :, :], ACT.Abs))
                        nc.scalar.activation(delta_x[:, :, :], delta_x[:, :, :], ACT.Exp,
                                             scale=-1.0).then_inc(sp_a, 1)
                        sc.wait_ge(sp_u, 1)
                        nc.scalar.activation(d_rows[1][0:INNER, :, :], d_rows[0][0:INNER, :, :],
                                             ACT.Ln).then_inc(sp_l, 1)

                    def a_scan(g):
                        if not run_a:
                            return
                        sc.wait_ge(d_in[g % 2], 16 * (g // 2 + 1))
                        if g >= 2:
                            sc.wait_ge(scan_done, g - 1)
                        for k in range(PATHS):
                            at = g * PATHS + k
                            rest = slice(1, TOKENS) if k < 2 else slice(0, TOKENS - 1)
                            ins = nc.scalar.activation(decay[g % 2][:, k, rest], d_rows[g % 2][:, k, rest],
                                                       ACT.Exp, scale=a_neg[:, at:at + 1])
                        ins.then_inc(decay_done, 1)

                    def copy_second(done, src):
                        nc.scalar.activation(hT[0:64, 1, :], src[0:64, 0:TOKENS],
                                             ACT.Copy).then_inc(done, 1)

                    def attention(l):
                        causal = l == 0
                        sc.wait_ge(h_turned[l], 1)
                        copy_second(hT_done[l], ps[:, 3, :])
                        for ht in range(HTILES):
                            sc.wait_ge(k_done[l], ht // 2 + 1)
                            nc.scalar.activation(kT[:, ht, :], head_rows(2, ht), ACT.Identity,
                                                 bias=b_k[l][:, ht:ht + 1]).then_inc(k_copied[l], 1)
                        for u in range(UNITS):
                            a_scan(l * UNITS + u)
                            sc.wait_ge(st_done[l], u + 1)
                            if u >= 2:
                                sc.wait_ge(av_done[l], u - 1)
                            pair = ps[:, 2 * (u % 2):2 * (u % 2) + 2, :]
                            if causal:
                                for kt in range(TILES):
                                    ins = nc.scalar.activation(
                                        probs[u % 2][:, :, kt, 128 * kt:TOKENS],
                                        pair[:, :, TOKENS * kt + 128 * kt:TOKENS * (kt + 1)], ACT.Exp)
                            else:
                                ins = nc.scalar.activation(
                                    probs[u % 2][:, :, :, :].rearrange("p j t q -> p j (t q)"), pair, ACT.Exp)
                            ins.then_inc(p_done[l], 1)
                        sc.wait_ge(ctx_turned[l], 1)
                        copy_second(ctxT_done[l], ps[:, 1, :])

                    def gelu(e):
                        for m in range(HCH):
                            n = e * HCH + m
                            sc.wait_ge(up_done, n // 2 + 1)
                            if m == 0 and e >= 2:
                                sc.wait_ge(dn_done, e - 1)
                            nc.scalar.activation(act[e % 2][:, m, :],
                                                 ps[:, n // 2 % 4, TOKENS * (n % 2):TOKENS * (n % 2 + 1)],
                                                 ACT.Gelu, bias=b_up[:, e, m:m + 1]).then_inc(gelu_done, 1)

                    def phase_b():
                        sc.wait_ge(w_b, 16 * len(b_loads))
                        attention(0)
                        attention(1)
                        sc.wait_ge(m_turned[0], 1)
                        copy_second(mT_done[0], ps[:, 3, :])
                        gelu(0)
                        sc.wait_ge(m_turned[1], 1)
                        copy_second(mT_done[1], ps[:, 3, :])
                        sc.wait_ge(lg_shift, 1)
                        nc.scalar.activation(gate[:, :, :], gate[:, :, :], ACT.Exp).then_inc(gate_e, 1)
                        for e in range(1, 1 + EXPERTS):
                            gelu(e)

                    a_prep()
                    if run_b:
                        phase_b()
                    else:
                        for g in range(GROUPS):
                            a_scan(g)

                @block.gpsimd
                def _(pool):
                    def rstd(i):
                        pool.wait_ge(var_done[i], 1)
                        nc.gpsimd.tensor_tensor(norm_rstd[:, i, :], norm_var[:, i, :], half[:, :],
                                                ALU.pow).then_inc(rstd_done[i], 1)

                    def a_prep():
                        if not run_a:
                            return
                        pool.wait_ge(gn_v, 1)
                        nc.gpsimd.tensor_tensor(gn_rstd[:, :], gn_var[:, :], half[:, :],
                                                ALU.pow).then_inc(gn_r, 1)
                        pool.wait_ge(u_done, 1)
                        nc.gpsimd.tensor_copy(xs[:, 1, :].rearrange("p (w h) -> p w h", h=SIDE),
                                              xs[:, 0, :].rearrange("p (h w) -> p w h", w=SIDE)
                                              ).then_inc(xs_done, 1)

                    def a_scan(g):
                        if not run_a:
                            return
                        pool.wait_ge(scan_done, g + 1)
                        if g == 0:
                            pool.wait_ge(bc_in, 16 * 2 * PACK)
                        C_path = C_rows[:, :].rearrange("p (k l) -> p k l", k=PATHS)
                        nc.gpsimd.tensor_tensor(state[g % 2][:, 0::2, :], state[g % 2][:, 0::2, :],
                                                C_path[:, 0::2, :], ALU.mult)
                        nc.gpsimd.tensor_tensor(
                            by_row[g % 2][:, :, :].rearrange("p k (h w) -> p k w h", w=SIDE),
                            state[g % 2][:, 1::2, :].rearrange("p k (w h) -> p k w h", h=SIDE),
                            C_path[:, 1::2, :].rearrange("p k (w h) -> p k w h", h=SIDE),
                            ALU.mult).then_inc(sc_done, 1)

                    def rows(gain):
                        return gain[:, :].unsqueeze(1).to_broadcast([128, TILES, gain.shape[1]])

                    def phase_b():
                        pool.wait_ge(w_b, 16 * len(b_loads))
                        rstd(1)
                        nc.gpsimd.tensor_tensor(res[:, :, :], x1[:, :, :], rows(b_o[0]),
                                                ALU.add).then_inc(res_done[0], 1)
                        for g in range(UNITS):
                            a_scan(g)
                        rstd(2)
                        rstd(3)
                        pool.wait_ge(h_done[1], TILES)
                        nc.gpsimd.tensor_tensor(res[:, :, :], v_tok[:, :, :], rows(b_o[1]),
                                                ALU.add).then_inc(res_done[1], 1)
                        for g in range(UNITS, GROUPS):
                            a_scan(g)
                        pool.wait_ge(v2_done, 1)
                        nc.gpsimd.tensor_tensor(res[:, :, :], v2[:, :, :], rows(b_dn),
                                                ALU.add).then_inc(mres_done, 1)
                        pool.wait_ge(v3_done, 1)
                        rstd(4)
                        nc.gpsimd.tensor_tensor(out_tok[:, :, :], v3[:, :, :], x2[:, :, :],
                                                ALU.add).then_inc(base_done, 1)

                    a_prep()
                    if run_b:
                        phase_b()
                    else:
                        for g in range(GROUPS):
                            a_scan(g)
                    if run_a:
                        rstd(0)

            nc.all_engine_barrier(sems_to_clear=clear_range)

        image(0, None)
        with nc.Fori(1, IMAGES) as n:
            image(n, n - 1)
        image(None, IMAGES - 1)


_HOST = {
    "x": (IMAGES, TOKENS, WIDTH), "w_in": (WIDTH, 2 * INNER), "w_conv": (INNER, 9), "b_conv": (INNER, 1),
    "w_x": (INNER, PATHS, RANK + 2 * STATE), "w_dt": (RANK, PATHS, INNER), "b_dt": (INNER, PATHS),
    "a_log": (128, GROUPS * PATHS), "ds": (INNER, PATHS), "on_g": (INNER,), "on_b": (INNER,),
    "w_out": (INNER, WIDTH),
    "w_qkv0": (WIDTH, 3 * WIDTH), "b_qkv0": (3 * WIDTH,), "w_o0": (WIDTH, WIDTH), "b_o0": (WIDTH,),
    "w_qkv1": (WIDTH, 3 * WIDTH), "b_qkv1": (3 * WIDTH,), "w_o1": (WIDTH, WIDTH), "b_o1": (WIDTH,),
    "ln_g0": (WIDTH,), "ln_b0": (WIDTH,), "ln_g1": (WIDTH,), "ln_b1": (WIDTH,),
    "mlp_w1": (WIDTH, HIDDEN), "mlp_w2": (HIDDEN, WIDTH), "mlp_b2": (WIDTH,),
    "exp_w1": (EXPERTS, WIDTH, HIDDEN), "exp_w2": (EXPERTS, HIDDEN, WIDTH), "exp_b2": (EXPERTS, WIDTH),
    "b_up": (128, 1 + EXPERTS, HCH), "w_gate": (WIDTH, EXPERTS), "b_gate": (EXPERTS,),
}


def kernel(**inputs):
    import numpy as np
    import concourse.bacc as bacc
    from concourse.bass_utils import run_bass_kernel_spmd

    i = {k: np.asarray(v) for k, v in inputs.items()}
    host = {
        "x": i["x"].reshape(IMAGES, TOKENS, WIDTH),
        "w_in": i["L0_conv_in_proj_w"].T,
        "w_conv": i["L0_conv_conv_w"].reshape(INNER, 9),
        "b_conv": i["L0_conv_conv_b"].reshape(INNER, 1),
        "w_x": i["L0_conv_x_proj_w"].transpose(2, 0, 1),
        "w_dt": i["L0_conv_dt_projs_w"].transpose(2, 0, 1),
        "b_dt": i["L0_conv_dt_projs_b"].T,
        "a_log": i["L0_conv_A_logs"].reshape(PATHS, GROUPS, PACK, STATE).transpose(2, 3, 1, 0)
        .reshape(128, GROUPS * PATHS),
        "ds": i["L0_conv_Ds"].reshape(PATHS, INNER).T,
        "on_g": i["L0_conv_out_norm_g"], "on_b": i["L0_conv_out_norm_b"],
        "w_out": i["L0_conv_out_proj_w"].T,
        "w_qkv0": i["L1_attn_W_attn"], "b_qkv0": i["L1_attn_b_attn"],
        "w_o0": i["L1_attn_W_proj"], "b_o0": i["L1_attn_b_proj"],
        "w_qkv1": i["L1_ffn_in_w"].T, "b_qkv1": i["L1_ffn_in_b"],
        "w_o1": i["L1_ffn_out_w"].T, "b_o1": i["L1_ffn_out_b"],
        "ln_g0": i["L1_ffn_ln1_g"], "ln_b0": i["L1_ffn_ln1_b"],
        "ln_g1": i["L1_ffn_ln2_g"], "ln_b1": i["L1_ffn_ln2_b"],
        "mlp_w1": i["L1_ffn_mlp_w1"], "mlp_w2": i["L1_ffn_mlp_w2"], "mlp_b2": i["L1_ffn_mlp_b2"],
        "exp_w1": i["L1_ffn_exp_w1"], "exp_w2": i["L1_ffn_exp_w2"], "exp_b2": i["L1_ffn_exp_b2"],
        "b_up": np.concatenate([i["L1_ffn_mlp_b1"][None], i["L1_ffn_exp_b1"]])
        .reshape(1 + EXPERTS, HCH, 128).transpose(2, 0, 1),
        "w_gate": i["L1_ffn_gate_w"].T, "b_gate": i["L1_ffn_gate_b"],
    }
    nc = bacc.Bacc("TRN2", target_bir_lowering=False, num_devices=1)
    t, arrays = {}, {}
    for name, shape in _HOST.items():
        arrays[f"{name}_dram"] = np.ascontiguousarray(host[name])
        assert arrays[f"{name}_dram"].shape == shape
        t[name] = nc.dram_tensor(f"{name}_dram", shape, F32, kind="ExternalInput").ap()
    t["out"] = nc.dram_tensor("out_dram", (IMAGES, TOKENS, WIDTH), F32, kind="ExternalOutput").ap()
    build(nc, t)
    r = run_bass_kernel_spmd(nc, [arrays], core_ids=[0])
    return r.results[0]["out_dram"].reshape(IMAGES, SIDE, SIDE, WIDTH)
```

```python
from contextlib import ExitStack

import concourse.bass as bass
from concourse import mybir

F32 = mybir.dt.float32
BF16 = mybir.dt.bfloat16
F32R = mybir.dt.float32r
ALU = mybir.AluOpType
ACT = mybir.ActivationFunctionType
AX = mybir.AxisListType

IMAGES, SIDE, WIDTH = 4, 16, 192
TOKENS = SIDE * SIDE
TILES = TOKENS // 128
INNER, STATE, PATHS, RANK = 96, 16, 4, 12
PACK = 128 // STATE
GROUPS = INNER // PACK
GN_GROUP = WIDTH // 32
HEADS, HEAD = 12, 16
QUAD = 4
HTILES = HEADS // QUAD
UNITS = HEADS // 2
HIDDEN, EXPERTS, TOPK = 768, 4, 2
HCH = HIDDEN // 128
CGROUP = WIDTH // 2
HIGH_PARTS = [slice(0, 3, 2), slice(0, 2)]
LOW_PARTS = [slice(1, 2), slice(2, 3)]
TOP_ROW = 3 * HEAD
CH = [(0, 128), (128, 64)]
EPS = 1e-5
MASKED = -1e30
A_LOG_MAX = 80.0

SLOTS = [(l, s) for l in range(2) for s in ("turned", "projected", *range(2 * UNITS), "context", "spread",
                                            "output")]

SSM_STEPS = {
    (0, "turned"): [("x_turn",)],
    (0, "projected"): [("group_sums",)],
    (0, 1): [("in_proj",)],
    (0, 2): [("silu",)],
    (0, 5): [("x_dbl", 0)],
    (0, 6): [("x_dbl", 1)],
    (0, 7): [("dt", 0)],
    (0, 8): [("dt", 1)],
    (0, 9): [("softplus", 0)],
    (0, 10): [("softplus", 1)],
    (0, "context"): [("softplus_log",)],
    (1, 9): [("y_copy",)],
    (1, 10): [("y_norm",)],
    (1, "context"): [("y_turn",)],
    (1, "spread"): [("y_out",)],
}
DECAYS = {
    (0, "spread"): [0, 1],
    (0, "output"): [2],
    (1, "turned"): [3],
    (1, "projected"): [4],
    (1, 0): [5],
    (1, 1): [6],
    (1, 2): [7],
    (1, 3): [8],
    (1, 5): [9],
    (1, 6): [10],
    (1, 7): [11],
}
SCANS = {
    (0, "output"): [0, 1],
    (1, "projected"): [2],
    (1, 0): [3],
    (1, 1): [4],
    (1, 2): [5],
    (1, 3): [6, 7],
    (1, 4): [8],
    (1, 6): [9],
    (1, 7): [10, 11],
}
Y_SUMS = {
    (1, "projected"): [0, 1],
    (1, 0): [2],
    (1, 1): [3],
    (1, 2): [4],
    (1, 3): [5],
    (1, 4): [6],
    (1, 5): [7],
    (1, 6): [8],
    (1, 7): [9, 10],
    (1, 9): [11],
}

FFN_STEPS = {
    (0, "turned"): [("turn", 0)],
    (0, "projected"): [("up", 0, 0)],
    (0, 0): [("up", 0, 1)],
    (0, 1): [("up", 0, 2)],
    (0, 2): [("down", 0, 0)],
    (0, 3): [("down", 0, 1)],
    (0, 4): [("norm", 0)],
    (0, 6): [("norm", 1), ("turn", 1)],
    (0, 7): [("up", 1, 0)],
    (0, 8): [("logits",)],
    (0, 9): [("up", 1, 1)],
    (0, 10): [("turn_gates",)],
    (0, "context"): [("bias",)],
    (0, "spread"): [("up", 1, 2)],
    (0, "output"): [("up", 2, 0), ("down", 1, 0), ("up", 2, 1), ("down", 1, 1), ("up", 2, 2), ("add", 1)],
    (1, "turned"): [("up", 3, 0)],
    (1, "projected"): [("down", 2, 0)],
    (1, 0): [("down", 2, 1)],
    (1, 1): [("up", 3, 1), ("add", 2)],
    (1, 2): [("up", 3, 2)],
    (1, 4): [("down", 3, 0)],
    (1, 5): [("up", 4, 0)],
    (1, 7): [("down", 3, 1), ("up", 4, 1), ("add", 3)],
    (1, 9): [("up", 4, 2)],
    (1, 10): [("down", 4, 0)],
    (1, "context"): [("down", 4, 1)],
    (1, "spread"): [("add", 4)],
}


def build(nc, t):
    ctx = ExitStack()
    with ctx:
        def sb(name, shape, dt=F32):
            return ctx.enter_context(nc.sbuf_tensor(name, shape, dt))

        def bank(name):
            return ctx.enter_context(nc.psum_tensor(name, [128, 512], F32))

        def sem(name):
            return ctx.enter_context(nc.semaphore(name))

        ident = sb("ident", [128, 128])
        identb = sb("identb", [128, 128], BF16)
        maskq = sb("maskq", [128, 128], BF16)
        maskk = sb("maskk", [128, 128], BF16)
        gsum = sb("gsum", [128, 2, WIDTH])
        sel = sb("sel", [128, (2 * GROUPS - 1) * PACK])
        den_sel = sb("den_sel", [128, QUAD, 32])
        dsum = sb("dsum", [INNER, 1])
        ddiag = sb("ddiag", [INNER, INNER])
        half = sb("half", [128, 2])
        lower = sb("lower", [128, EXPERTS, EXPERTS])
        w_in = sb("w_in", [128, 2, WIDTH])
        w_conv = sb("w_conv", [INNER, 9])
        b_conv = sb("b_conv", [INNER, 1])
        w_x = sb("w_x", [INNER, PATHS, RANK + 2 * STATE])
        w_dt = sb("w_dt", [RANK, PATHS, INNER])
        b_dt = sb("b_dt", [INNER, PATHS])
        a_log = sb("a_log", [128, GROUPS * PATHS])
        a_neg = sb("a_neg", [128, GROUPS * PATHS])
        ds_in = sb("ds_in", [INNER, PATHS])
        on_g = sb("on_g", [128, INNER])
        on_b = sb("on_b", [128, INNER])
        w_out = sb("w_out", [INNER, WIDTH])
        w_qkv = [sb(f"w_qkv{l}", [128, 2, 3 * WIDTH]) for l in range(2)]
        to_stack = sb("to_stack", [128, 2, 2, 128], F32R)
        top_one = sb("top_one", [128, 1])
        w_o = [sb(f"w_o{l}", [128, HTILES, WIDTH]) for l in range(2)]
        b_qk = [sb(f"b_qk{l}", [CGROUP, 2, 2]) for l in range(2)]
        b_v = [sb(f"b_v{l}", [128, WIDTH]) for l in range(2)]
        b_o = [sb(f"b_o{l}", [128, WIDTH]) for l in range(2)]
        ln_g = [sb(f"ln_g{i}", [128, WIDTH]) for i in range(2)]
        ln_b = [sb(f"ln_b{i}", [128, WIDTH]) for i in range(2)]
        w_up = sb("w_up", [128, 1 + EXPERTS, 2, HIDDEN])
        b_up = sb("b_up", [128, 1 + EXPERTS, HCH])
        w_dn = sb("w_dn", [128, 1 + EXPERTS, HCH, WIDTH])
        b_dn = sb("b_dn", [128, WIDTH])
        b_ex = sb("b_ex", [EXPERTS, WIDTH])
        w_gate = sb("w_gate", [128, 2, EXPERTS])
        b_gate = sb("b_gate", [128, EXPERTS])

        x_tok = sb("x_tok", [128, TILES, WIDTH])
        gn_raw = sb("gn_raw", [128, 2, 6])
        gn_mv = sb("gn_mv", [128, 2, 2])
        gn_sq = sb("gn_sq", [128, 2])
        gn_m = sb("gn_m", [128, 2, 2])
        gn_var = sb("gn_var", [128, 2])
        gn_rstd = sb("gn_rstd", [128, 2])
        gn_shift = sb("gn_shift", [128, 2])
        pad = sb("pad", [INNER, SIDE + 2, SIDE + 2])
        z_gate = sb("z_gate", [128, TILES, INNER])
        xs = sb("xs", [INNER, 2, TOKENS])
        xdbl = sb("xdbl", [RANK + 2 * STATE, PATHS, TOKENS])
        delta = sb("delta", [INNER, PATHS, TOKENS])
        delta_x = sb("delta_x", [INNER, PATHS, TOKENS])
        B_rows = sb("B_rows", [128, PATHS * TOKENS])
        C_rows = sb("C_rows", [128, PATHS * TOKENS])
        d_rows = [sb(f"d_rows{i}", [128, PATHS, TOKENS]) for i in range(2)]
        dx_rows = [sb(f"dx_rows{i}", [128, PATHS * TOKENS]) for i in range(2)]
        decay = [sb(f"decay{i}", [128, PATHS, TOKENS]) for i in range(2)]
        state = [sb(f"state{i}", [128, PATHS, TOKENS]) for i in range(2)]
        by_row = [sb(f"by_row{i}", [128, 2, TOKENS]) for i in range(2)]
        xgT = state[0][:, 0:2, :]
        conv = state[0][0:INNER, 2, :]
        conv_e = state[0][0:INNER, 3, :]
        z_e = state[1][:, 0, 0:TILES * INNER].rearrange("p (t c) -> p t c", t=TILES)
        y_g = by_row[1][:, 0, 0:TILES * INNER].rearrange("p (t c) -> p t c", t=TILES)
        yT = by_row[0][0:INNER, 0, :]
        x1 = sb("x1", [128, TILES, WIDTH])

        norm_raw = sb("norm_raw", [128, 5, TILES, 6])
        norm_mv = sb("norm_mv", [128, 5, TILES, 2])
        norm_var = sb("norm_var", [128, 5, TILES])
        norm_rstd = sb("norm_rstd", [128, 5, TILES])
        norm_shift = sb("norm_shift", [128, 5, TILES])
        h_tok = sb("h_tok", [128, TILES, WIDTH])
        hT = sb("hT", [128, 2, TOKENS])
        q_stack = sb("q_stack", [128, UNITS, TOKENS], F32R)
        k_stack = sb("k_stack", [128, UNITS, TOKENS], F32R)
        high = [[stack[0:CGROUP, 2 + 2 * c, :] for c in range(2)] for stack in (q_stack, k_stack)]
        low = [[stack[0:CGROUP, 3 + 2 * c, :] for c in range(2)] for stack in (q_stack, k_stack)]
        v_aug = sb("v_aug", [128, TILES, HEADS, 32])
        top = sb("top", [128, 2, TILES, 128], F32R)
        probs = [sb(f"probs{i}", [128, 2, 2, TOKENS]) for i in range(2)]
        inv_den = sb("inv_den", [128, TOKENS])
        cT = sb("cT", [128, HTILES, TOKENS])
        x2 = sb("x2", [128, TILES, WIDTH])
        v_tok = sb("v_tok", [128, TILES, WIDTH])
        v2 = sb("v2", [128, TILES, WIDTH])
        f_tok = sb("f_tok", [128, TILES, WIDTH])
        fT = sb("fT", [128, 2, TOKENS])
        v3 = sb("v3", [128, TILES, WIDTH])
        act = [sb(f"act{i}", [128, HCH, TOKENS]) for i in range(2)]
        logit = sb("logit", [128, TILES, EXPERTS])
        beats = sb("beats", [128, TILES, EXPERTS, EXPERTS])
        ties = sb("ties", [128, TILES, EXPERTS, EXPERTS])
        rank = sb("rank", [128, TILES, EXPERTS])
        best = sb("best", [128, TILES])
        gate = sb("gate", [128, TILES, EXPERTS])
        gsumr = sb("gsumr", [128, TILES])
        gateT = sb("gateT", [EXPERTS, TOKENS])
        out_tok = sb("out_tok", [128, TILES, WIDTH])

        ps = ctx.enter_context(nc.psum_tensor("ps", [128, 4, 512], F32))
        pm = bank("pm")
        py = bank("py")
        pu = bank("pu")
        pd = bank("pd")

        w_a = sem("weights_a_loaded")
        w_b = sem("weights_b_loaded")
        zeroed = sem("zeroed")
        cleared = sem("values_cleared")
        consts = sem("constants_built")
        pool_set = sem("pool_setup_chain")
        pool_late = sem("attention_constants_chain")
        ready_a = sem("decay_rates_ready")

        per_image = []

        def isem(name):
            s = sem(name)
            per_image.append(s)
            return s

        x_in = isem("x_loaded")
        x_turned = isem("x_turned")
        gn_stats = isem("gn_channel_stats")
        gn_sums = isem("gn_group_sums")
        gn_v = isem("gn_variance")
        gn_r = isem("gn_rstd")
        xg_done = isem("x_group_normed")
        xh_done = isem("conv_input_and_z_ready")
        conv_done = isem("conv_done")
        silu_e = isem("silu_exponentials")
        u_done = isem("scan_input_ready")
        z_copied = isem("z_copied")
        xs_done = isem("scan_orders_ready")
        xd_done = isem("x_dbl_ready")
        xd_copied = isem("x_dbl_copied")
        bc_in = isem("BC_rows_loaded")
        dt_done = isem("dt_ready")
        dt_sum = isem("dt_with_bias_ready")
        sp_a = isem("softplus_exp_ready")
        sp_u = isem("softplus_sum_ready")
        sp_l = isem("softplus_log_ready")
        d_done = isem("delta_ready")
        dx_done = isem("delta_x_ready")
        d_in = [isem(f"delta_rows_loaded{i}") for i in range(2)]
        dx_in = [isem(f"delta_x_rows_loaded{i}") for i in range(2)]
        decay_done = isem("decay_ready")
        scan_done = isem("state_scanned")
        sc_done = isem("state_times_C")
        y_part = isem("y_group_summed")
        yg_done = isem("y_gated")
        y_back = isem("y_by_tokens")
        y_turned = isem("y_turned")
        yT_done = isem("yT_copied")
        o_done = isem("scan_output_projected")
        x1_done = isem("x1_ready")
        var_done = [isem(f"variance_ready{i}") for i in range(5)]
        rstd_done = [isem(f"rstd_ready{i}") for i in range(5)]
        h_done = isem("normed_ready")
        h_turned = [isem(f"normed_turned{i}") for i in range(2)]
        hT_done = [isem(f"normed_T_copied{i}") for i in range(2)]
        v_done = [isem(f"values_projected{i}") for i in range(2)]
        qk_done = [isem(f"queries_keys_projected{i}") for i in range(2)]
        high_done = [isem(f"high_parts_ready{i}") for i in range(2)]
        low_done = [isem(f"low_parts_ready{i}") for i in range(2)]
        v_copied = [isem(f"values_copied{i}") for i in range(2)]
        stack_psum = [isem(f"stack_in_psum{i}") for i in range(2)]
        stack_even = [isem(f"even_stack_copied{i}") for i in range(2)]
        stack_odd = [isem(f"odd_stack_copied{i}") for i in range(2)]
        s_done = [isem(f"scores_ready{i}") for i in range(2)]
        top_done = [isem(f"row_max_ready{i}") for i in range(2)]
        top_turned = [isem(f"row_max_turned{i}") for i in range(2)]
        q_shifted = [isem(f"row_max_in_q{i}") for i in range(2)]
        st_done = [isem(f"shifted_scores_ready{i}") for i in range(2)]
        p_done = [isem(f"probs_ready{i}") for i in range(2)]
        av_done = [isem(f"context_summed{i}") for i in range(2)]
        ctx_done = [isem(f"context_ready{i}") for i in range(2)]
        ctx_copied = [isem(f"context_copied{i}") for i in range(2)]
        den_inv = [isem(f"sums_inverted{i}") for i in range(2)]
        den_done = [isem(f"sums_spread{i}") for i in range(2)]
        proj_done = [isem(f"attention_projected{i}") for i in range(2)]
        res_done = [isem(f"residual_ready{i}") for i in range(2)]
        x2_kept = isem("x2_kept")
        m_turned = isem("ffn_input_turned")
        mT_done = isem("ffn_input_T_copied")
        v2_done = isem("v2_ready")
        mres_done = isem("mlp_residual_ready")
        xm_done = isem("moe_input_ready")
        v3_done = isem("v3_ready")
        base_done = isem("output_residual_ready")
        up_done = isem("hidden_ready")
        gelu_done = isem("gelu_ready")
        dn_done = isem("down_ready")
        dn_used = isem("down_used")
        lg_done = isem("logits_ready")
        lg_shift = isem("logits_shifted")
        gate_e = isem("gate_exponentials")
        gate_done = isem("gates_ready")
        gate_turned = isem("gates_turned")
        gateT_done = isem("gates_T_copied")
        gb_done = isem("gated_biases_ready")
        acc_done = isem("output_started")
        out_done = isem("output_ready")
        stored = isem("output_stored")
        dve_chain = isem("vector_chain")
        act_chain = isem("scalar_chain")
        pool_chain = isem("gpsimd_chain")
        numbers = sorted(s.num for s in per_image)
        assert numbers == list(range(numbers[0], numbers[0] + len(numbers)))
        clear_range = range(numbers[0], numbers[-1] + 1)

        def chained(eng, chain):
            count = [0]

            def link(ins):
                count[0] += 1
                ins.then_inc(chain, 1)
                eng.wait_ge(chain, count[0])
            return link

        a_loads = [
            (w_in[:, 0, :], t["w_in"][0:128, :]), (w_in[0:64, 1, :], t["w_in"][128:192, :]),
            (w_conv[:, :], t["w_conv"]), (b_conv[:, :], t["b_conv"]),
            (w_x[:, :, :], t["w_x"]), (w_dt[:, :, :], t["w_dt"]), (b_dt[:, :], t["b_dt"]),
            (a_log[:, :], t["a_log"]), (ds_in[:, :], t["ds"]),
            (on_g[:, :], t["on_g"].partition_broadcast(128)),
            (on_b[:, :], t["on_b"].partition_broadcast(128)),
            (w_out[:, :], t["w_out"]),
        ]
        b_loads = []
        for l in range(2):
            w, b = t[f"w_qkv{l}"], t[f"b_qkv{l}"]
            for c, (c0, cn) in enumerate(CH):
                b_loads.append((w_qkv[l][0:cn, c, :], w[c0:c0 + cn, :]))
            w_heads = t[f"w_o{l}"].rearrange("(t j i) n -> j i t n", j=QUAD, i=HEAD)
            for j in range(QUAD):
                b_loads.append((w_o[l][32 * j:32 * j + HEAD, :, :], w_heads[j]))
            b_loads.append((b_qk[l][:, :, :], b[0:2 * WIDTH].rearrange("(p c r) -> r p c", p=2, r=CGROUP)))
            b_loads.append((b_v[l][:, :], b[2 * WIDTH:3 * WIDTH].partition_broadcast(128)))
            b_loads.append((b_o[l][:, :], t[f"b_o{l}"].partition_broadcast(128)))
            b_loads.append((ln_g[l][:, :], t[f"ln_g{l}"].partition_broadcast(128)))
            b_loads.append((ln_b[l][:, :], t[f"ln_b{l}"].partition_broadcast(128)))
        for c, (c0, cn) in enumerate(CH):
            b_loads.append((w_up[0:cn, 0, c, :], t["mlp_w1"][c0:c0 + cn, :]))
            b_loads.append((w_gate[0:cn, c, :], t["w_gate"][c0:c0 + cn, :]))
            b_loads.append((w_up[0:cn, 1:1 + EXPERTS, c, :],
                            t["exp_w1"][:, c0:c0 + cn, :].rearrange("e k n -> k e n")))
        b_loads.append((w_dn[:, 0, :, :], t["mlp_w2"].rearrange("(m p) n -> p m n", p=128)))
        b_loads.append((w_dn[:, 1:1 + EXPERTS, :, :].rearrange("p e m n -> p (e m) n"),
                        t["exp_w2"].rearrange("e (m p) n -> p (e m) n", p=128)))
        b_loads += [
            (b_up[:, :, :], t["b_up"]), (b_dn[:, :], t["mlp_b2"].partition_broadcast(128)),
            (b_ex[:, :], t["exp_b2"]), (b_gate[:, :], t["b_gate"].partition_broadcast(128)),
        ]

        with nc.Block() as block:
            @block.sync
            def _(sp):
                with nc.allow_non_contiguous_dma(reason="short rows of heads and biases, once"):
                    for dst, src in a_loads:
                        sp.dma_start(dst, src).then_inc(w_a, 16)
    
            @block.gpsimd
            def _(pool):
                link = chained(pool, pool_set)
                for tile, value in ((ident, 0.0), (gsum, 1.0 / GN_GROUP), (sel, 1.0), (ddiag, 0.0),
                                    (half, -0.5)):
                    ins = nc.gpsimd.memset(tile[:], value)
                link(ins)
                link(nc.gpsimd.affine_select(out=ident[:, :], in_=ident[:, :], compare_op=ALU.not_equal,
                                             fill=1.0, base=0, pattern=[[-1, 128]], channel_multiplier=1))
                for c, (c0, cn) in enumerate(CH):
                    for base, sign in ((c0, 1), (GN_GROUP - 1 - c0, -1)):
                        link(nc.gpsimd.affine_select(
                            out=gsum[:, c, :], in_=gsum[:, c, :], compare_op=ALU.is_ge, fill=0.0, base=base,
                            pattern=[[-GN_GROUP * sign, WIDTH // GN_GROUP], [0, GN_GROUP]],
                            channel_multiplier=sign))
                shift = STATE * PACK * (GROUPS - 1)
                for base, sign in ((shift, 1), (STATE - 1 - shift, -1)):
                    ins = nc.gpsimd.affine_select(out=sel[:, :], in_=sel[:, :], compare_op=ALU.is_ge, fill=0.0,
                                                  base=base, pattern=[[-STATE * sign, (2 * GROUPS - 1) * PACK]],
                                                  channel_multiplier=sign)
                    if sign == 1:
                        link(ins)
                ins.then_inc(consts, 1)

            @block.vector
            def _(dve):
                for l in range(2):
                    nc.vector.memset(w_o[l][:], 0.0)
                nc.vector.memset(v_aug[:], 0.0).then_inc(cleared, 1)
                dve.wait_ge(cleared, 1)
                for buf in (pad, gn_raw, gn_mv, gn_m, decay[0], decay[1]):
                    nc.vector.memset(buf[:], 0.0)
                nc.vector.tensor_copy(top[:, :, :, :].rearrange("p a b m -> p (a b m)"),
                                      v_aug[:, :, :, :].rearrange("p t h m -> p (t h m)")
                                      [:, 0:4 * 128]).then_inc(cleared, 1)
                dve.wait_ge(cleared, 2)
                nc.vector.memset(v_aug[:, :, :, HEAD:HEAD + 1], 1.0).then_inc(zeroed, 1)
                dve.wait_ge(w_a, 16 * len(a_loads))
                dve.wait_ge(consts, 1)
                nc.vector.tensor_reduce(dsum[:, :], ds_in[:, :], AX.X, ALU.add)
                nc.vector.tensor_scalar(a_log[:, :], a_log[:, :], A_LOG_MAX, None,
                                        ALU.min).then_inc(zeroed, 1)
                dve.wait_ge(zeroed, 2)
                nc.vector.tensor_scalar(ddiag[:, :], ident[0:INNER, 0:INNER], dsum[:, 0:1], None,
                                        ALU.mult).then_inc(zeroed, 1)
                dve.wait_ge(ready_a, 1)
                nc.vector.tensor_scalar(a_neg[:, :], a_neg[:, :], -1.0, None, ALU.mult).then_inc(zeroed, 1)

            @block.scalar
            def _(sc):
                sc.wait_ge(zeroed, 2)
                nc.scalar.activation(a_neg[:, :], a_log[:, :], ACT.Exp).then_inc(ready_a, 1)

        def attention_constants(pool):
            link = chained(pool, pool_late)
            for tile, value in ((maskq, 0.0), (maskk, 0.0), (den_sel, 0.0), (lower, 1.0), (top_one, 0.0),
                                (act[0], 0.0)):
                ins = nc.gpsimd.memset(tile[:], value)
            link(ins)
            link(nc.gpsimd.affine_select(out=maskq[:, :], in_=maskq[:, :], compare_op=ALU.is_ge,
                                         fill=MASKED, base=0, pattern=[[-1, 128]], channel_multiplier=1))
            link(nc.gpsimd.affine_select(out=maskk[:, :], in_=maskk[:, :], compare_op=ALU.is_ge,
                                         fill=MASKED, base=0, pattern=[[1, 128]], channel_multiplier=-1))
            link(nc.gpsimd.affine_select(out=lower[:, :, :], in_=lower[:, :, :], compare_op=ALU.is_gt,
                                         fill=0.0, base=0, pattern=[[1, EXPERTS], [-1, EXPERTS]],
                                         channel_multiplier=0))
            link(nc.gpsimd.affine_select(out=den_sel[:, :, :], in_=den_sel[:, :, :],
                                         compare_op=ALU.not_equal, fill=1.0, base=-HEAD,
                                         pattern=[[-32, QUAD], [0, 32]], channel_multiplier=1))
            for j in range(2):
                link(nc.gpsimd.affine_select(
                    out=top_one[:, :], in_=top_one[:, :], compare_op=ALU.not_equal, fill=1.0,
                    base=-(64 * j + TOP_ROW), pattern=[[0, 1]], channel_multiplier=1))
            spread_of = act[0][:, 0:2, :].rearrange("p a (x j r i) -> p a x j r i", x=2, j=2, r=4)
            for part in range(2):
                for level, parts in ((0, HIGH_PARTS[part]), (1, LOW_PARTS[part])):
                    into = spread_of[:, part, level, :, parts, :]
                    for row in range(0, CGROUP, 32):
                        link(nc.gpsimd.affine_select(
                            out=into, in_=into, compare_op=ALU.not_equal, fill=1.0, base=-row,
                            pattern=[[-HEAD, 2], [0, into.shape[2]], [-1, HEAD]], channel_multiplier=1))
            link(nc.gpsimd.tensor_copy(to_stack[:, :, :, :].rearrange("p a b m -> p a (b m)"),
                                       act[0][:, 0:2, :]))
            link(nc.gpsimd.tensor_copy(identb[:, :], ident[:, :]))

        def turn(first, second, src):
            for tl in range(TILES):
                for c, (c0, cn) in enumerate(CH):
                    mm = nc.tensor.transpose((first, second)[c][0:cn, tl * 128:(tl + 1) * 128],
                                             src[:, tl, c0:c0 + cn], ident[:, :])
            return mm

        def chunks(out, lhs, rhs, start=True):
            for c, (_, cn) in enumerate(CH):
                mm = nc.tensor.matmul(out, lhs(c, cn), rhs(c, cn), start=(c == 0), stop=(c == 1))
            return mm

        def flat(buf):
            return buf[:, :, :].rearrange("p k l -> p (k l)")

        def two_tiles(bank):
            return bank[:, 0:TILES * WIDTH].rearrange("p (t c) -> p t c", t=TILES)

        def rows(gain):
            return gain[:, :].unsqueeze(1).to_broadcast([128, TILES, gain.shape[1]])

        def block_of(ssm_at, att_at, ffn_at, late_setup=False):
            run_s, run_a, run_f = ssm_at is not None, att_at is not None, ffn_at is not None

            up_banks = 1 if run_a else 4

            def up_bank(n):
                return pu if run_a else ps[:, n % up_banks, :]

            def steps(table, slot):
                return table.get(slot, [])

            with nc.Block() as block:
                @block.sync
                def _(sp):
                    if run_s:
                        sp.dma_start(x_tok[:, :, :],
                                     t["x"][bass.ds(ssm_at, 1)].rearrange("o (t p) c -> p (o t) c", p=128)
                                     ).then_inc(x_in, 16)
                    if late_setup:
                        with nc.allow_non_contiguous_dma(reason="short rows of heads and biases, once"):
                            for dst, src in b_loads:
                                sp.dma_start(dst, src).then_inc(w_b, 16)
                    if run_s:
                        sp.wait_ge(xd_copied, 2)
                        for dst, first in ((B_rows, RANK), (C_rows, RANK + STATE)):
                            for c in range(PACK):
                                sp.dma_start(dst[STATE * c:STATE * (c + 1), :], xdbl[first:first + STATE, :, :]
                                             .rearrange("n k l -> n (k l)")).then_inc(bc_in, 16)
                        for g in range(GROUPS):
                            channels = slice(PACK * g, PACK * (g + 1))
                            if g == 0:
                                sp.wait_ge(d_done, 1)
                            if g >= 2:
                                sp.wait_ge(decay_done, g - 1)
                            sp.dma_start(d_rows[g % 2][:, :, :],
                                         delta[channels, :, :].rearrange("c k l -> c (k l)")
                                         .unsqueeze(1).to_broadcast([PACK, STATE, PATHS * TOKENS])
                                         ).then_inc(d_in[g % 2], 16)
                            if g == 0:
                                sp.wait_ge(dx_done, 1)
                            if g >= 2:
                                sp.wait_ge(scan_done, g - 1)
                            sp.dma_start(dx_rows[g % 2][:, :],
                                         delta_x[channels, :, :].rearrange("c k l -> c (k l)")
                                         .unsqueeze(1).to_broadcast([PACK, STATE, PATHS * TOKENS])
                                         ).then_inc(dx_in[g % 2], 16)
                    if run_f:
                        sp.wait_ge(out_done, TILES)
                        sp.dma_start(t["out"][bass.ds(ffn_at, 1)].rearrange("o (t p) c -> p (o t) c", p=128),
                                     out_tok[:, :, :]).then_inc(stored, 16)
                        sp.wait_ge(stored, 16)

                @block.tensor
                def _(pe):
                    def x_turn():
                        pe.wait_ge(x_in, 16)
                        turn(py[:, 0:TOKENS], py[:, TOKENS:2 * TOKENS], x_tok).then_inc(x_turned, 1)

                    def group_sums():
                        pe.wait_ge(gn_stats, 1)
                        for m, (m0, mn) in enumerate(CH):
                            mm = chunks(py[0:mn, 2 * m:2 * m + 2],
                                        lambda c, cn: gsum[0:cn, c, m0:m0 + mn],
                                        lambda c, cn: gn_mv[0:cn, c, :])
                        mm.then_inc(gn_sums, 1)

                    def in_proj():
                        pe.wait_ge(xg_done, 2)
                        chunks(py[0:INNER, 0:TOKENS], lambda c, cn: w_in[0:cn, c, 0:INNER],
                               lambda c, cn: xgT[0:cn, c, :])
                        for tl in range(TILES):
                            at = TOKENS + INNER * tl
                            mm = chunks(py[:, at:at + INNER],
                                        lambda c, cn: xgT[0:cn, c, 128 * tl:128 * (tl + 1)],
                                        lambda c, cn: w_in[0:cn, c, INNER:2 * INNER])
                        mm.then_inc(xh_done, 1)

                    def x_dbl(half_paths):
                        if half_paths == 0:
                            pe.wait_ge(xs_done, 1)
                        else:
                            pe.wait_ge(xd_copied, 1)
                        for o in range(2):
                            mm = nc.tensor.matmul(py[0:RANK + 2 * STATE, TOKENS * o:TOKENS * (o + 1)],
                                                  w_x[:, 2 * half_paths + o, :], xs[:, o, :],
                                                  start=True, stop=True)
                        mm.then_inc(xd_done, 1)

                    def dt(half_paths):
                        if half_paths == 0:
                            pe.wait_ge(xd_copied, 2)
                        else:
                            pe.wait_ge(dt_sum, 1)
                        for o in range(2):
                            k = 2 * half_paths + o
                            mm = nc.tensor.matmul(py[0:INNER, TOKENS * o:TOKENS * (o + 1)],
                                                  w_dt[:, k, :], xdbl[0:RANK, k, :], start=True, stop=True)
                        mm.then_inc(dt_done, 1)

                    def y_sum(g):
                        if g == 0:
                            pe.wait_ge(dt_sum, 2)
                            nc.tensor.matmul(py[0:INNER, 0:TOKENS], ddiag[:, :], xs[:, 0, :],
                                             start=True, stop=False, skip_group_check=True)
                        pe.wait_ge(sc_done, g + 1)
                        first = PACK * (GROUPS - 1 - g)
                        for part in (state[g % 2][:, 0, :], state[g % 2][:, 2, :],
                                     by_row[g % 2][:, 0, :], by_row[g % 2][:, 1, :]):
                            mm = nc.tensor.matmul(py[0:INNER, 0:TOKENS], sel[:, first:first + INNER], part,
                                                  start=False, stop=(g == GROUPS - 1), skip_group_check=True)
                        mm.then_inc(y_part, 1)

                    def y_norm():
                        pe.wait_ge(yT_done, 1)
                        for tl in range(TILES):
                            mm = nc.tensor.transpose(py[:, INNER * tl:INNER * (tl + 1)],
                                                     yT[:, 128 * tl:128 * (tl + 1)], ident[0:INNER, 0:INNER])
                        mm.then_inc(y_back, 1)

                    def y_turn():
                        pe.wait_ge(yg_done, 1)
                        for tl in range(TILES):
                            mm = nc.tensor.transpose(py[0:INNER, 128 * tl:128 * (tl + 1)],
                                                     y_g[:, tl, :], ident[:, :])
                        mm.then_inc(y_turned, 1)

                    def y_out():
                        pe.wait_ge(yT_done, 2)
                        for tl in range(TILES):
                            mm = nc.tensor.matmul(py[:, WIDTH * tl:WIDTH * (tl + 1)],
                                                  yT[:, 128 * tl:128 * (tl + 1)], w_out[:, :],
                                                  start=True, stop=True)
                        mm.then_inc(o_done, 1)

                    ssm = {"x_turn": x_turn, "group_sums": group_sums, "in_proj": in_proj, "x_dbl": x_dbl,
                           "dt": dt, "y_norm": y_norm, "y_turn": y_turn, "y_out": y_out}

                    def ffn_turn(i):
                        if i == 1:
                            pe.wait_ge(xm_done, 1)
                        turn(pu, pu[:, TOKENS:2 * TOKENS], (v2, f_tok)[i]).then_inc(m_turned, 1)

                    def up(e, i):
                        n = e * HCH // 2 + i
                        if i == 0 and e < 2:
                            pe.wait_ge(mT_done, e + 1)
                        if n >= up_banks:
                            pe.wait_ge(gelu_done, n + 1 - up_banks)
                        bank = up_bank(n)
                        for m in range(2):
                            first = 128 * (2 * i + m)
                            mm = chunks(bank[:, TOKENS * m:TOKENS * (m + 1)],
                                        lambda c, cn: w_up[0:cn, e, c, first:first + 128],
                                        lambda c, cn: fT[0:cn, c, :])
                        mm.then_inc(up_done, 1)

                    def down(e, tl):
                        if tl == 0:
                            pe.wait_ge(gelu_done, HCH // 2 * (e + 1))
                            if e == 1:
                                pe.wait_ge(acc_done, 1)
                            if e >= 2:
                                pe.wait_ge(dn_used, e - 1)
                        for m in range(HCH):
                            mm = nc.tensor.matmul(pd[:, WIDTH * tl:WIDTH * (tl + 1)],
                                                  act[e % 2][:, m, 128 * tl:128 * (tl + 1)],
                                                  w_dn[:, e, m, :], start=(m == 0), stop=(m == HCH - 1))
                        mm.then_inc(dn_done, 1)

                    def logits():
                        pe.wait_ge(mT_done, 2)
                        for tl in range(TILES):
                            mm = chunks(pd[:, EXPERTS * tl:EXPERTS * (tl + 1)],
                                        lambda c, cn: fT[0:cn, c, 128 * tl:128 * (tl + 1)],
                                        lambda c, cn: w_gate[0:cn, c, :])
                        mm.then_inc(lg_done, 1)

                    def turn_gates():
                        pe.wait_ge(gate_done, 1)
                        for tl in range(TILES):
                            mm = nc.tensor.transpose(pd[0:EXPERTS, 128 * tl:128 * (tl + 1)],
                                                     gate[:, tl, :], ident[:, :])
                        mm.then_inc(gate_turned, 1)

                    def bias():
                        pe.wait_ge(gateT_done, 1)
                        for tl in range(TILES):
                            mm = nc.tensor.matmul(pd[:, WIDTH * tl:WIDTH * (tl + 1)],
                                                  gateT[:, 128 * tl:128 * (tl + 1)], b_ex[:, :],
                                                  start=True, stop=True)
                        mm.then_inc(gb_done, 1)

                    ffn = {"turn": ffn_turn, "up": up, "down": down, "logits": logits,
                           "turn_gates": turn_gates, "bias": bias}

                    def sums(slot):
                        if run_s:
                            for g in steps(Y_SUMS, slot):
                                y_sum(g)

                    def others(slot):
                        if run_s:
                            for name, *at in steps(SSM_STEPS, slot):
                                if name in ssm:
                                    ssm[name](*at)
                        if run_f:
                            for name, *at in steps(FFN_STEPS, slot):
                                if name in ffn:
                                    ffn[name](*at)

                    def attention(l):
                        causal = l == 0
                        if l == 1:
                            pe.wait_ge(h_done, 1)
                        turn(pm, ps[:, 3, :], h_tok).then_inc(h_turned[l], 1)
                        others((l, "turned"))
                        pe.wait_ge(hT_done[l], 2)
                        for c in range(2):
                            for part in range(2):
                                first = WIDTH * part + CGROUP * c
                                chunks(ps[0:CGROUP, 2 * c + part, 0:TOKENS],
                                       lambda ch, cn: w_qkv[l][0:cn, ch, first:first + CGROUP],
                                       lambda ch, cn: hT[0:cn, ch, :]).then_inc(qk_done[l], 1)
                        for tl in range(TILES):
                            mm = chunks(pm[:, WIDTH * tl:WIDTH * (tl + 1)],
                                        lambda c, cn: hT[0:cn, c, 128 * tl:128 * (tl + 1)],
                                        lambda c, cn: w_qkv[l][0:cn, c, 2 * WIDTH:3 * WIDTH])
                        mm.then_inc(v_done[l], 1)

                        def stack(u):
                            pe.wait_ge(low_done[l], 4 if u >= 2 else 2)
                            if u >= 4:
                                pe.wait_ge((stack_even, stack_odd)[u % 2][l], 1)
                            channels = slice(32 * (u % 3), 32 * (u % 3) + 32)
                            for part in range(2):
                                for level, source in ((0, high[part]), (1, low[part])):
                                    mm = nc.tensor.matmul(ps[:, u % 4, TOKENS * part:TOKENS * (part + 1)],
                                                          to_stack[channels, part, level, :],
                                                          source[u // 3][channels, :],
                                                          start=(level == 0), stop=(level == 1))
                            mm.then_inc(stack_psum[l], 1)

                        for u in range(4):
                            stack(u)
                        sums((l, "projected"))
                        others((l, "projected"))
                        for u in (4, 5):
                            stack(u)

                        def scores(u):
                            if u == 0:
                                pe.wait_ge(stack_even[l], 3)
                                pe.wait_ge(stack_odd[l], 3)
                                pe.wait_ge(v_copied[l], 1)
                            if u >= 2:
                                pe.wait_ge(p_done[l], u - 1)
                            for j in range(2):
                                rows = slice(64 * j, 64 * j + TOP_ROW)
                                b = ps[:, 2 * (u % 2) + j, :]
                                for i in range(TILES):
                                    keys = 128 * (i + 1) if causal else TOKENS
                                    mm = nc.tensor.matmul(b[:, TOKENS * i:TOKENS * i + keys],
                                                          q_stack[rows, u, 128 * i:128 * (i + 1)],
                                                          k_stack[rows, u, 0:keys],
                                                          start=(i == 0), stop=not causal,
                                                          skip_group_check=True)
                            if causal:
                                for j in range(2):
                                    for i in range(TILES):
                                        at = TOKENS * i + 128 * i
                                        mm = nc.tensor.matmul(ps[:, 2 * (u % 2) + j, at:at + 128],
                                                              identb[:, :], maskq[:, :], start=False,
                                                              stop=True, skip_group_check=True)
                            mm.then_inc(s_done[l], 1)

                        def row_max(u):
                            pe.wait_ge(top_done[l], u + 1)
                            for i in range(TILES):
                                mm = nc.tensor.transpose(ps[:, 2 * (u % 2), 128 * i:128 * (i + 1)],
                                                         top[:, u % 2, i, :].bitcast(F32), ident[:, :])
                            mm.then_inc(top_turned[l], 1)

                        def shifted(u):
                            pe.wait_ge(q_shifted[l], u + 1)
                            for j in range(2):
                                rows = slice(64 * j, 64 * j + TOP_ROW + 1)
                                b = ps[:, 2 * (u % 2) + j, :]
                                for i in range(TILES):
                                    q0 = 128 * i if causal else 0
                                    mm = nc.tensor.matmul(b[:, TOKENS * i + q0:TOKENS * (i + 1)],
                                                          k_stack[rows, u, 128 * i:128 * (i + 1)],
                                                          q_stack[rows, u, q0:TOKENS],
                                                          start=(i == 0), stop=not causal,
                                                          skip_group_check=True)
                            if causal:
                                for j in range(2):
                                    for i in range(TILES):
                                        at = TOKENS * i + 128 * i
                                        mm = nc.tensor.matmul(ps[:, 2 * (u % 2) + j, at:at + 128],
                                                              identb[:, :], maskk[:, :], start=False,
                                                              stop=True, skip_group_check=True)
                            mm.then_inc(st_done[l], 1)

                        def context(u):
                            pe.wait_ge(p_done[l], u + 1)
                            if u in (2, 4):
                                pe.wait_ge(den_inv[l], u // 2)
                            for j in range(2):
                                head = 2 * u + j
                                row = 32 * (head % QUAD)
                                for kt in range(TILES):
                                    q0 = 128 * kt if causal else 0
                                    mm = nc.tensor.matmul(pm[row:row + 32, q0:TOKENS], v_aug[:, kt, head, :],
                                                          probs[u % 2][:, j, kt, q0:TOKENS],
                                                          start=(kt == 0), stop=(kt == TILES - 1),
                                                          tile_position=(0, row), skip_group_check=True)
                            mm.then_inc(av_done[l], 1)

                        def spread(ht):
                            pe.wait_ge(ctx_copied[l], ht + 1)
                            nc.tensor.matmul(pm[:, TOKENS:2 * TOKENS],
                                             den_sel[:, :, :].rearrange("p j i -> p (j i)"), cT[:, ht, :],
                                             start=True, stop=True).then_inc(den_done[l], 1)

                        scores(0)
                        for u in range(UNITS):
                            if u + 1 < UNITS:
                                scores(u + 1)
                            row_max(u)
                            if u >= 1:
                                context(u - 1)
                            others((l, 2 * u))
                            sums((l, 2 * u))
                            shifted(u)
                            if u in (2, 4):
                                spread(u // 2 - 1)
                            others((l, 2 * u + 1))
                            sums((l, 2 * u + 1))
                        context(UNITS - 1)
                        others((l, "context"))
                        spread(HTILES - 1)
                        others((l, "spread"))
                        pe.wait_ge(ctx_done[l], HTILES)
                        for tl in range(TILES):
                            for ht in range(HTILES):
                                mm = nc.tensor.matmul(ps[:, 2, WIDTH * tl:WIDTH * (tl + 1)],
                                                      cT[:, ht, 128 * tl:128 * (tl + 1)], w_o[l][:, ht, :],
                                                      start=(ht == 0), stop=(ht == HTILES - 1))
                        mm.then_inc(proj_done[l], 1)
                        others((l, "output"))

                    if run_a or run_f:
                        pe.wait_ge(w_b, 16 * len(b_loads))
                    if run_a:
                        attention(0)
                        attention(1)
                    else:
                        for slot in SLOTS:
                            sums(slot)
                            others(slot)

                @block.vector
                def _(dve):
                    link = chained(dve, dve_chain)

                    def norm_stats(i, src):
                        for tl in range(TILES):
                            ins = nc.vector.bn_stats(norm_raw[:, i, tl, :], src(tl))
                        link(ins)
                        for tl in range(TILES):
                            ins = nc.vector.bn_aggr(norm_mv[:, i, tl, :], norm_raw[:, i, tl, :])
                        link(ins)
                        nc.vector.tensor_scalar(norm_var[:, i, :], norm_mv[:, i, :, 1], EPS, None,
                                                ALU.add).then_inc(var_done[i], 1)

                    def norm_apply(i, src, dst):
                        dve.wait_ge(rstd_done[i], 1)
                        link(nc.vector.scalar_tensor_tensor(
                            out=norm_shift[:, i, :], in0=norm_mv[:, i, :, 0], scalar=-1.0,
                            in1=norm_rstd[:, i, :], op0=ALU.mult, op1=ALU.mult))
                        for tl in range(TILES):
                            ins = nc.vector.tensor_scalar(dst(tl), src(tl), norm_rstd[:, i, tl:tl + 1],
                                                          norm_shift[:, i, tl:tl + 1], ALU.mult, ALU.add)
                        return ins

                    def norm(i, src, dst):
                        norm_stats(i, src)
                        return norm_apply(i, src, dst)

                    def x_turn():
                        dve.wait_ge(x_turned, 1)
                        for c, (_, cn) in enumerate(CH):
                            ins = nc.vector.tensor_copy(xgT[0:cn, c, :], py[0:cn, TOKENS * c:TOKENS * (c + 1)])
                        link(ins)
                        for c, (_, cn) in enumerate(CH):
                            ins = nc.vector.bn_stats(gn_raw[0:cn, c, :], xgT[0:cn, c, :])
                        link(ins)
                        for c, (_, cn) in enumerate(CH):
                            ins = nc.vector.bn_aggr(gn_mv[0:cn, c, :], gn_raw[0:cn, c, :])
                        link(ins)
                        link(nc.vector.tensor_tensor(gn_sq[:, :], gn_mv[:, :, 0], gn_mv[:, :, 0], ALU.mult))
                        nc.vector.tensor_tensor(gn_mv[:, :, 1], gn_mv[:, :, 1], gn_sq[:, :],
                                                ALU.add).then_inc(gn_stats, 1)

                    def group_sums():
                        dve.wait_ge(gn_sums, 1)
                        for c, (_, cn) in enumerate(CH):
                            ins = nc.vector.tensor_copy(gn_m[0:cn, c, :], py[0:cn, 2 * c:2 * c + 2])
                        link(ins)
                        link(nc.vector.tensor_tensor(gn_sq[:, :], gn_m[:, :, 0], gn_m[:, :, 0], ALU.mult))
                        link(nc.vector.tensor_tensor(gn_var[:, :], gn_m[:, :, 1], gn_sq[:, :], ALU.subtract))
                        nc.vector.tensor_scalar(gn_var[:, :], gn_var[:, :], 0.0, EPS,
                                                ALU.max, ALU.add).then_inc(gn_v, 1)
                        dve.wait_ge(gn_r, 1)
                        link(nc.vector.scalar_tensor_tensor(
                            out=gn_shift[:, :], in0=gn_m[:, :, 0], scalar=-1.0, in1=gn_rstd[:, :],
                            op0=ALU.mult, op1=ALU.mult))
                        for c, (_, cn) in enumerate(CH):
                            nc.vector.tensor_scalar(xgT[0:cn, c, :], xgT[0:cn, c, :], gn_rstd[0:cn, c:c + 1],
                                                    gn_shift[0:cn, c:c + 1], ALU.mult,
                                                    ALU.add).then_inc(xg_done, 1)

                    def in_proj():
                        dve.wait_ge(xh_done, 1)
                        nc.vector.tensor_copy(z_gate[:, :, :], py[:, TOKENS:TOKENS + TILES * INNER]
                                              .rearrange("p (t c) -> p t c", t=TILES)).then_inc(z_copied, 1)
                        link(nc.vector.tensor_copy(pad[:, 1:SIDE + 1, 1:SIDE + 1],
                                                   py[0:INNER, 0:TOKENS].rearrange("p (h w) -> p h w",
                                                                                   w=SIDE)))
                        conv2 = conv.rearrange("p (h w) -> p h w", w=SIDE)
                        for tap in range(9):
                            window = pad[:, tap // 3:tap // 3 + SIDE, tap % 3:tap % 3 + SIDE]
                            if tap == 0:
                                ins = nc.vector.tensor_scalar(conv2, window, w_conv[:, 0:1], b_conv[:, 0:1],
                                                              ALU.mult, ALU.add)
                            else:
                                ins = nc.vector.scalar_tensor_tensor(
                                    out=conv2, in0=window, scalar=w_conv[:, tap:tap + 1], in1=conv2,
                                    op0=ALU.mult, op1=ALU.add)
                            if tap < 8:
                                link(ins)
                        ins.then_inc(conv_done, 1)

                    def silu():
                        dve.wait_ge(silu_e, 2)
                        link(nc.vector.tensor_scalar(conv_e, conv_e, 1.0, None, ALU.add))
                        link(nc.vector.reciprocal(conv_e, conv_e))
                        nc.vector.tensor_tensor(xs[:, 0, :], conv, conv_e, ALU.mult).then_inc(u_done, 1)
                        link(nc.vector.tensor_scalar(z_e, z_e, 1.0, None, ALU.add))
                        link(nc.vector.reciprocal(z_e, z_e))
                        link(nc.vector.tensor_tensor(z_gate[:, :, :], z_gate[:, :, :], z_e, ALU.mult))

                    def x_dbl(half_paths):
                        if half_paths == 0:
                            dve.wait_ge(xd_done, 1)
                            nc.vector.tensor_copy(xdbl[:, 0:2, :], py[0:RANK + 2 * STATE, :]
                                                  .rearrange("p (k l) -> p k l", k=2)).then_inc(xd_copied, 1)

                    def dt(half_paths):
                        dve.wait_ge(dt_done, half_paths + 1)
                        for o in range(2):
                            k = 2 * half_paths + o
                            ins = nc.vector.tensor_scalar(delta[:, k, :],
                                                          py[0:INNER, TOKENS * o:TOKENS * (o + 1)],
                                                          b_dt[:, k:k + 1], None, ALU.add)
                        ins.then_inc(dt_sum, 1)

                    def softplus(half_paths):
                        dve.wait_ge(sp_a, half_paths + 1)
                        ks = slice(2 * half_paths, 2 * half_paths + 2)
                        one_e, e, d = d_rows[0][0:INNER, ks, :], delta_x[:, ks, :], delta[:, ks, :]
                        nc.vector.tensor_scalar(one_e, e, 1.0, None, ALU.add).then_inc(sp_u, 1)
                        dve.wait_ge(sp_u, half_paths + 1)
                        link(nc.vector.scalar_tensor_tensor(out=e, in0=one_e, scalar=1.0, in1=e,
                                                            op0=ALU.subtract, op1=ALU.subtract))
                        link(nc.vector.scalar_tensor_tensor(out=d, in0=d, scalar=0.0, in1=e,
                                                            op0=ALU.max, op1=ALU.subtract))

                    def softplus_log():
                        dve.wait_ge(sp_l, 1)
                        nc.vector.tensor_tensor(flat(delta), flat(delta),
                                                d_rows[1][0:INNER, :, :].rearrange("p k l -> p (k l)"),
                                                ALU.add).then_inc(d_done, 1)
                        dve.wait_ge(d_done, 1)
                        dve.wait_ge(xs_done, 1)
                        nc.vector.tensor_tensor(
                            delta_x[:, :, :].rearrange("p (d o) l -> p d (o l)", d=2),
                            delta[:, :, :].rearrange("p (d o) l -> p d (o l)", d=2),
                            xs[:, :, :].rearrange("p o l -> p (o l)").unsqueeze(1)
                            .to_broadcast([INNER, 2, 2 * TOKENS]), ALU.mult).then_inc(dx_done, 1)

                    def scan(g):
                        dve.wait_ge(dx_in[g % 2], 16 * (g // 2 + 1))
                        if g == 0:
                            dve.wait_ge(bc_in, 16 * 2 * PACK)
                        link(nc.vector.tensor_tensor(dx_rows[g % 2][:, :], dx_rows[g % 2][:, :],
                                                     B_rows[:, :], ALU.mult))
                        dve.wait_ge(decay_done, g + 1)
                        if g >= 2:
                            dve.wait_ge(y_part, g - 1)
                        for both in (slice(0, 2 * TOKENS), slice(4 * TOKENS - 1, 2 * TOKENS - 1, -1)):
                            ins = nc.vector.tensor_tensor_scan(
                                flat(state[g % 2])[:, both], flat(decay[g % 2])[:, both],
                                dx_rows[g % 2][:, both], 0.0, ALU.mult, ALU.add)
                        ins.then_inc(scan_done, 1)

                    def y_copy():
                        dve.wait_ge(y_part, GROUPS)
                        nc.vector.tensor_copy(yT, py[0:INNER, 0:TOKENS]).then_inc(yT_done, 1)

                    def y_norm():
                        dve.wait_ge(y_back, 1)
                        link(norm(0, lambda tl: py[:, INNER * tl:INNER * (tl + 1)],
                                  lambda tl: y_g[:, tl, :]))
                        link(nc.vector.tensor_tensor(y_g, y_g, rows(on_g), ALU.mult))
                        link(nc.vector.tensor_tensor(y_g, y_g, rows(on_b), ALU.add))
                        nc.vector.tensor_tensor(y_g, y_g, z_gate[:, :, :],
                                                ALU.mult).then_inc(yg_done, 1)

                    def y_turn():
                        dve.wait_ge(y_turned, 1)
                        nc.vector.tensor_copy(yT, py[0:INNER, 0:TOKENS]).then_inc(yT_done, 1)

                    def y_out():
                        dve.wait_ge(o_done, 1)
                        link(nc.vector.tensor_tensor(x1[:, :, :], two_tiles(py), x_tok[:, :, :], ALU.add))
                        norm(1, lambda tl: x1[:, tl, :], lambda tl: h_tok[:, tl, :])

                    ssm = {"x_turn": x_turn, "group_sums": group_sums, "in_proj": in_proj, "silu": silu,
                           "x_dbl": x_dbl, "dt": dt, "softplus": softplus,
                           "softplus_log": softplus_log, "y_copy": y_copy, "y_norm": y_norm,
                           "y_turn": y_turn, "y_out": y_out}

                    def affine(i, src, dst, done):
                        link(norm_apply(3 + i, src, lambda tl: dst[:, tl, :]))
                        link(nc.vector.tensor_tensor(dst[:, :, :], dst[:, :, :], rows(ln_g[i]), ALU.mult))
                        nc.vector.tensor_tensor(dst[:, :, :], dst[:, :, :], rows(ln_b[i]),
                                                ALU.add).then_inc(done, 1)

                    def ffn_turn(i):
                        dve.wait_ge(m_turned, i + 1)
                        for c, (_, cn) in enumerate(CH):
                            ins = nc.vector.tensor_copy(fT[0:cn, c, :], pu[0:cn, TOKENS * c:TOKENS * (c + 1)])
                        ins.then_inc(mT_done, 1)

                    def ffn_norm(part):
                        if part == 1:
                            affine(1, lambda tl: v3[:, tl, :], f_tok, xm_done)
                            return
                        dve.wait_ge(dn_done, TILES)
                        dve.wait_ge(mres_done, 1)
                        nc.vector.tensor_tensor(v3[:, :, :], two_tiles(pd), v2[:, :, :],
                                                ALU.add).then_inc(v3_done, 1)
                        dve.wait_ge(v3_done, 1)
                        norm_stats(4, lambda tl: v3[:, tl, :])

                    def logits():
                        dve.wait_ge(lg_done, 1)
                        link(nc.vector.tensor_tensor(
                            logit[:, :, :], pd[:, 0:TILES * EXPERTS].rearrange("p (t e) -> p t e", t=TILES),
                            rows(b_gate), ALU.add))
                        for tl in range(TILES):
                            other = logit[:, tl, :].unsqueeze(1).to_broadcast([128, EXPERTS, EXPERTS])
                            own = logit[:, tl, :].unsqueeze(2).to_broadcast([128, EXPERTS, EXPERTS])
                            nc.vector.tensor_tensor(beats[:, tl, :, :], other, own, ALU.is_gt)
                            ins = nc.vector.tensor_tensor(ties[:, tl, :, :], other, own, ALU.is_equal)
                        nc.vector.tensor_reduce(best[:, :], logit[:, :, :], AX.X, ALU.max)
                        link(ins)
                        for tl in range(TILES):
                            ins = nc.vector.tensor_tensor(ties[:, tl, :, :], ties[:, tl, :, :],
                                                          lower[:, :, :], ALU.mult)
                        link(ins)
                        nc.vector.tensor_tensor(gate[:, :, :], logit[:, :, :],
                                                best[:, :].unsqueeze(2).to_broadcast([128, TILES, EXPERTS]),
                                                ALU.subtract).then_inc(lg_shift, 1)
                        link(nc.vector.tensor_tensor(beats[:, :, :, :], beats[:, :, :, :], ties[:, :, :, :],
                                                     ALU.add))
                        link(nc.vector.tensor_reduce(rank[:, :, :], beats[:, :, :, :], AX.X, ALU.add))
                        dve.wait_ge(gate_e, 1)
                        link(nc.vector.scalar_tensor_tensor(
                            out=gate[:, :, :], in0=rank[:, :, :], scalar=TOPK - 0.5, in1=gate[:, :, :],
                            op0=ALU.is_lt, op1=ALU.mult))
                        link(nc.vector.tensor_reduce(gsumr[:, :], gate[:, :, :], AX.X, ALU.add))
                        link(nc.vector.reciprocal(gsumr[:, :], gsumr[:, :]))
                        nc.vector.tensor_tensor(gate[:, :, :], gate[:, :, :],
                                                gsumr[:, :].unsqueeze(2).to_broadcast([128, TILES, EXPERTS]),
                                                ALU.mult).then_inc(gate_done, 1)

                    def turn_gates():
                        dve.wait_ge(gate_turned, 1)
                        nc.vector.tensor_copy(gateT[:, :], pd[0:EXPERTS, 0:TOKENS]).then_inc(gateT_done, 1)

                    def bias():
                        dve.wait_ge(gb_done, 1)
                        dve.wait_ge(base_done, 1)
                        nc.vector.tensor_tensor(out_tok[:, :, :], two_tiles(pd), out_tok[:, :, :],
                                                ALU.add).then_inc(acc_done, 1)

                    def add(e):
                        dve.wait_ge(dn_done, TILES * (e + 1))
                        if e == 1:
                            dve.wait_ge(acc_done, 1)
                            dve.wait_ge(gate_done, 1)
                        else:
                            dve.wait_ge(dn_used, e - 1)
                        for i in range(TILES):
                            ins = nc.vector.scalar_tensor_tensor(
                                out=out_tok[:, i, :], in0=pd[:, WIDTH * i:WIDTH * (i + 1)],
                                scalar=gate[:, i, e - 1:e], in1=out_tok[:, i, :],
                                op0=ALU.mult, op1=ALU.add)
                            if e == EXPERTS:
                                ins.then_inc(out_done, 1)
                        if e < EXPERTS:
                            ins.then_inc(dn_used, 1)

                    ffn = {"turn": ffn_turn, "norm": ffn_norm, "logits": logits, "turn_gates": turn_gates,
                           "bias": bias, "add": add}

                    def others(slot):
                        if run_s:
                            for name, *at in steps(SSM_STEPS, slot):
                                ssm[name](*at)
                            for g in steps(SCANS, slot):
                                scan(g)
                        if run_f:
                            for name, *at in steps(FFN_STEPS, slot):
                                if name in ffn:
                                    ffn[name](*at)

                    def attention(l):
                        causal = l == 0
                        dve.wait_ge(h_turned[l], 1)
                        nc.vector.tensor_copy(hT[:, 0, :], pm[:, 0:TOKENS]).then_inc(hT_done[l], 1)
                        others((l, "turned"))
                        for c in range(2):
                            for part in range(2):
                                n = 2 * c + part
                                dve.wait_ge(high_done[l], n + 1)
                                nc.vector.scalar_tensor_tensor(
                                    out=low[part][c], in0=ps[0:CGROUP, n, 0:TOKENS],
                                    scalar=b_qk[l][:, part, c:c + 1], in1=high[part][c].bitcast(F32),
                                    op0=ALU.add, op1=ALU.subtract).then_inc(low_done[l], 1)
                        dve.wait_ge(v_done[l], 1)
                        nc.vector.tensor_tensor(
                            v_aug[:, :, :, 0:HEAD],
                            pm[:, 0:TILES * WIDTH].rearrange("p (t h d) -> p t h d", t=TILES, d=HEAD),
                            b_v[l][:, :].rearrange("p (h d) -> p h d", d=HEAD).unsqueeze(1)
                            .to_broadcast([128, TILES, HEADS, HEAD]), ALU.add).then_inc(v_copied[l], 1)

                        def copy_stack(u):
                            dve.wait_ge(stack_psum[l], u + 1)
                            nc.vector.tensor_copy(q_stack[:, u, :], ps[:, u % 4, 0:TOKENS])
                            nc.vector.tensor_scalar(k_stack[:, u, :], ps[:, u % 4, TOKENS:2 * TOKENS],
                                                    top_one[:, :], None, ALU.add).then_inc(stack_odd[l], 1)

                        copy_stack(1)
                        copy_stack(3)

                        def row_max(u):
                            dve.wait_ge(s_done[l], u + 1)
                            par = u % 2
                            pair = ps[:, 2 * par:2 * par + 2, :]
                            if causal:
                                for i in range(TILES):
                                    ins = nc.vector.tensor_reduce(
                                        top[:, par, i, TOP_ROW::64],
                                        pair[:, :, TOKENS * i:TOKENS * i + 128 * (i + 1)],
                                        AX.X, ALU.max, negate=True)
                            else:
                                ins = nc.vector.tensor_reduce(
                                    top[:, par, :, TOP_ROW::64],
                                    pair.rearrange("p j (i k) -> p i j k", i=TILES),
                                    AX.X, ALU.max, negate=True)
                            ins.then_inc(top_done[l], 1)

                        def shift(u):
                            dve.wait_ge(top_turned[l], u + 1)
                            nc.vector.tensor_tensor(q_stack[:, u, :], q_stack[:, u, :].bitcast(F32),
                                                    ps[:, 2 * (u % 2), 0:TOKENS],
                                                    ALU.add).then_inc(q_shifted[l], 1)

                        def context_copy(ht):
                            dve.wait_ge(av_done[l], 2 * ht + 2)
                            nc.vector.tensor_copy(cT[:, ht, :], pm[:, 0:TOKENS]).then_inc(ctx_copied[l], 1)

                        def invert_sums(ht):
                            dve.wait_ge(den_done[l], ht + 1)
                            if ht:
                                dve.wait_ge(ctx_done[l], ht)
                            nc.vector.reciprocal(inv_den[:, :],
                                                 pm[:, TOKENS:2 * TOKENS]).then_inc(den_inv[l], 1)

                        others((l, "projected"))
                        copy_stack(5)
                        row_max(0)
                        for u in range(UNITS):
                            shift(u)
                            if u in (2, 4):
                                context_copy(u // 2 - 1)
                            others((l, 2 * u))
                            if u + 1 < UNITS:
                                row_max(u + 1)
                            if u in (2, 4):
                                invert_sums(u // 2 - 1)
                            others((l, 2 * u + 1))
                        context_copy(HTILES - 1)
                        others((l, "context"))
                        invert_sums(HTILES - 1)
                        others((l, "spread"))
                        dve.wait_ge(proj_done[l], 1)
                        dve.wait_ge(res_done[l], 1)
                        if l == 0:
                            if run_f:
                                dve.wait_ge(x2_kept, 1)
                            link(nc.vector.tensor_tensor(x2[:, :, :], two_tiles(ps[:, 2, :]), x1[:, :, :],
                                                         ALU.add))
                            link(norm(2, lambda tl: x2[:, tl, :], lambda tl: v_tok[:, tl, :]))
                            norm_stats(3, lambda tl: v_tok[:, tl, :])
                            affine(0, lambda tl: v_tok[:, tl, :], h_tok, h_done)
                        else:
                            nc.vector.tensor_tensor(v2[:, :, :], two_tiles(ps[:, 2, :]), v_tok[:, :, :],
                                                    ALU.add)
                        others((l, "output"))

                    if run_a or run_f:
                        dve.wait_ge(w_b, 16 * len(b_loads))
                    if run_a:
                        attention(0)
                        attention(1)
                    else:
                        for slot in SLOTS:
                            others(slot)

                @block.scalar
                def _(sc):
                    link = chained(sc, act_chain)

                    def in_proj():
                        sc.wait_ge(z_copied, 1)
                        nc.scalar.activation(z_e, z_gate[:, :, :], ACT.Exp, scale=-1.0).then_inc(silu_e, 1)
                        sc.wait_ge(conv_done, 1)
                        nc.scalar.activation(conv_e, conv, ACT.Exp, scale=-1.0).then_inc(silu_e, 1)

                    def x_dbl(half_paths):
                        if half_paths == 1:
                            sc.wait_ge(xd_done, 2)
                            nc.scalar.activation(xdbl[:, 2:4, :], py[0:RANK + 2 * STATE, :]
                                                 .rearrange("p (k l) -> p k l", k=2),
                                                 ACT.Copy).then_inc(xd_copied, 1)

                    def softplus(half_paths):
                        ks = slice(2 * half_paths, 2 * half_paths + 2)
                        sc.wait_ge(dt_sum, half_paths + 1)
                        link(nc.scalar.activation(delta_x[:, ks, :], delta[:, ks, :], ACT.Abs))
                        nc.scalar.activation(delta_x[:, ks, :], delta_x[:, ks, :], ACT.Exp,
                                             scale=-1.0).then_inc(sp_a, 1)

                    def softplus_log():
                        sc.wait_ge(sp_u, 2)
                        nc.scalar.activation(d_rows[1][0:INNER, :, :], d_rows[0][0:INNER, :, :],
                                             ACT.Ln).then_inc(sp_l, 1)

                    def decays(g):
                        sc.wait_ge(d_in[g % 2], 16 * (g // 2 + 1))
                        if g >= 2:
                            sc.wait_ge(scan_done, g - 1)
                        for k in range(PATHS):
                            at = g * PATHS + k
                            rest = slice(1, TOKENS) if k < 2 else slice(0, TOKENS - 1)
                            ins = nc.scalar.activation(decay[g % 2][:, k, rest], d_rows[g % 2][:, k, rest],
                                                       ACT.Exp, scale=a_neg[:, at:at + 1])
                        ins.then_inc(decay_done, 1)

                    ssm = {"in_proj": in_proj, "x_dbl": x_dbl, "softplus": softplus,
                           "softplus_log": softplus_log}

                    def up(e, i):
                        sc.wait_ge(up_done, e * HCH // 2 + i + 1)
                        if i == 0 and e >= 2:
                            sc.wait_ge(dn_done, TILES * (e - 1))
                        for m in range(2):
                            ins = nc.scalar.activation(act[e % 2][:, 2 * i + m, :],
                                                       up_bank(e * HCH // 2 + i)[:, TOKENS * m:TOKENS * (m + 1)],
                                                       ACT.Gelu,
                                                       bias=b_up[:, e, 2 * i + m:2 * i + m + 1])
                        ins.then_inc(gelu_done, 1)

                    def logits():
                        sc.wait_ge(lg_shift, 1)
                        nc.scalar.activation(gate[:, :, :], gate[:, :, :], ACT.Exp).then_inc(gate_e, 1)

                    ffn = {"up": up, "logits": logits}

                    def others(slot):
                        if run_s:
                            for name, *at in steps(SSM_STEPS, slot):
                                if name in ssm:
                                    ssm[name](*at)
                        if run_f:
                            for name, *at in steps(FFN_STEPS, slot):
                                if name in ffn:
                                    ffn[name](*at)
                        if run_s:
                            for g in steps(DECAYS, slot):
                                decays(g)

                    def attention(l):
                        causal = l == 0
                        sc.wait_ge(h_turned[l], 1)
                        nc.scalar.activation(hT[0:64, 1, :], ps[0:64, 3, 0:TOKENS],
                                             ACT.Copy).then_inc(hT_done[l], 1)
                        others((l, "turned"))
                        for c in range(2):
                            for part in range(2):
                                n = 2 * c + part
                                sc.wait_ge(qk_done[l], n + 1)
                                nc.scalar.activation(high[part][c], ps[0:CGROUP, n, 0:TOKENS],
                                                     ACT.Identity, bias=b_qk[l][:, part, c:c + 1]
                                                     ).then_inc(high_done[l], 1)

                        def copy_stack(u):
                            sc.wait_ge(stack_psum[l], UNITS if u == 4 else u + 1)
                            nc.scalar.activation(q_stack[:, u, :], ps[:, u % 4, 0:TOKENS], ACT.Copy)
                            nc.scalar.activation(k_stack[:, u, :], ps[:, u % 4, TOKENS:2 * TOKENS], ACT.Identity,
                                                 bias=top_one[:, :]).then_inc(stack_even[l], 1)

                        copy_stack(0)
                        copy_stack(2)
                        others((l, "projected"))
                        copy_stack(4)
                        for u in range(UNITS):
                            others((l, 2 * u))
                            sc.wait_ge(st_done[l], u + 1)
                            if u >= 2:
                                sc.wait_ge(av_done[l], u - 1)
                            pair = ps[:, 2 * (u % 2):2 * (u % 2) + 2, :]
                            if causal:
                                for kt in range(TILES):
                                    ins = nc.scalar.activation(
                                        probs[u % 2][:, :, kt, 128 * kt:TOKENS],
                                        pair[:, :, TOKENS * kt + 128 * kt:TOKENS * (kt + 1)], ACT.Exp,
                                        scale=HEAD ** -0.5)
                            else:
                                ins = nc.scalar.activation(
                                    probs[u % 2][:, :, :, :].rearrange("p j t q -> p j (t q)"), pair, ACT.Exp,
                                    scale=HEAD ** -0.5)
                            ins.then_inc(p_done[l], 1)
                            others((l, 2 * u + 1))
                        others((l, "context"))
                        others((l, "spread"))
                        others((l, "output"))

                    if run_a or run_f:
                        sc.wait_ge(w_b, 16 * len(b_loads))
                    if run_a:
                        attention(0)
                        attention(1)
                    else:
                        for slot in SLOTS:
                            others(slot)

                @block.gpsimd
                def _(pool):
                    def rstd(i):
                        pool.wait_ge(var_done[i], 1)
                        nc.gpsimd.tensor_tensor(norm_rstd[:, i, :], norm_var[:, i, :], half[:, :],
                                                ALU.pow).then_inc(rstd_done[i], 1)

                    def group_sums():
                        pool.wait_ge(gn_v, 1)
                        nc.gpsimd.tensor_tensor(gn_rstd[:, :], gn_var[:, :], half[:, :],
                                                ALU.pow).then_inc(gn_r, 1)

                    def silu():
                        pool.wait_ge(u_done, 1)
                        nc.gpsimd.tensor_copy(xs[:, 1, :].rearrange("p (w h) -> p w h", h=SIDE),
                                              xs[:, 0, :].rearrange("p (h w) -> p w h", w=SIDE)
                                              ).then_inc(xs_done, 1)

                    def times_C(g):
                        pool.wait_ge(scan_done, g + 1)
                        if g == 0:
                            pool.wait_ge(bc_in, 16 * 2 * PACK)
                        C_path = C_rows[:, :].rearrange("p (k l) -> p k l", k=PATHS)
                        nc.gpsimd.tensor_tensor(state[g % 2][:, 0::2, :], state[g % 2][:, 0::2, :],
                                                C_path[:, 0::2, :], ALU.mult)
                        nc.gpsimd.tensor_tensor(
                            by_row[g % 2][:, :, :].rearrange("p k (h w) -> p k w h", w=SIDE),
                            state[g % 2][:, 1::2, :].rearrange("p k (w h) -> p k w h", h=SIDE),
                            C_path[:, 1::2, :].rearrange("p k (w h) -> p k w h", h=SIDE),
                            ALU.mult).then_inc(sc_done, 1)

                    ssm = {"group_sums": group_sums, "silu": silu,
                           "y_norm": lambda: rstd(0), "y_out": lambda: rstd(1)}

                    def ffn_norm(part):
                        if part == 1:
                            return
                        rstd(4)
                        pool.wait_ge(v3_done, 1)
                        pool.wait_ge(x2_kept, 1)
                        nc.gpsimd.tensor_tensor(out_tok[:, :, :], out_tok[:, :, :], v3[:, :, :],
                                                ALU.add).then_inc(base_done, 1)

                    def ffn_turn(i):
                        if i == 0:
                            pool.wait_ge(m_turned, 1)
                            nc.gpsimd.tensor_tensor(v2[:, :, :], v2[:, :, :], rows(b_dn),
                                                    ALU.add).then_inc(mres_done, 1)

                    ffn = {"turn": ffn_turn, "norm": ffn_norm}

                    def others(slot):
                        if run_s:
                            for name, *at in steps(SSM_STEPS, slot):
                                if name in ssm:
                                    ssm[name](*at)
                        if run_f:
                            for name, *at in steps(FFN_STEPS, slot):
                                if name in ffn:
                                    ffn[name](*at)
                        if run_s:
                            for g in steps(SCANS, slot):
                                times_C(g)

                    if run_a or run_f:
                        pool.wait_ge(w_b, 16 * len(b_loads))
                    if run_f:
                        nc.gpsimd.tensor_copy(out_tok[:, :, :], x2[:, :, :]).then_inc(x2_kept, 1)
                    if run_a:
                        nc.gpsimd.tensor_tensor(x1[:, :, :], x1[:, :, :], rows(b_o[0]),
                                                ALU.add).then_inc(res_done[0], 1)
                    def context_scale(l, ht):
                        pool.wait_ge(den_inv[l], ht + 1)
                        nc.gpsimd.tensor_tensor(cT[:, ht, :], cT[:, ht, :], inv_den[:, :],
                                                ALU.mult).then_inc(ctx_done[l], 1)

                    if late_setup:
                        attention_constants(pool)
                    for slot in SLOTS:
                        l, at = slot
                        if run_a and at in (5, 9, "spread"):
                            context_scale(l, {5: 0, 9: 1, "spread": 2}[at])
                        if run_a and slot == (0, "output"):
                            rstd(2)
                            rstd(3)
                            pool.wait_ge(h_done, 1)
                            nc.gpsimd.tensor_tensor(v_tok[:, :, :], v_tok[:, :, :], rows(b_o[1]),
                                                    ALU.add).then_inc(res_done[1], 1)
                        others(slot)

            nc.all_engine_barrier(sems_to_clear=clear_range)

        block_of(0, None, None, late_setup=True)
        block_of(1, 0, None)
        with nc.Fori(1, IMAGES - 1) as n:
            block_of(n + 1, n, n - 1)
        block_of(None, IMAGES - 1, IMAGES - 2)
        block_of(None, None, IMAGES - 1)


_HOST = {
    "x": (IMAGES, TOKENS, WIDTH), "w_in": (WIDTH, 2 * INNER), "w_conv": (INNER, 9), "b_conv": (INNER, 1),
    "w_x": (INNER, PATHS, RANK + 2 * STATE), "w_dt": (RANK, PATHS, INNER), "b_dt": (INNER, PATHS),
    "a_log": (128, GROUPS * PATHS), "ds": (INNER, PATHS), "on_g": (INNER,), "on_b": (INNER,),
    "w_out": (INNER, WIDTH),
    "w_qkv0": (WIDTH, 3 * WIDTH), "b_qkv0": (3 * WIDTH,), "w_o0": (WIDTH, WIDTH), "b_o0": (WIDTH,),
    "w_qkv1": (WIDTH, 3 * WIDTH), "b_qkv1": (3 * WIDTH,), "w_o1": (WIDTH, WIDTH), "b_o1": (WIDTH,),
    "ln_g0": (WIDTH,), "ln_b0": (WIDTH,), "ln_g1": (WIDTH,), "ln_b1": (WIDTH,),
    "mlp_w1": (WIDTH, HIDDEN), "mlp_w2": (HIDDEN, WIDTH), "mlp_b2": (WIDTH,),
    "exp_w1": (EXPERTS, WIDTH, HIDDEN), "exp_w2": (EXPERTS, HIDDEN, WIDTH), "exp_b2": (EXPERTS, WIDTH),
    "b_up": (128, 1 + EXPERTS, HCH), "w_gate": (WIDTH, EXPERTS), "b_gate": (EXPERTS,),
}


def kernel(**inputs):
    import numpy as np
    import concourse.bacc as bacc
    from concourse.bass_utils import run_bass_kernel_spmd

    i = {k: np.asarray(v) for k, v in inputs.items()}
    host = {
        "x": i["x"].reshape(IMAGES, TOKENS, WIDTH),
        "w_in": i["L0_conv_in_proj_w"].T,
        "w_conv": i["L0_conv_conv_w"].reshape(INNER, 9),
        "b_conv": i["L0_conv_conv_b"].reshape(INNER, 1),
        "w_x": i["L0_conv_x_proj_w"].transpose(2, 0, 1),
        "w_dt": i["L0_conv_dt_projs_w"].transpose(2, 0, 1),
        "b_dt": i["L0_conv_dt_projs_b"].T,
        "a_log": i["L0_conv_A_logs"].reshape(PATHS, GROUPS, PACK, STATE).transpose(2, 3, 1, 0)
        .reshape(128, GROUPS * PATHS),
        "ds": i["L0_conv_Ds"].reshape(PATHS, INNER).T,
        "on_g": i["L0_conv_out_norm_g"], "on_b": i["L0_conv_out_norm_b"],
        "w_out": i["L0_conv_out_proj_w"].T,
        "w_qkv0": i["L1_attn_W_attn"], "b_qkv0": i["L1_attn_b_attn"],
        "w_o0": i["L1_attn_W_proj"], "b_o0": i["L1_attn_b_proj"],
        "w_qkv1": i["L1_ffn_in_w"].T, "b_qkv1": i["L1_ffn_in_b"],
        "w_o1": i["L1_ffn_out_w"].T, "b_o1": i["L1_ffn_out_b"],
        "ln_g0": i["L1_ffn_ln1_g"], "ln_b0": i["L1_ffn_ln1_b"],
        "ln_g1": i["L1_ffn_ln2_g"], "ln_b1": i["L1_ffn_ln2_b"],
        "mlp_w1": i["L1_ffn_mlp_w1"], "mlp_w2": i["L1_ffn_mlp_w2"], "mlp_b2": i["L1_ffn_mlp_b2"],
        "exp_w1": i["L1_ffn_exp_w1"], "exp_w2": i["L1_ffn_exp_w2"], "exp_b2": i["L1_ffn_exp_b2"],
        "b_up": np.concatenate([i["L1_ffn_mlp_b1"][None], i["L1_ffn_exp_b1"]])
        .reshape(1 + EXPERTS, HCH, 128).transpose(2, 0, 1),
        "w_gate": i["L1_ffn_gate_w"].T, "b_gate": i["L1_ffn_gate_b"],
    }
    nc = bacc.Bacc("TRN2", target_bir_lowering=False, num_devices=1)
    t, arrays = {}, {}
    for name, shape in _HOST.items():
        arrays[f"{name}_dram"] = np.ascontiguousarray(host[name])
        assert arrays[f"{name}_dram"].shape == shape
        t[name] = nc.dram_tensor(f"{name}_dram", shape, F32, kind="ExternalInput").ap()
    t["out"] = nc.dram_tensor("out_dram", (IMAGES, TOKENS, WIDTH), F32, kind="ExternalOutput").ap()
    build(nc, t)
    r = run_bass_kernel_spmd(nc, [arrays], core_ids=[0])
    return r.results[0]["out_dram"].reshape(IMAGES, SIDE, SIDE, WIDTH)
```

```python
from contextlib import ExitStack

import concourse.bass as bass
from concourse import mybir

F32 = mybir.dt.float32
BF16 = mybir.dt.bfloat16
F32R = mybir.dt.float32r
ALU = mybir.AluOpType
ACT = mybir.ActivationFunctionType
AX = mybir.AxisListType

IMAGES, SIDE, WIDTH = 4, 16, 192
TOKENS = SIDE * SIDE
TILES = TOKENS // 128
INNER, STATE, PATHS, RANK = 96, 16, 4, 12
PACK = 128 // STATE
GROUPS = INNER // PACK
GN_GROUP = WIDTH // 32
HEADS, HEAD = 12, 16
QUAD = 4
HTILES = HEADS // QUAD
UNITS = HEADS // 2
HIDDEN, EXPERTS, TOPK = 768, 4, 2
HCH = HIDDEN // 128
CGROUP = WIDTH // 2
HIGH_PARTS = [slice(0, 3, 2), slice(0, 2)]
LOW_PARTS = [slice(1, 2), slice(2, 3)]
TOP_ROW = 3 * HEAD
CH = [(0, 128), (128, 64)]
EPS = 1e-5
MASKED = -1e30
A_LOG_MAX = 80.0

SLOTS = [(l, s) for l in range(2) for s in ("turned", "projected", *range(2 * UNITS), "context", "spread",
                                            "output")]

SSM_STEPS = {
    (0, "turned"): [("x_turn",)],
    (0, "projected"): [("group_sums",)],
    (0, 1): [("in_proj",)],
    (0, 2): [("silu",)],
    (0, 5): [("x_dbl", 0)],
    (0, 7): [("x_dbl", 1)],
    (0, 9): [("dt", 0)],
    (0, "spread"): [("dt", 1), ("softplus", 0), ("softplus", 1), ("softplus_log",)],
    (1, 9): [("y_copy",)],
    (1, 10): [("y_norm",)],
    (1, "context"): [("y_turn",)],
    (1, "spread"): [("y_out",)],
}
DECAYS = {
    (0, "output"): [0, 1, 2],
    (1, "turned"): [3],
    (1, "projected"): [4],
    (1, 0): [5],
    (1, 1): [6],
    (1, 3): [7],
    (1, 4): [8],
    (1, 5): [9],
    (1, 6): [10, 11],
}
SCANS = {
    (0, "output"): [0, 1],
    (1, "projected"): [2],
    (1, 0): [3, 4],
    (1, 1): [5],
    (1, 3): [6, 7],
    (1, 4): [8],
    (1, 5): [9],
    (1, 7): [10, 11],
}
Y_SUMS = {
    (1, "projected"): [0, 1],
    (1, 0): [2],
    (1, 1): [3],
    (1, 3): [4, 5],
    (1, 4): [6],
    (1, 5): [7],
    (1, 6): [8],
    (1, 7): [9],
    (1, 8): [10],
    (1, 9): [11],
}

FFN_STEPS = {
    (0, "turned"): [("turn", 0)],
    (0, "projected"): [("up", 0, 0)],
    (0, 0): [("up", 0, 1), ("up", 0, 2)],
    (0, 1): [("down", 0, 0), ("down", 0, 1)],
    (0, 3): [("norm", 0)],
    (0, 5): [("norm", 1)],
    (0, 6): [("turn", 1)],
    (0, 7): [("up", 1, 0)],
    (0, 8): [("logits",)],
    (0, 9): [("up", 1, 1)],
    (0, 10): [("turn_gates",)],
    (0, "context"): [("bias",)],
    (0, "spread"): [("up", 1, 2)],
    (0, "output"): [("up", 2, 0), ("down", 1, 0), ("up", 2, 1), ("down", 1, 1), ("up", 2, 2)],
    (1, "turned"): [("add", 1), ("up", 3, 0)],
    (1, "projected"): [("down", 2, 0)],
    (1, 0): [("down", 2, 1)],
    (1, 1): [("up", 3, 1), ("add", 2), ("up", 3, 2)],
    (1, 5): [("down", 3, 0)],
    (1, 7): [("up", 4, 0)],
    (1, 8): [("down", 3, 1), ("up", 4, 1), ("add", 3)],
    (1, 9): [("up", 4, 2)],
    (1, 11): [("down", 4, 0)],
    (1, "context"): [("down", 4, 1), ("add", 4)],
}


def build(nc, t):
    ctx = ExitStack()
    with ctx:
        def sb(name, shape, dt=F32):
            return ctx.enter_context(nc.sbuf_tensor(name, shape, dt))

        def bank(name):
            return ctx.enter_context(nc.psum_tensor(name, [128, 512], F32))

        def sem(name):
            return ctx.enter_context(nc.semaphore(name))

        ident = sb("ident", [128, 128])
        identb = sb("identb", [128, 128], BF16)
        maskq = sb("maskq", [128, 128], BF16)
        maskk = sb("maskk", [128, 128], BF16)
        gsum = sb("gsum", [128, 2, WIDTH])
        sel = sb("sel", [128, (2 * GROUPS - 1) * PACK])
        den_sel = sb("den_sel", [128, QUAD, 32])
        dsum = sb("dsum", [INNER, 1])
        ddiag = sb("ddiag", [INNER, INNER])
        half = sb("half", [128, 2])
        lower = sb("lower", [128, EXPERTS, EXPERTS])
        w_in = sb("w_in", [128, 2, WIDTH])
        w_conv = sb("w_conv", [INNER, 9])
        b_conv = sb("b_conv", [INNER, 1])
        w_x = sb("w_x", [INNER, PATHS, RANK + 2 * STATE])
        w_dt = sb("w_dt", [RANK, PATHS, INNER])
        b_dt = sb("b_dt", [INNER, PATHS])
        a_log = sb("a_log", [128, GROUPS * PATHS])
        a_neg = sb("a_neg", [128, GROUPS * PATHS])
        ds_in = sb("ds_in", [INNER, PATHS])
        on_g = sb("on_g", [128, INNER])
        on_b = sb("on_b", [128, INNER])
        w_out = sb("w_out", [INNER, WIDTH])
        w_qkv = [sb(f"w_qkv{l}", [128, 2, 3 * WIDTH]) for l in range(2)]
        to_stack = sb("to_stack", [128, 2, 2, 128], F32R)
        top_one = sb("top_one", [128, 1])
        w_o = [sb(f"w_o{l}", [128, HTILES, WIDTH]) for l in range(2)]
        b_qk = [sb(f"b_qk{l}", [CGROUP, 2, 2]) for l in range(2)]
        b_v = [sb(f"b_v{l}", [128, WIDTH]) for l in range(2)]
        b_o = [sb(f"b_o{l}", [128, WIDTH]) for l in range(2)]
        h_g = sb("h_g", [128, 2])
        h_b = sb("h_b", [128, 2])
        f_g = sb("f_g", [128, WIDTH])
        f_b = sb("f_b", [128, WIDTH])
        w_up = sb("w_up", [128, 1 + EXPERTS, HIDDEN])
        w_up_stack = sb("w_up_stack", [128, 1 + EXPERTS, HIDDEN], F32R)
        b_up = sb("b_up", [128, 1 + EXPERTS, HCH])
        w_dn = sb("w_dn", [128, 1 + EXPERTS, HCH, WIDTH])
        b_dn = sb("b_dn", [128, WIDTH])
        b_ex = sb("b_ex", [EXPERTS, WIDTH])
        w_gate = sb("w_gate", [128, 2, EXPERTS])
        b_gate = sb("b_gate", [128, EXPERTS])

        x_tok = sb("x_tok", [128, TILES, WIDTH])
        gn_raw = sb("gn_raw", [128, 2, 6])
        gn_mv = sb("gn_mv", [128, 2, 2])
        gn_sq = sb("gn_sq", [128, 2])
        gn_m = sb("gn_m", [128, 2, 2])
        gn_var = sb("gn_var", [128, 2])
        gn_rstd = sb("gn_rstd", [128, 2])
        gn_shift = sb("gn_shift", [128, 2])
        pad = sb("pad", [INNER, SIDE + 2, SIDE + 2])
        z_gate = sb("z_gate", [128, TILES, INNER])
        xs = sb("xs", [INNER, 2, TOKENS])
        xdbl = sb("xdbl", [RANK + 2 * STATE, PATHS, TOKENS])
        delta = sb("delta", [INNER, PATHS, TOKENS])
        delta_x = sb("delta_x", [INNER, PATHS, TOKENS])
        B_rows = sb("B_rows", [128, PATHS * TOKENS])
        C_rows = sb("C_rows", [128, PATHS * TOKENS])
        d_rows = [sb(f"d_rows{i}", [128, PATHS, TOKENS]) for i in range(2)]
        dx_rows = [sb(f"dx_rows{i}", [128, PATHS * TOKENS]) for i in range(2)]
        decay = [sb(f"decay{i}", [128, PATHS, TOKENS]) for i in range(2)]
        state = [sb(f"state{i}", [128, PATHS, TOKENS]) for i in range(2)]
        by_row = [sb(f"by_row{i}", [128, 2, TOKENS]) for i in range(2)]
        xgT = state[0][:, 0:2, :]
        conv = state[0][0:INNER, 2, :]
        conv_e = state[0][0:INNER, 3, :]
        z_e = state[1][:, 0, 0:TILES * INNER].rearrange("p (t c) -> p t c", t=TILES)
        y_g = by_row[1][:, 0, 0:TILES * INNER].rearrange("p (t c) -> p t c", t=TILES)
        yT = by_row[0][0:INNER, 0, :]
        x1 = sb("x1", [128, TILES, WIDTH])

        norm_raw = sb("norm_raw", [128, 5, TILES, 6])
        norm_mv = sb("norm_mv", [128, 5, TILES, 2])
        norm_var = sb("norm_var", [128, 5, TILES])
        norm_rstd = sb("norm_rstd", [128, 5, TILES])
        norm_shift = sb("norm_shift", [128, 5, TILES])
        h_tok = sb("h_tok", [128, TILES, WIDTH])
        hT = sb("hT", [128, 2, TOKENS])
        q_stack = sb("q_stack", [128, UNITS, TOKENS], F32R)
        k_stack = sb("k_stack", [128, UNITS, TOKENS], F32R)
        high = [[stack[0:CGROUP, 2 + 2 * c, :] for c in range(2)] for stack in (q_stack, k_stack)]
        low = [[stack[0:CGROUP, 3 + 2 * c, :] for c in range(2)] for stack in (q_stack, k_stack)]
        v_aug = sb("v_aug", [128, TILES, HEADS, 32])
        top = sb("top", [128, 2, TILES, 128], F32R)
        probs = [sb(f"probs{i}", [128, 2, 2, TOKENS]) for i in range(2)]
        inv_den = sb("inv_den", [128, TOKENS])
        cT = sb("cT", [128, HTILES, TOKENS])
        x2 = sb("x2", [128, TILES, WIDTH])
        v_tok = sb("v_tok", [128, TILES, WIDTH])
        v2 = sb("v2", [128, TILES, WIDTH])
        f_tok = sb("f_tok", [128, TILES, WIDTH])
        fT = sb("fT", [128, TOKENS])
        fT_high = sb("fT_high", [128, TOKENS], F32R)
        fT_parts = sb("fT_parts", [128, TOKENS], F32R)
        v3 = sb("v3", [128, TILES, WIDTH])
        act = [sb(f"act{i}", [128, HCH, TOKENS]) for i in range(2)]
        up_raw = [(2 * i + h, 0, act[i][:, 3 * h:3 * (h + 1), :].rearrange("p m l -> p (m l)"))
                  for i in range(2) for h in range(2)]
        up_raw += [(EXPERTS, TILES * WIDTH * h, buf[:, :, :].rearrange("p t c -> p (t c)"))
                   for h, buf in enumerate((v3, f_tok))]
        logit = sb("logit", [128, TILES, EXPERTS])
        beats = sb("beats", [128, TILES, EXPERTS, EXPERTS])
        ties = sb("ties", [128, TILES, EXPERTS, EXPERTS])
        rank = sb("rank", [128, TILES, EXPERTS])
        best = sb("best", [128, TILES])
        gate = sb("gate", [128, TILES, EXPERTS])
        gsumr = sb("gsumr", [128, TILES])
        gateT = sb("gateT", [EXPERTS, TOKENS])
        out_tok = sb("out_tok", [128, TILES, WIDTH])

        ps = ctx.enter_context(nc.psum_tensor("ps", [128, 4, 512], F32))
        pm = bank("pm")
        py = bank("py")
        pu = bank("pu")
        pd = bank("pd")

        w_a = sem("weights_a_loaded")
        w_b = sem("weights_b_loaded")
        up_high = sem("w_up_high_parts_ready")
        consts = sem("scan_constants_built")
        pool_set = sem("constants_chain")
        rates = sem("skip_and_decay_rates")
        rates_e = sem("decay_rate_exponentials")

        per_image = []

        def isem(name):
            s = sem(name)
            per_image.append(s)
            return s

        x_in = isem("x_loaded")
        x_turned = isem("x_turned")
        gn_stats = isem("gn_channel_stats")
        gn_sums = isem("gn_group_sums")
        gn_v = isem("gn_variance")
        gn_r = isem("gn_rstd")
        xg_done = isem("x_group_normed")
        xh_done = isem("conv_input_and_z_ready")
        conv_done = isem("conv_done")
        silu_e = isem("silu_exponentials")
        u_done = isem("scan_input_ready")
        z_copied = isem("z_copied")
        xs_done = isem("scan_orders_ready")
        xd_done = isem("x_dbl_ready")
        xd_copied = isem("x_dbl_copied")
        bc_in = isem("BC_rows_loaded")
        dt_done = isem("dt_ready")
        dt_sum = isem("dt_with_bias_ready")
        sp_a = isem("softplus_exp_ready")
        sp_u = isem("softplus_sum_ready")
        sp_l = isem("softplus_log_ready")
        d_done = isem("delta_ready")
        dx_done = isem("delta_x_ready")
        d_in = [isem(f"delta_rows_loaded{i}") for i in range(2)]
        dx_in = [isem(f"delta_x_rows_loaded{i}") for i in range(2)]
        decay_done = isem("decay_ready")
        scan_done = isem("state_scanned")
        c_done = isem("state_times_C")
        sc_done = isem("states_ready")
        y_part = isem("y_group_summed")
        yg_done = isem("y_gated")
        y_back = isem("y_by_tokens")
        y_turned = isem("y_turned")
        yT_done = isem("yT_copied")
        o_done = isem("scan_output_projected")
        x1_done = isem("x1_ready")
        var_done = [isem(f"variance_ready{i}") for i in range(5)]
        rstd_done = [isem(f"rstd_ready{i}") for i in range(5)]
        h_done = isem("normed_ready")
        h_turned = [isem(f"normed_turned{i}") for i in range(2)]
        hT_done = [isem(f"normed_T_copied{i}") for i in range(2)]
        v_done = [isem(f"values_projected{i}") for i in range(2)]
        qk_done = [isem(f"queries_keys_projected{i}") for i in range(2)]
        high_done = [isem(f"high_parts_ready{i}") for i in range(2)]
        low_done = [isem(f"low_parts_ready{i}") for i in range(2)]
        v_copied = [isem(f"values_copied{i}") for i in range(2)]
        stack_psum = [isem(f"stack_in_psum{i}") for i in range(2)]
        stack_even = [isem(f"even_stack_copied{i}") for i in range(2)]
        stack_odd = [isem(f"odd_stack_copied{i}") for i in range(2)]
        s_done = [isem(f"scores_ready{i}") for i in range(2)]
        top_done = [isem(f"row_max_ready{i}") for i in range(2)]
        top_turned = [isem(f"row_max_turned{i}") for i in range(2)]
        q_shifted = [isem(f"row_max_in_q{i}") for i in range(2)]
        st_done = [isem(f"shifted_scores_ready{i}") for i in range(2)]
        p_done = [isem(f"probs_ready{i}") for i in range(2)]
        av_done = [isem(f"context_summed{i}") for i in range(2)]
        ctx_done = [isem(f"context_ready{i}") for i in range(2)]
        ctx_copied = [isem(f"context_copied{i}") for i in range(2)]
        den_inv = [isem(f"sums_inverted{i}") for i in range(2)]
        den_done = [isem(f"sums_spread{i}") for i in range(2)]
        proj_done = [isem(f"attention_projected{i}") for i in range(2)]
        res_done = [isem(f"residual_ready{i}") for i in range(2)]
        x2_kept = isem("x2_kept")
        m_turned = isem("ffn_input_turned")
        mT_done = isem("ffn_input_T_copied")
        v2_done = isem("v2_ready")
        mres_done = isem("mlp_residual_ready")
        xm_done = isem("moe_input_ready")
        v3_done = isem("v3_ready")
        base_done = isem("output_residual_ready")
        up_done = isem("hidden_ready")
        gelu_done = isem("gelu_ready")
        dn_done = isem("down_ready")
        dn_used = isem("down_used")
        lg_done = isem("logits_ready")
        lg_shift = isem("logits_shifted")
        gate_e = isem("gate_exponentials")
        gate_done = isem("gates_ready")
        gate_turned = isem("gates_turned")
        gateT_done = isem("gates_T_copied")
        gb_done = isem("gated_biases_ready")
        acc_done = isem("output_started")
        out_done = isem("output_ready")
        stored = isem("output_stored")
        dve_chain = isem("vector_chain")
        act_chain = isem("scalar_chain")
        pool_chain = isem("gpsimd_chain")
        numbers = sorted(s.num for s in per_image)
        assert numbers == list(range(numbers[0], numbers[0] + len(numbers)))
        clear_range = range(numbers[0], numbers[-1] + 1)

        def chained(eng, chain, first=0):
            count = [first]

            def link(ins):
                count[0] += 1
                ins.then_inc(chain, 1)
                eng.wait_ge(chain, count[0])
            return link

        def load_x(sp, image):
            sp.dma_start(x_tok[:, :, :], t["x"][bass.ds(image, 1)].rearrange("o (t p) c -> p (o t) c", p=128)
                         ).then_inc(x_in, 16)

        a_loads = [
            (w_in[:, 0, :], t["w_in"][0:128, :]), (w_in[0:64, 1, :], t["w_in"][128:192, :]),
            (w_conv[:, :], t["w_conv"]), (b_conv[:, :], t["b_conv"]),
            (w_x[:, :, :], t["w_x"]), (w_dt[:, :, :], t["w_dt"]), (b_dt[:, :], t["b_dt"]),
            (a_log[:, :], t["a_log"]), (ds_in[:, :], t["ds"]),
            (on_g[:, :], t["on_g"].partition_broadcast(128)),
            (on_b[:, :], t["on_b"].partition_broadcast(128)),
            (w_out[:, :], t["w_out"]),
        ]
        b_loads = []
        for l in range(2):
            w, b = t[f"w_qkv{l}"], t[f"b_qkv{l}"]
            for c, (c0, cn) in enumerate(CH):
                b_loads.append((w_qkv[l][0:cn, c, :], w[c0:c0 + cn, :]))
            w_heads = t[f"w_o{l}"].rearrange("(t j i) n -> j i t n", j=QUAD, i=HEAD)
            for j in range(QUAD):
                b_loads.append((w_o[l][32 * j:32 * j + HEAD, :, :], w_heads[j]))
            b_loads.append((b_qk[l][:, :, :], b[0:2 * WIDTH].rearrange("(p c r) -> r p c", p=2, r=CGROUP)))
            b_loads.append((b_v[l][:, :], b[2 * WIDTH:3 * WIDTH].partition_broadcast(128)))
            b_loads.append((b_o[l][:, :], t[f"b_o{l}"].partition_broadcast(128)))
        b_loads.append((f_g[:, :], t["ln_g1"].partition_broadcast(128)))
        b_loads.append((f_b[:, :], t["ln_b1"].partition_broadcast(128)))
        for c, (c0, cn) in enumerate(CH):
            b_loads.append((h_g[0:cn, c:c + 1], t["ln_g0"][c0:c0 + cn].unsqueeze(1)))
            b_loads.append((h_b[0:cn, c:c + 1], t["ln_b0"][c0:c0 + cn].unsqueeze(1)))
            b_loads.append((w_gate[0:cn, c, :], t["w_gate"][c0:c0 + cn, :]))
        b_loads.append((w_gate[64:128, 1, :], t["w_gate"][128:WIDTH, :]))
        b_loads.append((w_up[:, 0, :], t["mlp_w1"][0:128, :]))
        b_loads.append((w_up[:, 1:1 + EXPERTS, :], t["exp_w1"][:, 0:128, :].rearrange("e k n -> k e n")))
        for e, n0, buf in up_raw:
            last = (t["exp_w1"][e - 1] if e else t["mlp_w1"])[128:WIDTH, n0:n0 + buf.shape[1]]
            b_loads += [(buf[0:64, :], last), (buf[64:128, :], last)]
        b_loads.append((w_dn[:, 0, :, :], t["mlp_w2"].rearrange("(m p) n -> p m n", p=128)))
        b_loads.append((w_dn[:, 1:1 + EXPERTS, :, :].rearrange("p e m n -> p (e m) n"),
                        t["exp_w2"].rearrange("e (m p) n -> p (e m) n", p=128)))
        b_loads += [
            (b_up[:, :, :], t["b_up"]), (b_dn[:, :], t["mlp_b2"].partition_broadcast(128)),
            (b_ex[:, :], t["exp_b2"]), (b_gate[:, :], t["b_gate"].partition_broadcast(128)),
        ]

        with nc.Block() as block:
            @block.sync
            def _(sp):
                load_x(sp, 0)
                with nc.allow_non_contiguous_dma(reason="short rows of biases, once"):
                    for dst, src in a_loads:
                        sp.dma_start(dst, src).then_inc(w_a, 16)

            @block.gpsimd
            def _(pool):
                nc.gpsimd.memset(half[:], -0.5)
                nc.gpsimd.memset(ident[:], 0.0).then_inc(pool_set, 1)
                pool.wait_ge(pool_set, 1)
                nc.gpsimd.affine_select(out=ident[:, :], in_=ident[:, :], compare_op=ALU.not_equal, fill=1.0,
                                        base=0, pattern=[[-1, 128]], channel_multiplier=1).then_inc(pool_set, 1)

            @block.vector
            def _(dve):
                for buf in (w_o[0], w_o[1], pad, gn_raw, gn_mv, gn_m):
                    nc.vector.memset(buf[:], 0.0)
                for buf in decay:
                    nc.vector.memset(buf[:, 0:2, 0:1], 0.0)
                    nc.vector.memset(buf[:, 2:4, TOKENS - 1:TOKENS], 0.0)

        def scan_constants(pool, link):
            nc.gpsimd.memset(sel[:], 1.0)
            link(nc.gpsimd.memset(gsum[:], 1.0 / GN_GROUP))
            for c, (c0, cn) in enumerate(CH):
                for base, sign in ((c0, 1), (GN_GROUP - 1 - c0, -1)):
                    ins = nc.gpsimd.affine_select(
                        out=gsum[:, c, :], in_=gsum[:, c, :], compare_op=ALU.is_ge, fill=0.0, base=base,
                        pattern=[[-GN_GROUP * sign, WIDTH // GN_GROUP], [0, GN_GROUP]],
                        channel_multiplier=sign)
                    if (c, sign) != (1, -1):
                        link(ins)
            ins.then_inc(consts, 1)
            pool.wait_ge(consts, 1)
            shift = STATE * PACK * (GROUPS - 1)
            for base, sign in ((shift, 1), (STATE - 1 - shift, -1)):
                ins = nc.gpsimd.affine_select(out=sel[:, :], in_=sel[:, :], compare_op=ALU.is_ge, fill=0.0,
                                              base=base, pattern=[[-STATE * sign, (2 * GROUPS - 1) * PACK]],
                                              channel_multiplier=sign)
                if sign == 1:
                    link(ins)
            ins.then_inc(consts, 1)
            pool.wait_ge(consts, 2)

        def attention_constants(link):
            for tile, value in ((maskq, 0.0), (maskk, 0.0), (den_sel, 0.0), (lower, 1.0), (top_one, 0.0),
                                (cT, 0.0), (v_aug, 0.0)):
                ins = nc.gpsimd.memset(tile[:], value)
            link(ins)
            link(nc.gpsimd.tensor_copy(top[:, :, :, :].rearrange("p a b m -> p (a b m)"),
                                       v_aug[:, :, :, :].rearrange("p t h m -> p (t h m)")[:, 0:4 * 128]))
            link(nc.gpsimd.memset(v_aug[:, :, :, HEAD:HEAD + 1], 1.0))
            link(nc.gpsimd.affine_select(out=maskq[:, :], in_=maskq[:, :], compare_op=ALU.is_ge,
                                         fill=MASKED, base=0, pattern=[[-1, 128]], channel_multiplier=1))
            link(nc.gpsimd.affine_select(out=maskk[:, :], in_=maskk[:, :], compare_op=ALU.is_ge,
                                         fill=MASKED, base=0, pattern=[[1, 128]], channel_multiplier=-1))
            link(nc.gpsimd.affine_select(out=lower[:, :, :], in_=lower[:, :, :], compare_op=ALU.is_gt,
                                         fill=0.0, base=0, pattern=[[1, EXPERTS], [-1, EXPERTS]],
                                         channel_multiplier=0))
            link(nc.gpsimd.affine_select(out=den_sel[:, :, :], in_=den_sel[:, :, :],
                                         compare_op=ALU.not_equal, fill=1.0, base=-HEAD,
                                         pattern=[[-32, QUAD], [0, 32]], channel_multiplier=1))
            for j in range(2):
                link(nc.gpsimd.affine_select(
                    out=top_one[:, :], in_=top_one[:, :], compare_op=ALU.not_equal, fill=1.0,
                    base=-(64 * j + TOP_ROW), pattern=[[0, 1]], channel_multiplier=1))
            spread_of = cT[:, 0:2, :].rearrange("p a (x j r i) -> p a x j r i", x=2, j=2, r=4)
            for part in range(2):
                for level, parts in ((0, HIGH_PARTS[part]), (1, LOW_PARTS[part])):
                    into = spread_of[:, part, level, :, parts, :]
                    for row in range(0, CGROUP, 32):
                        link(nc.gpsimd.affine_select(
                            out=into, in_=into, compare_op=ALU.not_equal, fill=1.0, base=-row,
                            pattern=[[-HEAD, 2], [0, into.shape[2]], [-1, HEAD]], channel_multiplier=1))
            link(nc.gpsimd.tensor_copy(to_stack[:, :, :, :].rearrange("p a b m -> p a (b m)"),
                                       cT[:, 0:2, :]))
            link(nc.gpsimd.tensor_copy(identb[:, :], ident[:, :]))

        def turn(first, second, src):
            for tl in range(TILES):
                for c, (c0, cn) in enumerate(CH):
                    mm = nc.tensor.transpose((first, second)[c][0:cn, tl * 128:(tl + 1) * 128],
                                             src[:, tl, c0:c0 + cn], ident[:, :])
            return mm

        def chunks(out, lhs, rhs, start=True):
            for c, (_, cn) in enumerate(CH):
                mm = nc.tensor.matmul(out, lhs(c, cn), rhs(c, cn), start=(c == 0), stop=(c == 1))
            return mm

        def flat(buf):
            return buf[:, :, :].rearrange("p k l -> p (k l)")

        def two_tiles(bank):
            return bank[:, 0:TILES * WIDTH].rearrange("p (t c) -> p t c", t=TILES)

        def rows(gain):
            return gain[:, :].unsqueeze(1).to_broadcast([128, TILES, gain.shape[1]])

        def block_of(ssm_at, att_at, ffn_at, opening=False, split_w_up=False):
            run_s, run_a, run_f = ssm_at is not None, att_at is not None, ffn_at is not None

            up_banks = 1 if run_a else 4

            add_paths = run_f

            states = [buf[:, :, :] for buf in state]
            states_by_row = [buf[:, :, :] for buf in by_row]
            if opening:
                states += [buf[:, :, :, :].rearrange("p j t q -> p (j t) q") for buf in probs]
                states_by_row += [hT[:, :, :], cT[:, 0:2, :]]
            held = len(states)

            def up_bank(n):
                return pu if run_a else ps[:, n % up_banks, :]

            def steps(table, slot):
                return table.get(slot, [])

            with nc.Block() as block:
                @block.sync
                def _(sp):
                    if run_s and not opening:
                        load_x(sp, ssm_at)
                    if opening:
                        with nc.allow_non_contiguous_dma(reason="short rows of heads and biases, once"):
                            for dst, src in b_loads:
                                sp.dma_start(dst, src).then_inc(w_b, 16)
                    if run_s:
                        sp.wait_ge(xd_copied, 2)
                        for dst, first in ((B_rows, RANK), (C_rows, RANK + STATE)):
                            for c in range(PACK):
                                sp.dma_start(dst[STATE * c:STATE * (c + 1), :], xdbl[first:first + STATE, :, :]
                                             .rearrange("n k l -> n (k l)")).then_inc(bc_in, 16)
                        for g in range(GROUPS):
                            channels = slice(PACK * g, PACK * (g + 1))
                            if g == 0:
                                sp.wait_ge(d_done, 1)
                            if g >= 2:
                                sp.wait_ge(decay_done, g - 1)
                            sp.dma_start(d_rows[g % 2][:, :, :],
                                         delta[channels, :, :].rearrange("c k l -> c (k l)")
                                         .unsqueeze(1).to_broadcast([PACK, STATE, PATHS * TOKENS])
                                         ).then_inc(d_in[g % 2], 16)
                            if g == 0:
                                sp.wait_ge(dx_done, 1)
                            if g >= 2:
                                sp.wait_ge(scan_done, g - 1)
                            sp.dma_start(dx_rows[g % 2][:, :],
                                         delta_x[channels, :, :].rearrange("c k l -> c (k l)")
                                         .unsqueeze(1).to_broadcast([PACK, STATE, PATHS * TOKENS])
                                         ).then_inc(dx_in[g % 2], 16)
                    if run_f:
                        sp.wait_ge(out_done, TILES)
                        sp.dma_start(t["out"][bass.ds(ffn_at, 1)].rearrange("o (t p) c -> p (o t) c", p=128),
                                     out_tok[:, :, :]).then_inc(stored, 16)
                        sp.wait_ge(stored, 16)

                @block.tensor
                def _(pe):
                    def x_turn():
                        pe.wait_ge(x_in, 16)
                        turn(py[:, 0:TOKENS], py[:, TOKENS:2 * TOKENS], x_tok).then_inc(x_turned, 1)

                    def group_sums():
                        if opening:
                            pe.wait_ge(consts, 1)
                        pe.wait_ge(gn_stats, 1)
                        for m, (m0, mn) in enumerate(CH):
                            mm = chunks(py[0:mn, 2 * m:2 * m + 2],
                                        lambda c, cn: gsum[0:cn, c, m0:m0 + mn],
                                        lambda c, cn: gn_mv[0:cn, c, :])
                        mm.then_inc(gn_sums, 1)

                    def in_proj():
                        if opening:
                            pe.wait_ge(w_a, 16 * len(a_loads))
                        pe.wait_ge(xg_done, 2)
                        chunks(py[0:INNER, 0:TOKENS], lambda c, cn: w_in[0:cn, c, 0:INNER],
                               lambda c, cn: xgT[0:cn, c, :])
                        for tl in range(TILES):
                            at = TOKENS + INNER * tl
                            mm = chunks(py[:, at:at + INNER],
                                        lambda c, cn: xgT[0:cn, c, 128 * tl:128 * (tl + 1)],
                                        lambda c, cn: w_in[0:cn, c, INNER:2 * INNER])
                        mm.then_inc(xh_done, 1)

                    def x_dbl(half_paths):
                        if half_paths == 0:
                            pe.wait_ge(xs_done, 1)
                        else:
                            pe.wait_ge(xd_copied, 1)
                        for o in range(2):
                            mm = nc.tensor.matmul(py[0:RANK + 2 * STATE, TOKENS * o:TOKENS * (o + 1)],
                                                  w_x[:, 2 * half_paths + o, :], xs[:, o, :],
                                                  start=True, stop=True)
                        mm.then_inc(xd_done, 1)

                    def dt(half_paths):
                        if half_paths == 0:
                            pe.wait_ge(xd_copied, 2)
                        else:
                            pe.wait_ge(dt_sum, 1)
                        for o in range(2):
                            k = 2 * half_paths + o
                            mm = nc.tensor.matmul(py[0:INNER, TOKENS * o:TOKENS * (o + 1)],
                                                  w_dt[:, k, :], xdbl[0:RANK, k, :], start=True, stop=True)
                        mm.then_inc(dt_done, 1)

                    def y_sum(g):
                        if g == 0:
                            if opening:
                                pe.wait_ge(rates, 2)
                                pe.wait_ge(consts, 2)
                            pe.wait_ge(dt_sum, 2)
                            nc.tensor.matmul(py[0:INNER, 0:TOKENS], ddiag[:, :], xs[:, 0, :],
                                             start=True, stop=False, skip_group_check=True)
                        pe.wait_ge(sc_done, g + 1)
                        first = PACK * (GROUPS - 1 - g)
                        paths = 1 if add_paths else 2
                        for part in ([states[g % held][:, 2 * i, :] for i in range(paths)]
                                     + [states_by_row[g % held][:, i, :] for i in range(paths)]):
                            mm = nc.tensor.matmul(py[0:INNER, 0:TOKENS], sel[:, first:first + INNER], part,
                                                  start=False, stop=(g == GROUPS - 1), skip_group_check=True)
                        mm.then_inc(y_part, 1)

                    def y_norm():
                        pe.wait_ge(yT_done, 1)
                        for tl in range(TILES):
                            mm = nc.tensor.transpose(py[:, INNER * tl:INNER * (tl + 1)],
                                                     yT[:, 128 * tl:128 * (tl + 1)], ident[0:INNER, 0:INNER])
                        mm.then_inc(y_back, 1)

                    def y_turn():
                        pe.wait_ge(yg_done, 1)
                        for tl in range(TILES):
                            mm = nc.tensor.transpose(py[0:INNER, 128 * tl:128 * (tl + 1)],
                                                     y_g[:, tl, :], ident[:, :])
                        mm.then_inc(y_turned, 1)

                    def y_out():
                        pe.wait_ge(yT_done, 2)
                        for tl in range(TILES):
                            mm = nc.tensor.matmul(py[:, WIDTH * tl:WIDTH * (tl + 1)],
                                                  yT[:, 128 * tl:128 * (tl + 1)], w_out[:, :],
                                                  start=True, stop=True)
                        mm.then_inc(o_done, 1)

                    ssm = {"x_turn": x_turn, "group_sums": group_sums, "in_proj": in_proj, "x_dbl": x_dbl,
                           "dt": dt, "y_norm": y_norm, "y_turn": y_turn, "y_out": y_out}

                    def ffn_turn(i):
                        if i == 1:
                            pe.wait_ge(xm_done, 1)
                        src = (v2, f_tok)[i]
                        turn(pu, pu[:, TOKENS:2 * TOKENS], src)
                        for tl in range(TILES):
                            mm = nc.tensor.matmul(pu[64:128, TOKENS + 128 * tl:TOKENS + 128 * (tl + 1)],
                                                  src[:, tl, 128:WIDTH], ident[:, :], start=True, stop=True,
                                                  tile_position=(0, 64))
                        mm.then_inc(m_turned, 1)

                    def up(e, i):
                        n = e * HCH // 2 + i
                        if i == 0 and e < 2:
                            pe.wait_ge(mT_done, e + 1)
                        if n >= up_banks:
                            pe.wait_ge(gelu_done, n + 1 - up_banks)
                        bank = up_bank(n)
                        for m in range(2):
                            first = 128 * (2 * i + m)
                            out, hidden = bank[:, TOKENS * m:TOKENS * (m + 1)], slice(first, first + 128)
                            nc.tensor.matmul(out, w_up[:, e, hidden], fT[:, :], start=True, stop=False)
                            nc.tensor.matmul(out, w_up_stack[:, e, hidden], fT_high[:, :],
                                             start=False, stop=False)
                            mm = nc.tensor.matmul(out, w_up_stack[64:128, e, hidden], fT_parts[64:128, :],
                                                  start=False, stop=True)
                        mm.then_inc(up_done, 1)

                    def down(e, tl):
                        if tl == 0:
                            pe.wait_ge(gelu_done, HCH // 2 * (e + 1))
                            if e == 1:
                                pe.wait_ge(acc_done, 1)
                            if e >= 2:
                                pe.wait_ge(dn_used, e - 1)
                        for m in range(HCH):
                            mm = nc.tensor.matmul(pd[:, WIDTH * tl:WIDTH * (tl + 1)],
                                                  act[e % 2][:, m, 128 * tl:128 * (tl + 1)],
                                                  w_dn[:, e, m, :], start=(m == 0), stop=(m == HCH - 1))
                        mm.then_inc(dn_done, 1)

                    def logits():
                        pe.wait_ge(mT_done, 2)
                        for tl in range(TILES):
                            out, tokens = pd[:, EXPERTS * tl:EXPERTS * (tl + 1)], slice(128 * tl, 128 * (tl + 1))
                            nc.tensor.matmul(out, fT[:, tokens], w_gate[:, 0, :], start=True, stop=False)
                            mm = nc.tensor.matmul(out, fT_parts[:, tokens].bitcast(F32), w_gate[:, 1, :],
                                                  start=False, stop=True)
                        mm.then_inc(lg_done, 1)

                    def turn_gates():
                        pe.wait_ge(gate_done, 1)
                        for tl in range(TILES):
                            mm = nc.tensor.transpose(pd[0:EXPERTS, 128 * tl:128 * (tl + 1)],
                                                     gate[:, tl, :], ident[:, :])
                        mm.then_inc(gate_turned, 1)

                    def bias():
                        pe.wait_ge(gateT_done, 1)
                        for tl in range(TILES):
                            mm = nc.tensor.matmul(pd[:, WIDTH * tl:WIDTH * (tl + 1)],
                                                  gateT[:, 128 * tl:128 * (tl + 1)], b_ex[:, :],
                                                  start=True, stop=True)
                        mm.then_inc(gb_done, 1)

                    ffn = {"turn": ffn_turn, "up": up, "down": down, "logits": logits,
                           "turn_gates": turn_gates, "bias": bias}

                    def others(slot):
                        if run_s:
                            for name, *at in steps(SSM_STEPS, slot):
                                if name in ssm:
                                    ssm[name](*at)
                        if run_f:
                            for name, *at in steps(FFN_STEPS, slot):
                                if name in ffn:
                                    ffn[name](*at)
                        if run_s:
                            for g in steps(Y_SUMS, slot):
                                y_sum(g)

                    def attention(l):
                        causal = l == 0
                        if l == 1:
                            pe.wait_ge(h_done, 1)
                        turn(pm, ps[:, 3, :], h_tok).then_inc(h_turned[l], 1)
                        others((l, "turned"))
                        pe.wait_ge(hT_done[l], 2)
                        for c in range(2):
                            for part in range(2):
                                first = WIDTH * part + CGROUP * c
                                chunks(ps[0:CGROUP, 2 * c + part, 0:TOKENS],
                                       lambda ch, cn: w_qkv[l][0:cn, ch, first:first + CGROUP],
                                       lambda ch, cn: hT[0:cn, ch, :]).then_inc(qk_done[l], 1)
                        for tl in range(TILES):
                            mm = chunks(pm[:, WIDTH * tl:WIDTH * (tl + 1)],
                                        lambda c, cn: hT[0:cn, c, 128 * tl:128 * (tl + 1)],
                                        lambda c, cn: w_qkv[l][0:cn, c, 2 * WIDTH:3 * WIDTH])
                        mm.then_inc(v_done[l], 1)

                        def stack(u):
                            pe.wait_ge(low_done[l], 4 if u >= 2 else 2)
                            if u >= 4:
                                pe.wait_ge((stack_even, stack_odd)[u % 2][l], 1)
                            channels = slice(32 * (u % 3), 32 * (u % 3) + 32)
                            for part in range(2):
                                for level, source in ((0, high[part]), (1, low[part])):
                                    mm = nc.tensor.matmul(ps[:, u % 4, TOKENS * part:TOKENS * (part + 1)],
                                                          to_stack[channels, part, level, :],
                                                          source[u // 3][channels, :],
                                                          start=(level == 0), stop=(level == 1))
                            mm.then_inc(stack_psum[l], 1)

                        for u in range(4):
                            stack(u)
                        others((l, "projected"))
                        for u in (4, 5):
                            stack(u)

                        def scores(u):
                            if u == 0:
                                pe.wait_ge(stack_even[l], 3)
                                pe.wait_ge(stack_odd[l], 3)
                                pe.wait_ge(v_copied[l], 1)
                            if u >= 2:
                                pe.wait_ge(p_done[l], u - 1)
                            for j in range(2):
                                rows = slice(64 * j, 64 * j + TOP_ROW)
                                b = ps[:, 2 * (u % 2) + j, :]
                                for i in range(TILES):
                                    keys = 128 * (i + 1) if causal else TOKENS
                                    mm = nc.tensor.matmul(b[:, TOKENS * i:TOKENS * i + keys],
                                                          q_stack[rows, u, 128 * i:128 * (i + 1)],
                                                          k_stack[rows, u, 0:keys],
                                                          start=(i == 0), stop=not causal,
                                                          skip_group_check=True)
                            if causal:
                                for j in range(2):
                                    for i in range(TILES):
                                        at = TOKENS * i + 128 * i
                                        mm = nc.tensor.matmul(ps[:, 2 * (u % 2) + j, at:at + 128],
                                                              identb[:, :], maskq[:, :], start=False,
                                                              stop=True, skip_group_check=True)
                            mm.then_inc(s_done[l], 1)

                        def row_max(u):
                            pe.wait_ge(top_done[l], u + 1)
                            for i in range(TILES):
                                mm = nc.tensor.transpose(ps[:, 2 * (u % 2), 128 * i:128 * (i + 1)],
                                                         top[:, u % 2, i, :].bitcast(F32), ident[:, :])
                            mm.then_inc(top_turned[l], 1)

                        def shifted(u):
                            pe.wait_ge(q_shifted[l], u + 1)
                            for j in range(2):
                                rows = slice(64 * j, 64 * j + TOP_ROW + 1)
                                b = ps[:, 2 * (u % 2) + j, :]
                                for i in range(TILES):
                                    q0 = 128 * i if causal else 0
                                    mm = nc.tensor.matmul(b[:, TOKENS * i + q0:TOKENS * (i + 1)],
                                                          k_stack[rows, u, 128 * i:128 * (i + 1)],
                                                          q_stack[rows, u, q0:TOKENS],
                                                          start=(i == 0), stop=not causal,
                                                          skip_group_check=True)
                            if causal:
                                for j in range(2):
                                    for i in range(TILES):
                                        at = TOKENS * i + 128 * i
                                        mm = nc.tensor.matmul(ps[:, 2 * (u % 2) + j, at:at + 128],
                                                              identb[:, :], maskk[:, :], start=False,
                                                              stop=True, skip_group_check=True)
                            mm.then_inc(st_done[l], 1)

                        def context(u):
                            pe.wait_ge(p_done[l], u + 1)
                            if u in (2, 4):
                                pe.wait_ge(den_inv[l], u // 2)
                            for j in range(2):
                                head = 2 * u + j
                                row = 32 * (head % QUAD)
                                for kt in range(TILES):
                                    q0 = 128 * kt if causal else 0
                                    mm = nc.tensor.matmul(pm[row:row + 32, q0:TOKENS], v_aug[:, kt, head, :],
                                                          probs[u % 2][:, j, kt, q0:TOKENS],
                                                          start=(kt == 0), stop=(kt == TILES - 1),
                                                          tile_position=(0, row), skip_group_check=True)
                            mm.then_inc(av_done[l], 1)

                        def spread(ht):
                            pe.wait_ge(ctx_copied[l], ht + 1)
                            nc.tensor.matmul(pm[:, TOKENS:2 * TOKENS],
                                             den_sel[:, :, :].rearrange("p j i -> p (j i)"), cT[:, ht, :],
                                             start=True, stop=True).then_inc(den_done[l], 1)

                        scores(0)
                        for u in range(UNITS):
                            if u + 1 < UNITS:
                                scores(u + 1)
                            row_max(u)
                            if u >= 1:
                                context(u - 1)
                            others((l, 2 * u))
                            shifted(u)
                            if u in (2, 4):
                                spread(u // 2 - 1)
                            others((l, 2 * u + 1))
                        context(UNITS - 1)
                        others((l, "context"))
                        spread(HTILES - 1)
                        others((l, "spread"))
                        pe.wait_ge(ctx_done[l], HTILES)
                        for tl in range(TILES):
                            for ht in range(HTILES):
                                mm = nc.tensor.matmul(ps[:, 2, WIDTH * tl:WIDTH * (tl + 1)],
                                                      cT[:, ht, 128 * tl:128 * (tl + 1)], w_o[l][:, ht, :],
                                                      start=(ht == 0), stop=(ht == HTILES - 1))
                        mm.then_inc(proj_done[l], 1)
                        others((l, "output"))

                    if run_a or run_f:
                        pe.wait_ge(w_b, 16 * len(b_loads))
                    if run_a:
                        attention(0)
                        attention(1)
                    else:
                        for slot in SLOTS:
                            others(slot)

                @block.vector
                def _(dve):
                    link = chained(dve, dve_chain)

                    def norm_stats(i, src):
                        for tl in range(TILES):
                            ins = nc.vector.bn_stats(norm_raw[:, i, tl, :], src(tl))
                        link(ins)
                        for tl in range(TILES):
                            ins = nc.vector.bn_aggr(norm_mv[:, i, tl, :], norm_raw[:, i, tl, :])
                        link(ins)
                        nc.vector.tensor_scalar(norm_var[:, i, :], norm_mv[:, i, :, 1], EPS, None,
                                                ALU.add).then_inc(var_done[i], 1)

                    def norm_apply(i, src, dst):
                        dve.wait_ge(rstd_done[i], 1)
                        link(nc.vector.scalar_tensor_tensor(
                            out=norm_shift[:, i, :], in0=norm_mv[:, i, :, 0], scalar=-1.0,
                            in1=norm_rstd[:, i, :], op0=ALU.mult, op1=ALU.mult))
                        for tl in range(TILES):
                            ins = nc.vector.tensor_scalar(dst(tl), src(tl), norm_rstd[:, i, tl:tl + 1],
                                                          norm_shift[:, i, tl:tl + 1], ALU.mult, ALU.add)
                        return ins

                    def norm(i, src, dst):
                        norm_stats(i, src)
                        return norm_apply(i, src, dst)

                    def x_turn():
                        dve.wait_ge(x_turned, 1)
                        for c, (_, cn) in enumerate(CH):
                            ins = nc.vector.tensor_copy(xgT[0:cn, c, :], py[0:cn, TOKENS * c:TOKENS * (c + 1)])
                        link(ins)
                        for c, (_, cn) in enumerate(CH):
                            ins = nc.vector.bn_stats(gn_raw[0:cn, c, :], xgT[0:cn, c, :])
                        link(ins)
                        for c, (_, cn) in enumerate(CH):
                            ins = nc.vector.bn_aggr(gn_mv[0:cn, c, :], gn_raw[0:cn, c, :])
                        link(ins)
                        link(nc.vector.tensor_tensor(gn_sq[:, :], gn_mv[:, :, 0], gn_mv[:, :, 0], ALU.mult))
                        nc.vector.tensor_tensor(gn_mv[:, :, 1], gn_mv[:, :, 1], gn_sq[:, :],
                                                ALU.add).then_inc(gn_stats, 1)

                    def group_sums():
                        dve.wait_ge(gn_sums, 1)
                        for c, (_, cn) in enumerate(CH):
                            ins = nc.vector.tensor_copy(gn_m[0:cn, c, :], py[0:cn, 2 * c:2 * c + 2])
                        link(ins)
                        link(nc.vector.tensor_tensor(gn_sq[:, :], gn_m[:, :, 0], gn_m[:, :, 0], ALU.mult))
                        link(nc.vector.tensor_tensor(gn_var[:, :], gn_m[:, :, 1], gn_sq[:, :], ALU.subtract))
                        nc.vector.tensor_scalar(gn_var[:, :], gn_var[:, :], 0.0, EPS,
                                                ALU.max, ALU.add).then_inc(gn_v, 1)
                        dve.wait_ge(gn_r, 1)
                        link(nc.vector.scalar_tensor_tensor(
                            out=gn_shift[:, :], in0=gn_m[:, :, 0], scalar=-1.0, in1=gn_rstd[:, :],
                            op0=ALU.mult, op1=ALU.mult))
                        for c, (_, cn) in enumerate(CH):
                            nc.vector.tensor_scalar(xgT[0:cn, c, :], xgT[0:cn, c, :], gn_rstd[0:cn, c:c + 1],
                                                    gn_shift[0:cn, c:c + 1], ALU.mult,
                                                    ALU.add).then_inc(xg_done, 1)
                        if opening:
                            dve.wait_ge(w_a, 16 * len(a_loads))
                            nc.vector.tensor_reduce(dsum[:, :], ds_in[:, :], AX.X, ALU.add)
                            nc.vector.tensor_scalar(a_log[:, :], a_log[:, :], A_LOG_MAX, None,
                                                    ALU.min).then_inc(rates, 1)
                            dve.wait_ge(rates, 1)
                            nc.vector.tensor_scalar(ddiag[:, :], ident[0:INNER, 0:INNER], dsum[:, 0:1], None,
                                                    ALU.mult).then_inc(rates, 1)

                    def in_proj():
                        dve.wait_ge(xh_done, 1)
                        nc.vector.tensor_copy(z_gate[:, :, :], py[:, TOKENS:TOKENS + TILES * INNER]
                                              .rearrange("p (t c) -> p t c", t=TILES)).then_inc(z_copied, 1)
                        link(nc.vector.tensor_copy(pad[:, 1:SIDE + 1, 1:SIDE + 1],
                                                   py[0:INNER, 0:TOKENS].rearrange("p (h w) -> p h w",
                                                                                   w=SIDE)))
                        conv2 = conv.rearrange("p (h w) -> p h w", w=SIDE)
                        for tap in range(9):
                            window = pad[:, tap // 3:tap // 3 + SIDE, tap % 3:tap % 3 + SIDE]
                            if tap == 0:
                                ins = nc.vector.tensor_scalar(conv2, window, w_conv[:, 0:1], b_conv[:, 0:1],
                                                              ALU.mult, ALU.add)
                            else:
                                ins = nc.vector.scalar_tensor_tensor(
                                    out=conv2, in0=window, scalar=w_conv[:, tap:tap + 1], in1=conv2,
                                    op0=ALU.mult, op1=ALU.add)
                            if tap < 8:
                                link(ins)
                        ins.then_inc(conv_done, 1)

                    def silu():
                        dve.wait_ge(silu_e, 2)
                        link(nc.vector.tensor_scalar(conv_e, conv_e, 1.0, None, ALU.add))
                        link(nc.vector.reciprocal(conv_e, conv_e))
                        nc.vector.tensor_tensor(xs[:, 0, :], conv, conv_e, ALU.mult).then_inc(u_done, 1)
                        link(nc.vector.tensor_scalar(z_e, z_e, 1.0, None, ALU.add))
                        link(nc.vector.reciprocal(z_e, z_e))
                        link(nc.vector.tensor_tensor(z_gate[:, :, :], z_gate[:, :, :], z_e, ALU.mult))

                    def x_dbl(half_paths):
                        if opening and half_paths == 0:
                            dve.wait_ge(rates_e, 1)
                            nc.vector.tensor_scalar(a_neg[:, :], a_neg[:, :], -1.0, None,
                                                    ALU.mult).then_inc(rates, 1)
                        if half_paths == 0:
                            dve.wait_ge(xd_done, 1)
                            nc.vector.tensor_copy(xdbl[:, 0:2, :], py[0:RANK + 2 * STATE, :]
                                                  .rearrange("p (k l) -> p k l", k=2)).then_inc(xd_copied, 1)

                    def dt(half_paths):
                        dve.wait_ge(dt_done, half_paths + 1)
                        for o in range(2):
                            k = 2 * half_paths + o
                            ins = nc.vector.tensor_scalar(delta[:, k, :],
                                                          py[0:INNER, TOKENS * o:TOKENS * (o + 1)],
                                                          b_dt[:, k:k + 1], None, ALU.add)
                        ins.then_inc(dt_sum, 1)

                    def softplus(half_paths):
                        dve.wait_ge(sp_a, half_paths + 1)
                        ks = slice(2 * half_paths, 2 * half_paths + 2)
                        one_e, e, d = d_rows[0][0:INNER, ks, :], delta_x[:, ks, :], delta[:, ks, :]
                        nc.vector.tensor_scalar(one_e, e, 1.0, None, ALU.add).then_inc(sp_u, 1)
                        dve.wait_ge(sp_u, half_paths + 1)
                        link(nc.vector.scalar_tensor_tensor(out=e, in0=one_e, scalar=1.0, in1=e,
                                                            op0=ALU.subtract, op1=ALU.subtract))
                        link(nc.vector.scalar_tensor_tensor(out=d, in0=d, scalar=0.0, in1=e,
                                                            op0=ALU.max, op1=ALU.subtract))

                    def softplus_log():
                        dve.wait_ge(sp_l, 1)
                        nc.vector.tensor_tensor(flat(delta), flat(delta),
                                                d_rows[1][0:INNER, :, :].rearrange("p k l -> p (k l)"),
                                                ALU.add).then_inc(d_done, 1)
                        dve.wait_ge(d_done, 1)
                        dve.wait_ge(xs_done, 1)
                        nc.vector.tensor_tensor(
                            delta_x[:, :, :].rearrange("p (d o) l -> p d (o l)", d=2),
                            delta[:, :, :].rearrange("p (d o) l -> p d (o l)", d=2),
                            xs[:, :, :].rearrange("p o l -> p (o l)").unsqueeze(1)
                            .to_broadcast([INNER, 2, 2 * TOKENS]), ALU.mult).then_inc(dx_done, 1)

                    def scan(g):
                        dve.wait_ge(dx_in[g % 2], 16 * (g // 2 + 1))
                        if g == 0:
                            dve.wait_ge(bc_in, 16 * 2 * PACK)
                        link(nc.vector.tensor_tensor(dx_rows[g % 2][:, :], dx_rows[g % 2][:, :],
                                                     B_rows[:, :], ALU.mult))
                        dve.wait_ge(decay_done, g + 1)
                        if g >= held:
                            dve.wait_ge(y_part, g - held + 1)
                        for both in (slice(0, 2 * TOKENS), slice(4 * TOKENS - 1, 2 * TOKENS - 1, -1)):
                            ins = nc.vector.tensor_tensor_scan(
                                flat(states[g % held])[:, both], flat(decay[g % 2])[:, both],
                                dx_rows[g % 2][:, both], 0.0, ALU.mult, ALU.add)
                        ins.then_inc(scan_done, 1)

                    def y_copy():
                        dve.wait_ge(y_part, GROUPS)
                        nc.vector.tensor_copy(yT, py[0:INNER, 0:TOKENS]).then_inc(yT_done, 1)

                    def y_norm():
                        dve.wait_ge(y_back, 1)
                        link(norm(0, lambda tl: py[:, INNER * tl:INNER * (tl + 1)],
                                  lambda tl: y_g[:, tl, :]))
                        link(nc.vector.tensor_tensor(y_g, y_g, rows(on_g), ALU.mult))
                        link(nc.vector.tensor_tensor(y_g, y_g, rows(on_b), ALU.add))
                        nc.vector.tensor_tensor(y_g, y_g, z_gate[:, :, :],
                                                ALU.mult).then_inc(yg_done, 1)

                    def y_turn():
                        dve.wait_ge(y_turned, 1)
                        nc.vector.tensor_copy(yT, py[0:INNER, 0:TOKENS]).then_inc(yT_done, 1)

                    def y_out():
                        dve.wait_ge(o_done, 1)
                        link(nc.vector.tensor_tensor(x1[:, :, :], two_tiles(py), x_tok[:, :, :], ALU.add))
                        norm(1, lambda tl: x1[:, tl, :], lambda tl: h_tok[:, tl, :])

                    ssm = {"x_turn": x_turn, "group_sums": group_sums, "in_proj": in_proj, "silu": silu,
                           "x_dbl": x_dbl, "dt": dt, "softplus": softplus,
                           "softplus_log": softplus_log, "y_copy": y_copy, "y_norm": y_norm,
                           "y_turn": y_turn, "y_out": y_out}

                    def ffn_turn(i):
                        dve.wait_ge(m_turned, i + 1)
                        link(nc.vector.tensor_copy(fT_high[:, :], pu[:, TOKENS:2 * TOKENS]))
                        nc.vector.tensor_copy(fT[:, :], pu[:, 0:TOKENS])
                        if i == 1:
                            nc.vector.tensor_copy(fT_parts[0:64, :], pu[0:64, TOKENS:2 * TOKENS])
                        nc.vector.tensor_tensor(fT_parts[64:128, :], pu[64:128, TOKENS:2 * TOKENS],
                                                fT_high[64:128, :].bitcast(F32),
                                                ALU.subtract).then_inc(mT_done, 1)

                    def ffn_norm(part):
                        if part == 1:
                            link(norm_apply(4, lambda tl: v3[:, tl, :], lambda tl: f_tok[:, tl, :]))
                            link(nc.vector.tensor_tensor(f_tok[:, :, :], f_tok[:, :, :], rows(f_g), ALU.mult))
                            nc.vector.tensor_tensor(f_tok[:, :, :], f_tok[:, :, :], rows(f_b),
                                                    ALU.add).then_inc(xm_done, 1)
                            return
                        dve.wait_ge(dn_done, TILES)
                        dve.wait_ge(mres_done, 1)
                        nc.vector.tensor_tensor(v3[:, :, :], two_tiles(pd), v2[:, :, :],
                                                ALU.add).then_inc(v3_done, 1)
                        dve.wait_ge(v3_done, 1)
                        norm_stats(4, lambda tl: v3[:, tl, :])

                    def logits():
                        dve.wait_ge(lg_done, 1)
                        link(nc.vector.tensor_tensor(
                            logit[:, :, :], pd[:, 0:TILES * EXPERTS].rearrange("p (t e) -> p t e", t=TILES),
                            rows(b_gate), ALU.add))
                        for tl in range(TILES):
                            other = logit[:, tl, :].unsqueeze(1).to_broadcast([128, EXPERTS, EXPERTS])
                            own = logit[:, tl, :].unsqueeze(2).to_broadcast([128, EXPERTS, EXPERTS])
                            nc.vector.tensor_tensor(beats[:, tl, :, :], other, own, ALU.is_gt)
                            ins = nc.vector.tensor_tensor(ties[:, tl, :, :], other, own, ALU.is_equal)
                        nc.vector.tensor_reduce(best[:, :], logit[:, :, :], AX.X, ALU.max)
                        link(ins)
                        for tl in range(TILES):
                            ins = nc.vector.tensor_tensor(ties[:, tl, :, :], ties[:, tl, :, :],
                                                          lower[:, :, :], ALU.mult)
                        link(ins)
                        nc.vector.tensor_tensor(gate[:, :, :], logit[:, :, :],
                                                best[:, :].unsqueeze(2).to_broadcast([128, TILES, EXPERTS]),
                                                ALU.subtract).then_inc(lg_shift, 1)
                        link(nc.vector.tensor_tensor(beats[:, :, :, :], beats[:, :, :, :], ties[:, :, :, :],
                                                     ALU.add))
                        link(nc.vector.tensor_reduce(rank[:, :, :], beats[:, :, :, :], AX.X, ALU.add))
                        dve.wait_ge(gate_e, 1)
                        link(nc.vector.scalar_tensor_tensor(
                            out=gate[:, :, :], in0=rank[:, :, :], scalar=TOPK - 0.5, in1=gate[:, :, :],
                            op0=ALU.is_lt, op1=ALU.mult))
                        link(nc.vector.tensor_reduce(gsumr[:, :], gate[:, :, :], AX.X, ALU.add))
                        link(nc.vector.reciprocal(gsumr[:, :], gsumr[:, :]))
                        nc.vector.tensor_tensor(gate[:, :, :], gate[:, :, :],
                                                gsumr[:, :].unsqueeze(2).to_broadcast([128, TILES, EXPERTS]),
                                                ALU.mult).then_inc(gate_done, 1)

                    def turn_gates():
                        dve.wait_ge(gate_turned, 1)
                        nc.vector.tensor_copy(gateT[:, :], pd[0:EXPERTS, 0:TOKENS]).then_inc(gateT_done, 1)

                    def bias():
                        dve.wait_ge(gb_done, 1)
                        dve.wait_ge(base_done, 1)
                        nc.vector.tensor_tensor(out_tok[:, :, :], two_tiles(pd), out_tok[:, :, :],
                                                ALU.add).then_inc(acc_done, 1)

                    def add(e):
                        dve.wait_ge(dn_done, TILES * (e + 1))
                        if e == 1:
                            dve.wait_ge(acc_done, 1)
                            dve.wait_ge(gate_done, 1)
                        else:
                            dve.wait_ge(dn_used, e - 1)
                        for i in range(TILES):
                            ins = nc.vector.scalar_tensor_tensor(
                                out=out_tok[:, i, :], in0=pd[:, WIDTH * i:WIDTH * (i + 1)],
                                scalar=gate[:, i, e - 1:e], in1=out_tok[:, i, :],
                                op0=ALU.mult, op1=ALU.add)
                            if e == EXPERTS:
                                ins.then_inc(out_done, 1)
                        if e < EXPERTS:
                            ins.then_inc(dn_used, 1)

                    ffn = {"turn": ffn_turn, "norm": ffn_norm, "logits": logits, "turn_gates": turn_gates,
                           "bias": bias, "add": add}

                    def others(slot):
                        if run_s:
                            for name, *at in steps(SSM_STEPS, slot):
                                ssm[name](*at)
                            for g in steps(SCANS, slot):
                                scan(g)
                        if run_f:
                            for name, *at in steps(FFN_STEPS, slot):
                                if name in ffn:
                                    ffn[name](*at)

                    def attention(l):
                        causal = l == 0
                        dve.wait_ge(h_turned[l], 1)
                        if l == 0:
                            ins = nc.vector.tensor_copy(hT[:, 0, :], pm[:, 0:TOKENS])
                        else:
                            ins = nc.vector.tensor_scalar(hT[:, 0, :], pm[:, 0:TOKENS], h_g[:, 0:1], h_b[:, 0:1],
                                                          ALU.mult, ALU.add)
                        ins.then_inc(hT_done[l], 1)
                        others((l, "turned"))
                        for c in range(2):
                            for part in range(2):
                                n = 2 * c + part
                                dve.wait_ge(high_done[l], n + 1)
                                nc.vector.scalar_tensor_tensor(
                                    out=low[part][c], in0=ps[0:CGROUP, n, 0:TOKENS],
                                    scalar=b_qk[l][:, part, c:c + 1], in1=high[part][c].bitcast(F32),
                                    op0=ALU.add, op1=ALU.subtract).then_inc(low_done[l], 1)
                        dve.wait_ge(v_done[l], 1)
                        nc.vector.tensor_tensor(
                            v_aug[:, :, :, 0:HEAD],
                            pm[:, 0:TILES * WIDTH].rearrange("p (t h d) -> p t h d", t=TILES, d=HEAD),
                            b_v[l][:, :].rearrange("p (h d) -> p h d", d=HEAD).unsqueeze(1)
                            .to_broadcast([128, TILES, HEADS, HEAD]), ALU.add).then_inc(v_copied[l], 1)

                        def copy_stack(u):
                            dve.wait_ge(stack_psum[l], u + 1)
                            nc.vector.tensor_copy(q_stack[:, u, :], ps[:, u % 4, 0:TOKENS])
                            nc.vector.tensor_scalar(k_stack[:, u, :], ps[:, u % 4, TOKENS:2 * TOKENS],
                                                    top_one[:, :], None, ALU.add).then_inc(stack_odd[l], 1)

                        copy_stack(1)
                        copy_stack(3)

                        def row_max(u):
                            dve.wait_ge(s_done[l], u + 1)
                            par = u % 2
                            pair = ps[:, 2 * par:2 * par + 2, :]
                            if causal:
                                for i in range(TILES):
                                    ins = nc.vector.tensor_reduce(
                                        top[:, par, i, TOP_ROW::64],
                                        pair[:, :, TOKENS * i:TOKENS * i + 128 * (i + 1)],
                                        AX.X, ALU.max, negate=True)
                            else:
                                ins = nc.vector.tensor_reduce(
                                    top[:, par, :, TOP_ROW::64],
                                    pair.rearrange("p j (i k) -> p i j k", i=TILES),
                                    AX.X, ALU.max, negate=True)
                            ins.then_inc(top_done[l], 1)

                        def shift(u):
                            dve.wait_ge(top_turned[l], u + 1)
                            nc.vector.tensor_tensor(q_stack[:, u, :], q_stack[:, u, :].bitcast(F32),
                                                    ps[:, 2 * (u % 2), 0:TOKENS],
                                                    ALU.add).then_inc(q_shifted[l], 1)

                        def context_copy(ht):
                            dve.wait_ge(av_done[l], 2 * ht + 2)
                            nc.vector.tensor_copy(cT[:, ht, :], pm[:, 0:TOKENS]).then_inc(ctx_copied[l], 1)

                        def invert_sums(ht):
                            dve.wait_ge(den_done[l], ht + 1)
                            if ht:
                                dve.wait_ge(ctx_done[l], ht)
                            nc.vector.reciprocal(inv_den[:, :],
                                                 pm[:, TOKENS:2 * TOKENS]).then_inc(den_inv[l], 1)

                        others((l, "projected"))
                        copy_stack(5)
                        row_max(0)
                        for u in range(UNITS):
                            shift(u)
                            if u in (2, 4):
                                context_copy(u // 2 - 1)
                            others((l, 2 * u))
                            if u + 1 < UNITS:
                                row_max(u + 1)
                            if u in (2, 4):
                                invert_sums(u // 2 - 1)
                            others((l, 2 * u + 1))
                        context_copy(HTILES - 1)
                        others((l, "context"))
                        invert_sums(HTILES - 1)
                        others((l, "spread"))
                        dve.wait_ge(proj_done[l], 1)
                        dve.wait_ge(res_done[l], 1)
                        if l == 0:
                            if run_f:
                                dve.wait_ge(x2_kept, 1)
                            link(nc.vector.tensor_tensor(x2[:, :, :], two_tiles(ps[:, 2, :]), x1[:, :, :],
                                                         ALU.add))
                            link(norm(2, lambda tl: x2[:, tl, :], lambda tl: v_tok[:, tl, :]))
                            norm(3, lambda tl: v_tok[:, tl, :], lambda tl: h_tok[:, tl, :]).then_inc(h_done, 1)
                        else:
                            nc.vector.tensor_tensor(v2[:, :, :], two_tiles(ps[:, 2, :]), v_tok[:, :, :],
                                                    ALU.add)
                        others((l, "output"))

                    if run_a or run_f:
                        dve.wait_ge(w_b, 16 * len(b_loads))
                    if run_a:
                        attention(0)
                        attention(1)
                    else:
                        for slot in SLOTS:
                            others(slot)

                @block.scalar
                def _(sc):
                    link = chained(sc, act_chain)

                    def in_proj():
                        if opening:
                            sc.wait_ge(rates, 1)
                            nc.scalar.activation(a_neg[:, :], a_log[:, :], ACT.Exp).then_inc(rates_e, 1)
                        sc.wait_ge(z_copied, 1)
                        nc.scalar.activation(z_e, z_gate[:, :, :], ACT.Exp, scale=-1.0).then_inc(silu_e, 1)
                        sc.wait_ge(conv_done, 1)
                        nc.scalar.activation(conv_e, conv, ACT.Exp, scale=-1.0).then_inc(silu_e, 1)

                    def x_dbl(half_paths):
                        if half_paths == 1:
                            sc.wait_ge(xd_done, 2)
                            nc.scalar.activation(xdbl[:, 2:4, :], py[0:RANK + 2 * STATE, :]
                                                 .rearrange("p (k l) -> p k l", k=2),
                                                 ACT.Copy).then_inc(xd_copied, 1)

                    def softplus(half_paths):
                        ks = slice(2 * half_paths, 2 * half_paths + 2)
                        sc.wait_ge(dt_sum, half_paths + 1)
                        link(nc.scalar.activation(delta_x[:, ks, :], delta[:, ks, :], ACT.Abs))
                        nc.scalar.activation(delta_x[:, ks, :], delta_x[:, ks, :], ACT.Exp,
                                             scale=-1.0).then_inc(sp_a, 1)

                    def softplus_log():
                        sc.wait_ge(sp_u, 2)
                        nc.scalar.activation(d_rows[1][0:INNER, :, :], d_rows[0][0:INNER, :, :],
                                             ACT.Ln).then_inc(sp_l, 1)

                    def decays(g):
                        if opening and g == 0:
                            sc.wait_ge(rates, 3)
                        sc.wait_ge(d_in[g % 2], 16 * (g // 2 + 1))
                        if g >= 2:
                            sc.wait_ge(scan_done, g - 1)
                        for k in range(PATHS):
                            at = g * PATHS + k
                            rest = slice(1, TOKENS) if k < 2 else slice(0, TOKENS - 1)
                            ins = nc.scalar.activation(decay[g % 2][:, k, rest], d_rows[g % 2][:, k, rest],
                                                       ACT.Exp, scale=a_neg[:, at:at + 1])
                        ins.then_inc(decay_done, 1)

                    ssm = {"in_proj": in_proj, "x_dbl": x_dbl, "softplus": softplus,
                           "softplus_log": softplus_log}

                    def up(e, i):
                        sc.wait_ge(up_done, e * HCH // 2 + i + 1)
                        if i == 0 and e >= 2:
                            sc.wait_ge(dn_done, TILES * (e - 1))
                        for m in range(2):
                            ins = nc.scalar.activation(act[e % 2][:, 2 * i + m, :],
                                                       up_bank(e * HCH // 2 + i)[:, TOKENS * m:TOKENS * (m + 1)],
                                                       ACT.Gelu,
                                                       bias=b_up[:, e, 2 * i + m:2 * i + m + 1])
                        ins.then_inc(gelu_done, 1)

                    def logits():
                        sc.wait_ge(lg_shift, 1)
                        nc.scalar.activation(gate[:, :, :], gate[:, :, :], ACT.Exp).then_inc(gate_e, 1)

                    ffn = {"up": up, "logits": logits}

                    def others(slot):
                        if run_s:
                            for name, *at in steps(SSM_STEPS, slot):
                                if name in ssm:
                                    ssm[name](*at)
                        if run_f:
                            for name, *at in steps(FFN_STEPS, slot):
                                if name in ffn:
                                    ffn[name](*at)
                        if run_s:
                            for g in steps(DECAYS, slot):
                                decays(g)

                    def attention(l):
                        causal = l == 0
                        sc.wait_ge(h_turned[l], 1)
                        if l == 0:
                            ins = nc.scalar.activation(hT[0:64, 1, :], ps[0:64, 3, 0:TOKENS], ACT.Copy)
                        else:
                            ins = nc.scalar.activation(hT[0:64, 1, :], ps[0:64, 3, 0:TOKENS], ACT.Identity,
                                                       scale=h_g[0:64, 1:2], bias=h_b[0:64, 1:2])
                        ins.then_inc(hT_done[l], 1)
                        others((l, "turned"))
                        for c in range(2):
                            for part in range(2):
                                n = 2 * c + part
                                sc.wait_ge(qk_done[l], n + 1)
                                nc.scalar.activation(high[part][c], ps[0:CGROUP, n, 0:TOKENS],
                                                     ACT.Identity, bias=b_qk[l][:, part, c:c + 1]
                                                     ).then_inc(high_done[l], 1)

                        def copy_stack(u):
                            sc.wait_ge(stack_psum[l], UNITS if u == 4 else u + 1)
                            nc.scalar.activation(q_stack[:, u, :], ps[:, u % 4, 0:TOKENS], ACT.Copy)
                            nc.scalar.activation(k_stack[:, u, :], ps[:, u % 4, TOKENS:2 * TOKENS], ACT.Identity,
                                                 bias=top_one[:, :]).then_inc(stack_even[l], 1)

                        copy_stack(0)
                        copy_stack(2)
                        others((l, "projected"))
                        copy_stack(4)
                        for u in range(UNITS):
                            others((l, 2 * u))
                            sc.wait_ge(st_done[l], u + 1)
                            if u >= 2:
                                sc.wait_ge(av_done[l], u - 1)
                            pair = ps[:, 2 * (u % 2):2 * (u % 2) + 2, :]
                            if causal:
                                for kt in range(TILES):
                                    ins = nc.scalar.activation(
                                        probs[u % 2][:, :, kt, 128 * kt:TOKENS],
                                        pair[:, :, TOKENS * kt + 128 * kt:TOKENS * (kt + 1)], ACT.Exp,
                                        scale=HEAD ** -0.5)
                            else:
                                ins = nc.scalar.activation(
                                    probs[u % 2][:, :, :, :].rearrange("p j t q -> p j (t q)"), pair, ACT.Exp,
                                    scale=HEAD ** -0.5)
                            ins.then_inc(p_done[l], 1)
                            others((l, 2 * u + 1))
                        others((l, "context"))
                        others((l, "spread"))
                        others((l, "output"))

                    if run_a or run_f:
                        sc.wait_ge(w_b, 16 * len(b_loads))
                    if split_w_up:
                        for e, n0, buf in up_raw:
                            nc.scalar.activation(w_up_stack[:, e, n0:n0 + buf.shape[1]], buf,
                                                 ACT.Copy).then_inc(up_high, 1)
                    if run_a:
                        attention(0)
                        attention(1)
                    else:
                        for slot in SLOTS:
                            others(slot)

                @block.gpsimd
                def _(pool):
                    if opening:
                        link = chained(pool, pool_set, 2)
                        scan_constants(pool, link)

                    def rstd(i):
                        pool.wait_ge(var_done[i], 1)
                        nc.gpsimd.tensor_tensor(norm_rstd[:, i, :], norm_var[:, i, :], half[:, :],
                                                ALU.pow).then_inc(rstd_done[i], 1)

                    def group_sums():
                        pool.wait_ge(gn_v, 1)
                        nc.gpsimd.tensor_tensor(gn_rstd[:, :], gn_var[:, :], half[:, :],
                                                ALU.pow).then_inc(gn_r, 1)
                        if opening:
                            attention_constants(link)

                    def silu():
                        pool.wait_ge(u_done, 1)
                        nc.gpsimd.tensor_copy(xs[:, 1, :].rearrange("p (w h) -> p w h", h=SIDE),
                                              xs[:, 0, :].rearrange("p (h w) -> p w h", w=SIDE)
                                              ).then_inc(xs_done, 1)

                    def times_C(g):
                        pool.wait_ge(scan_done, g + 1)
                        if g == 0:
                            pool.wait_ge(bc_in, 16 * 2 * PACK)
                        C_path = C_rows[:, :].rearrange("p (k l) -> p k l", k=PATHS)
                        now, now_by_row = states[g % held], states_by_row[g % held]
                        nc.gpsimd.tensor_tensor(now[:, 0::2, :], now[:, 0::2, :], C_path[:, 0::2, :], ALU.mult)
                        nc.gpsimd.tensor_tensor(
                            now_by_row.rearrange("p k (h w) -> p k w h", w=SIDE),
                            now[:, 1::2, :].rearrange("p k (w h) -> p k w h", h=SIDE),
                            C_path[:, 1::2, :].rearrange("p k (w h) -> p k w h", h=SIDE),
                            ALU.mult).then_inc(c_done if add_paths else sc_done, 1)
                        if not add_paths:
                            return
                        pool.wait_ge(c_done, g + 1)
                        nc.gpsimd.tensor_tensor(now[:, 0, :], now[:, 0, :], now[:, 2, :], ALU.add)
                        nc.gpsimd.tensor_tensor(now_by_row[:, 0, :], now_by_row[:, 0, :], now_by_row[:, 1, :],
                                                ALU.add).then_inc(sc_done, 1)

                    ssm = {"group_sums": group_sums, "silu": silu,
                           "y_norm": lambda: rstd(0), "y_out": lambda: rstd(1)}

                    def ffn_norm(part):
                        if part == 1:
                            return
                        rstd(4)
                        pool.wait_ge(v3_done, 1)
                        pool.wait_ge(x2_kept, 1)
                        nc.gpsimd.tensor_tensor(out_tok[:, :, :], out_tok[:, :, :], v3[:, :, :],
                                                ALU.add).then_inc(base_done, 1)

                    def ffn_turn(i):
                        if i == 0:
                            pool.wait_ge(m_turned, 1)
                            nc.gpsimd.tensor_tensor(v2[:, :, :], v2[:, :, :], rows(b_dn),
                                                    ALU.add).then_inc(mres_done, 1)

                    ffn = {"turn": ffn_turn, "norm": ffn_norm}

                    def others(slot):
                        if run_s:
                            for name, *at in steps(SSM_STEPS, slot):
                                if name in ssm:
                                    ssm[name](*at)
                        if run_f:
                            for name, *at in steps(FFN_STEPS, slot):
                                if name in ffn:
                                    ffn[name](*at)
                        if run_s:
                            for g in steps(SCANS, slot):
                                times_C(g)

                    if run_a or run_f:
                        pool.wait_ge(w_b, 16 * len(b_loads))
                    if run_f:
                        nc.gpsimd.tensor_copy(out_tok[:, :, :], x2[:, :, :]).then_inc(x2_kept, 1)
                    if run_a:
                        nc.gpsimd.tensor_tensor(x1[:, :, :], x1[:, :, :], rows(b_o[0]),
                                                ALU.add).then_inc(res_done[0], 1)
                    def context_scale(l, ht):
                        pool.wait_ge(den_inv[l], ht + 1)
                        nc.gpsimd.tensor_tensor(cT[:, ht, :], cT[:, ht, :], inv_den[:, :],
                                                ALU.mult).then_inc(ctx_done[l], 1)

                    for slot in SLOTS:
                        l, at = slot
                        if run_a and at in (5, 9, "spread"):
                            context_scale(l, {5: 0, 9: 1, "spread": 2}[at])
                        if run_a and slot == (0, "output"):
                            rstd(2)
                            rstd(3)
                            pool.wait_ge(h_done, 1)
                            nc.gpsimd.tensor_tensor(v_tok[:, :, :], v_tok[:, :, :], rows(b_o[1]),
                                                    ALU.add).then_inc(res_done[1], 1)
                        others(slot)
                        if split_w_up and at in range(len(up_raw)):
                            if l == 0:
                                e, n0, buf = up_raw[at]
                                low_rows = w_up_stack[0:64, e, n0:n0 + buf.shape[1]]
                                pool.wait_ge(up_high, at + 1)
                                nc.gpsimd.tensor_tensor(low_rows, buf[0:64, :], low_rows.bitcast(F32),
                                                        ALU.subtract)

            nc.all_engine_barrier(sems_to_clear=clear_range)

        block_of(0, None, None, opening=True)
        block_of(1, 0, None, split_w_up=True)
        with nc.Fori(1, IMAGES - 1) as n:
            block_of(n + 1, n, n - 1)
        block_of(None, IMAGES - 1, IMAGES - 2)
        block_of(None, None, IMAGES - 1)


_HOST = {
    "x": (IMAGES, TOKENS, WIDTH), "w_in": (WIDTH, 2 * INNER), "w_conv": (INNER, 9), "b_conv": (INNER, 1),
    "w_x": (INNER, PATHS, RANK + 2 * STATE), "w_dt": (RANK, PATHS, INNER), "b_dt": (INNER, PATHS),
    "a_log": (128, GROUPS * PATHS), "ds": (INNER, PATHS), "on_g": (INNER,), "on_b": (INNER,),
    "w_out": (INNER, WIDTH),
    "w_qkv0": (WIDTH, 3 * WIDTH), "b_qkv0": (3 * WIDTH,), "w_o0": (WIDTH, WIDTH), "b_o0": (WIDTH,),
    "w_qkv1": (WIDTH, 3 * WIDTH), "b_qkv1": (3 * WIDTH,), "w_o1": (WIDTH, WIDTH), "b_o1": (WIDTH,),
    "ln_g0": (WIDTH,), "ln_b0": (WIDTH,), "ln_g1": (WIDTH,), "ln_b1": (WIDTH,),
    "mlp_w1": (WIDTH, HIDDEN), "mlp_w2": (HIDDEN, WIDTH), "mlp_b2": (WIDTH,),
    "exp_w1": (EXPERTS, WIDTH, HIDDEN), "exp_w2": (EXPERTS, HIDDEN, WIDTH), "exp_b2": (EXPERTS, WIDTH),
    "b_up": (128, 1 + EXPERTS, HCH), "w_gate": (WIDTH, EXPERTS), "b_gate": (EXPERTS,),
}


def kernel(**inputs):
    import numpy as np
    import concourse.bacc as bacc
    from concourse.bass_utils import run_bass_kernel_spmd

    i = {k: np.asarray(v) for k, v in inputs.items()}
    host = {
        "x": i["x"].reshape(IMAGES, TOKENS, WIDTH),
        "w_in": i["L0_conv_in_proj_w"].T,
        "w_conv": i["L0_conv_conv_w"].reshape(INNER, 9),
        "b_conv": i["L0_conv_conv_b"].reshape(INNER, 1),
        "w_x": i["L0_conv_x_proj_w"].transpose(2, 0, 1),
        "w_dt": i["L0_conv_dt_projs_w"].transpose(2, 0, 1),
        "b_dt": i["L0_conv_dt_projs_b"].T,
        "a_log": i["L0_conv_A_logs"].reshape(PATHS, GROUPS, PACK, STATE).transpose(2, 3, 1, 0)
        .reshape(128, GROUPS * PATHS),
        "ds": i["L0_conv_Ds"].reshape(PATHS, INNER).T,
        "on_g": i["L0_conv_out_norm_g"], "on_b": i["L0_conv_out_norm_b"],
        "w_out": i["L0_conv_out_proj_w"].T,
        "w_qkv0": i["L1_attn_W_attn"], "b_qkv0": i["L1_attn_b_attn"],
        "w_o0": i["L1_attn_W_proj"], "b_o0": i["L1_attn_b_proj"],
        "w_qkv1": i["L1_ffn_in_w"].T, "b_qkv1": i["L1_ffn_in_b"],
        "w_o1": i["L1_ffn_out_w"].T, "b_o1": i["L1_ffn_out_b"],
        "ln_g0": i["L1_ffn_ln1_g"], "ln_b0": i["L1_ffn_ln1_b"],
        "ln_g1": i["L1_ffn_ln2_g"], "ln_b1": i["L1_ffn_ln2_b"],
        "mlp_w1": i["L1_ffn_mlp_w1"], "mlp_w2": i["L1_ffn_mlp_w2"], "mlp_b2": i["L1_ffn_mlp_b2"],
        "exp_w1": i["L1_ffn_exp_w1"], "exp_w2": i["L1_ffn_exp_w2"], "exp_b2": i["L1_ffn_exp_b2"],
        "b_up": np.concatenate([i["L1_ffn_mlp_b1"][None], i["L1_ffn_exp_b1"]])
        .reshape(1 + EXPERTS, HCH, 128).transpose(2, 0, 1),
        "w_gate": i["L1_ffn_gate_w"].T, "b_gate": i["L1_ffn_gate_b"],
    }
    nc = bacc.Bacc("TRN2", target_bir_lowering=False, num_devices=1)
    t, arrays = {}, {}
    for name, shape in _HOST.items():
        arrays[f"{name}_dram"] = np.ascontiguousarray(host[name])
        assert arrays[f"{name}_dram"].shape == shape
        t[name] = nc.dram_tensor(f"{name}_dram", shape, F32, kind="ExternalInput").ap()
    t["out"] = nc.dram_tensor("out_dram", (IMAGES, TOKENS, WIDTH), F32, kind="ExternalOutput").ap()
    build(nc, t)
    r = run_bass_kernel_spmd(nc, [arrays], core_ids=[0])
    return r.results[0]["out_dram"].reshape(IMAGES, SIDE, SIDE, WIDTH)
```
